# Optimizing a Trainium2 kernel written in Bass

```python
import numpy as np
import jax
import jax.numpy as jnp

def _softmax(x, axis=-1):
    return jax.nn.softmax(x, axis=axis)

def _gelu(x):
    return jax.nn.gelu(x, approximate=True)

def _silu(x):
    return jax.nn.silu(x)

def _sigmoid(x):
    return jax.nn.sigmoid(x)

def _layernorm(x, axis=-1, eps=1e-05):
    m = jnp.mean(x, axis=axis, keepdims=True)
    v = jnp.var(x, axis=axis, keepdims=True)
    return (x - m) / jnp.sqrt(v + eps)

def _scatter_add(tgt, idx, src, axis=0):
    return tgt.at[idx].add(src)

def _segment_sum(src, seg, n):
    return jax.ops.segment_sum(src, seg, n)
kernel_name = 'mk_seq_preln_d1_jaxref_r4_ebba24'

def setup_inputs(seed: int=0):
    np.random.seed(seed)
    _w = jnp.asarray

    def _L0_attn_setup():
        import jax, jax.numpy as jnp
        import numpy as np
        EPS = 1e-05

        def layernorm(x, g, b):
            m = jnp.mean(x, axis=-1, keepdims=True)
            v = jnp.mean(jnp.square(x - m), axis=-1, keepdims=True)
            return (x - m) * jax.lax.rsqrt(v + EPS) * g + b

        def delta(x, gates_w, gates_b, lr_w, lr_b, out_w, out_b):
            N, T, C = x.shape
            qkv = x @ gates_w + gates_b
            q, k, v = jnp.split(qkv, 3, axis=-1)
            lr = x @ lr_w + lr_b
            k = k / jnp.linalg.norm(k, axis=-1, keepdims=True)
            K = jnp.tril(jnp.einsum('ntc,nsc->nts', k, k), k=-1)
            A = K + jnp.eye(T, dtype=x.dtype)
            u = jax.scipy.linalg.solve_triangular(A, v, lower=True)
            score = jnp.einsum('nsk,ntk->nst', q, k)
            y = jnp.einsum('nst,ntv->nsv', score, lr * u)
            return y @ out_w + out_b

        def mlp(x, w1, b1, w2, b2):
            return jax.nn.relu(x @ w1 + b1) @ w2 + b2
        N, T, C = (8, 512, 256)
        key = jax.random.key(seed)
        ks = jax.random.split(key, 16)
        s = 0.02
        return {'x': jax.random.normal(ks[0], (N, T, C), jnp.float32), 'dn_g': jnp.ones((C,), jnp.float32), 'dn_b': jnp.zeros((C,), jnp.float32), 'gates_w': jax.random.normal(ks[1], (C, 3 * C), jnp.float32) * s, 'gates_b': jnp.zeros((3 * C,), jnp.float32), 'lr_w': jax.random.normal(ks[2], (C, 1), jnp.float32) * s, 'lr_b': jnp.zeros((1,), jnp.float32), 'out_w': jax.random.normal(ks[3], (C, C), jnp.float32) * s, 'out_b': jnp.zeros((C,), jnp.float32), 'mn_g': jnp.ones((C,), jnp.float32), 'mn_b': jnp.zeros((C,), jnp.float32), 'w1': jax.random.normal(ks[4], (C, C), jnp.float32) * s, 'b1': jnp.zeros((C,), jnp.float32), 'w2': jax.random.normal(ks[5], (C, C), jnp.float32) * s, 'b2': jnp.zeros((C,), jnp.float32)}
    _L0_attn_in = _L0_attn_setup()

    def _L0_ffn_setup():
        import jax, jax.numpy as jnp
        import numpy as np
        DIM = 256
        HIDDEN = 768
        SCALE = 1.0 / 127.0

        def _dequant(w_int, dtype):
            return w_int.astype(dtype) * jnp.asarray(SCALE, dtype)
        key = jax.random.key(seed)
        k_x, k_g, k_u, k_d = jax.random.split(key, 4)
        x = jax.random.normal(k_x, (4, 512, DIM), dtype=jnp.float32)
        w_gate = jax.random.randint(k_g, (HIDDEN, DIM), -127, 128, dtype=jnp.int32)
        w_up = jax.random.randint(k_u, (HIDDEN, DIM), -127, 128, dtype=jnp.int32)
        w_down = jax.random.randint(k_d, (DIM, HIDDEN), -127, 128, dtype=jnp.int32)
        return {'x': x, 'w_gate': w_gate, 'w_up': w_up, 'w_down': w_down}
    _L0_ffn_in = _L0_ffn_setup()
    _d = {'L0_attn_x': _L0_attn_in['x'], 'L0_attn_dn_g': _L0_attn_in['dn_g'], 'L0_attn_dn_b': _L0_attn_in['dn_b'], 'L0_attn_gates_w': _L0_attn_in['gates_w'], 'L0_attn_gates_b': _L0_attn_in['gates_b'], 'L0_attn_lr_w': _L0_attn_in['lr_w'], 'L0_attn_lr_b': _L0_attn_in['lr_b'], 'L0_attn_out_w': _L0_attn_in['out_w'], 'L0_attn_out_b': _L0_attn_in['out_b'], 'L0_attn_mn_g': _L0_attn_in['mn_g'], 'L0_attn_mn_b': _L0_attn_in['mn_b'], 'L0_attn_w1': _L0_attn_in['w1'], 'L0_attn_b1': _L0_attn_in['b1'], 'L0_attn_w2': _L0_attn_in['w2'], 'L0_attn_b2': _L0_attn_in['b2'], 'L0_ffn_w_gate': _L0_ffn_in['w_gate'], 'L0_ffn_w_up': _L0_ffn_in['w_up'], 'L0_ffn_w_down': _L0_ffn_in['w_down']}
    _x0 = _d['L0_attn_x']
    _d['L0_attn_x'] = jax.random.normal(jax.random.fold_in(jax.random.key(seed), 1), (32, 512, 256), dtype=_x0.dtype)
    del _x0
    return _d

def reference(L0_attn_x, L0_attn_dn_g, L0_attn_dn_b, L0_attn_gates_w, L0_attn_gates_b, L0_attn_lr_w, L0_attn_lr_b, L0_attn_out_w, L0_attn_out_b, L0_attn_mn_g, L0_attn_mn_b, L0_attn_w1, L0_attn_b1, L0_attn_w2, L0_attn_b2, L0_ffn_w_gate, L0_ffn_w_up, L0_ffn_w_down):

    def _L0_attn_ref(x, dn_g, dn_b, gates_w, gates_b, lr_w, lr_b, out_w, out_b, mn_g, mn_b, w1, b1, w2, b2):
        import jax, jax.numpy as jnp
        import numpy as np
        EPS = 1e-05

        def layernorm(x, g, b):
            m = jnp.mean(x, axis=-1, keepdims=True)
            v = jnp.mean(jnp.square(x - m), axis=-1, keepdims=True)
            return (x - m) * jax.lax.rsqrt(v + EPS) * g + b

        def delta(x, gates_w, gates_b, lr_w, lr_b, out_w, out_b):
            N, T, C = x.shape
            qkv = x @ gates_w + gates_b
            q, k, v = jnp.split(qkv, 3, axis=-1)
            lr = x @ lr_w + lr_b
            k = k / jnp.linalg.norm(k, axis=-1, keepdims=True)
            K = jnp.tril(jnp.einsum('ntc,nsc->nts', k, k), k=-1)
            A = K + jnp.eye(T, dtype=x.dtype)
            u = jax.scipy.linalg.solve_triangular(A, v, lower=True)
            score = jnp.einsum('nsk,ntk->nst', q, k)
            y = jnp.einsum('nst,ntv->nsv', score, lr * u)
            return y @ out_w + out_b

        def mlp(x, w1, b1, w2, b2):
            return jax.nn.relu(x @ w1 + b1) @ w2 + b2
        x = x + delta(layernorm(x, dn_g, dn_b), gates_w, gates_b, lr_w, lr_b, out_w, out_b)
        x = x + mlp(layernorm(x, mn_g, mn_b), w1, b1, w2, b2)
        return x

    def _L0_ffn_ref(x, w_gate, w_up, w_down):
        import jax, jax.numpy as jnp
        import numpy as np
        DIM = 256
        HIDDEN = 768
        SCALE = 1.0 / 127.0

        def _dequant(w_int, dtype):
            return w_int.astype(dtype) * jnp.asarray(SCALE, dtype)
        wg = _dequant(w_gate, x.dtype)
        wu = _dequant(w_up, x.dtype)
        wd = _dequant(w_down, x.dtype)
        gate = jnp.einsum('bsd,hd->bsh', x, wg)
        up = jnp.einsum('bsd,hd->bsh', x, wu)
        h = jax.nn.silu(gate) * up
        return jnp.einsum('bsh,dh->bsd', h, wd)
    x = L0_attn_x
    x = x + _L0_attn_ref(_layernorm(x, axis=-1), L0_attn_dn_g, L0_attn_dn_b, L0_attn_gates_w, L0_attn_gates_b, L0_attn_lr_w, L0_attn_lr_b, L0_attn_out_w, L0_attn_out_b, L0_attn_mn_g, L0_attn_mn_b, L0_attn_w1, L0_attn_b1, L0_attn_w2, L0_attn_b2)
    x = x + _L0_ffn_ref(_layernorm(x, axis=-1), L0_ffn_w_gate, L0_ffn_w_up, L0_ffn_w_down)
    return x

_drawn_inputs = setup_inputs


def setup_inputs(seed=0):
    import zlib

    import numpy as np

    out = dict(_drawn_inputs(seed))
    spreads = {'L0_attn_dn_g': (1.0, 0.2),
     'L0_attn_dn_b': (0.0, 0.309),
     'L0_attn_gates_b': (0.0, 0.1),
     'L0_attn_out_b': (0.0, 0.1),
     'L0_attn_mn_g': (1.0, 0.6),
     'L0_attn_mn_b': (0.0, 0.8),
     'L0_attn_b1': (0.0, 0.556),
     'L0_attn_b2': (0.0, 0.1)}
    factors = {}
    for name, (base, spread) in spreads.items():
        noise = np.random.default_rng([zlib.crc32(name.encode()), seed]).standard_normal(out[name].shape)
        drawn = base * np.exp(spread * noise) if base else spread * noise
        out[name] = jnp.asarray(drawn.astype(out[name].dtype))
    for name, factor in factors.items():
        out[name] = (out[name] * factor).astype(out[name].dtype)
    return out
```

```python
from contextlib import ExitStack

import concourse.bass as bass
from concourse import mybir

ALU = mybir.AluOpType
ACT = mybir.ActivationFunctionType
F32 = mybir.dt.float32
F32R = mybir.dt.float32r
I32 = mybir.dt.int32

P = 128
EPS = 1e-5
QUANT = 1.0 / 127.0
SUB = 32
A0, A1, A2, S0, FG, FU, FO0, FO1 = range(8)


def wait(eng, sem, value):
    if isinstance(value, int) and value <= 0:
        return
    eng.wait_ge(sem, value)


def delta_block_kernel(nc, x, dn_g, dn_b, gates_w, gates_b, lr_w, lr_b, out_w, out_b, mn_g, mn_b,
                       w1, b1, w2, b2, w_gate, w_up, w_down, out):
    NS, T, C = x.shape
    H = w_gate.shape[0]
    TB, CB, HB = T // P, C // P, H // P
    LR, V0, WALL = 2 * C, 2 * C + 2, 3 * C + 2
    OFF = TB * P
    GCOL = {(1, 0): OFF, (3, 0): OFF + P, (3, 1): OFF + 2 * P, (3, 2): OFF + 3 * P,
            (2, 0): OFF + 4 * P, (2, 1): OFF + 5 * P}
    GW = OFF + 6 * P
    KXE = TB * C
    E_LR, E_S, E_B, E_R1, E_SH = (KXE + TB * q for q in range(5))
    KXW = KXE + 5 * TB
    NSUB = T // SUB
    GROUP = P // NSUB
    SLOTS = NS // GROUP
    QPB = P // SUB
    assert TB == 4 and CB == 2 and NS % GROUP == 0 and NS >= 3

    kx_d = nc.dram_tensor("kx_scratch", [NS, P, KXW], F32, kind="Internal").ap()
    gg_d = nc.dram_tensor("gg_scratch", [NS, P, GW], F32, kind="Internal").ap()
    low_d = nc.dram_tensor("low_scratch", [NS * NSUB, SUB * SUB], F32, kind="Internal").ap()
    inv_d = nc.dram_tensor("inv_scratch", [NS * NSUB, SUB * SUB], F32, kind="Internal").ap()
    x_v = x.rearrange("n (j p) c -> n p j c", p=P)
    out_v = out.rearrange("n (j p) c -> n p j c", p=P)
    low_v = low_d.rearrange("(n j a) (r c) -> n a r j c", j=TB, a=QPB, c=SUB)
    inv_v = inv_d.rearrange("(n j a) (r c) -> n a r j c", j=TB, a=QPB, c=SUB)
    low_lane = low_d.rearrange("(s l) e -> l s e", l=P)
    inv_lane = inv_d.rearrange("(s l) e -> l s e", l=P)

    with ExitStack() as ctx:
        def sb(name, shape, dt=F32, c=ctx):
            return c.enter_context(nc.sbuf_tensor(name, shape, dt))

        held = []

        def sem(name):
            held.append(nc.alloc_semaphore(name=name))
            return held[-1]

        def sems(name, n):
            return [sem(f"{name}{k}") for k in range(n)]

        def end_program():
            nc.clear_and_free_semaphores(held)
            held.clear()
            nc.all_engine_barrier()

        ps = ctx.enter_context(nc.psum_tensor("ps", [P, 8, 512], F32))

        ident = sb("ident", [P, P])
        mask32 = sb("mask32", [P, P])
        mask64 = sb("mask64", [P, P])
        eps4 = sb("eps4", [P, TB])
        mhalf4 = sb("mhalf4", [P, TB])
        zero4 = sb("zero4", [P, TB])
        one4 = sb("one4", [P, TB])
        wk = sb("wk", [P, CB, C + 2])
        wqT = sb("wqT", [P, CB, C])
        wvo = sb("wvo", [P, CB, C])
        w1f = sb("w1f", [P, CB, C])
        b1f = sb("b1f", [P, CB])
        w2f = sb("w2f", [P, CB, C])
        bo_bc = sb("bo_bc", [P, C])
        b2_bc = sb("b2_bc", [P, C])
        wgT = sb("wgT", [P, CB, H], F32R)
        wuT = sb("wuT", [P, CB, H], F32R)
        wdT = sb("wdT", [P, HB, C], F32R)

        xt = sb("xt", [P, TB, C])
        xh = sb("xh", [P, TB, C])
        xhT = sb("xhT", [P, CB, T])
        kx = sb("kx", [P, KXW])
        gg = sb("gg", [P, GW])
        x32 = sb("x32", [P, TB, P])
        kx3 = kx[:, 0:KXE].rearrange("p (j c) -> p j c", j=TB)
        ready = ctx.enter_context(nc.semaphore("ready"))

        with ExitStack() as sx:
            wall = sb("wall", [P, CB, WALL], c=sx)
            brow = sb("brow", [1, WALL], c=sx)
            dcol = sb("dcol", [P, 2, CB], c=sx)
            mcol = sb("mcol", [P, 3, CB], c=sx)
            wo = sb("wo", [P, CB, C], c=sx)
            w1raw = sb("w1raw", [P, CB, C], c=sx)
            borow = sb("borow", [P, C], c=sx)
            wgi = sb("wgi", [P, HB, C], I32, c=sx)
            wui = sb("wui", [P, HB, C], I32, c=sx)
            wdi = sb("wdi", [P, CB, H], I32, c=sx)
            wgf = sb("wgf", [P, HB, C], c=sx)
            wuf = sb("wuf", [P, HB, C], c=sx)
            wdf = sb("wdf", [P, CB, H], c=sx)
            ones = sb("ones", [P, P], c=sx)
            diff = sb("diff", [P, CB], c=sx)
            diff_bc = sb("diff_bc", [P, CB, P], c=sx)
            shift = sb("shift", [P, WALL], c=sx)
            wfold = sb("wfold", [P, CB, WALL], c=sx)
            wvT = sb("wvT", [P, CB, C], c=sx)
            minus = sem("minus")
            pads, loaded, ints_in = sem("pads"), sem("loaded"), sem("ints_in")
            ones_set, zeroed, diff_done, diff_bc_done = sem("ones_set"), sem("zeroed"), sem("diff_done"), sem("diff_bc_done")
            shift_ps, shift_done, fold_done = sem("shift_ps"), sem("shift_done"), sem("fold_done")
            id_done, tq_ps, tq_done, vo_ps, vo_done = sem("id_done"), sem("tq_ps"), sem("tq_done"), sem("vo_ps"), sem("vo_done")
            b1_ps, misc, ints_f, wt_ps, wt_ev, x32_zero = sem("b1_ps"), sem("misc"), sem("ints_f"), sem("wt_ps"), sem("wt_ev"), sem("x32_zero")
            with nc.Block() as block:
                @block.sync
                def _(sp):
                    sp.wait_ge(pads, 2)
                    gv = gates_w.rearrange("(k p) o -> p k o", p=P)
                    col = lambda v: v.rearrange("(k p) -> p k", p=P)
                    row = lambda v: v.rearrange("(a c) -> a c", a=1)
                    for dst, src in (
                        (wall[:, :, 0:2 * C], gv[:, :, 0:2 * C]),
                        (wall[:, :, V0:WALL], gv[:, :, 2 * C:3 * C]),
                        (wall[:, :, LR:LR + 1], lr_w.rearrange("(k p) o -> p k o", p=P)),
                        (brow[:, 0:2 * C], row(gates_b)[:, 0:2 * C]),
                        (brow[:, V0:WALL], row(gates_b)[:, 2 * C:3 * C]),
                        (brow[:, LR:LR + 1], row(lr_b)),
                        (dcol[:, 0, :], col(dn_g)), (dcol[:, 1, :], col(dn_b)),
                        (mcol[:, 0, :], col(mn_g)), (mcol[:, 1, :], col(mn_b)), (mcol[:, 2, :], col(b1)),
                        (wo[:, :, :], out_w.rearrange("(k p) o -> p k o", p=P)),
                        (w1raw[:, :, :], w1.rearrange("(k p) o -> p k o", p=P)),
                        (w2f[:, :, :], w2.rearrange("(k p) o -> p k o", p=P)),
                        (borow[:, :], row(out_b).partition_broadcast(P)),
                        (b2_bc[:, :], row(b2).partition_broadcast(P)),
                    ):
                        with nc.allow_non_contiguous_dma(reason="a few columns, once"):
                            sp.dma_start(dst, src).then_inc(loaded, 16)
                    sp.dma_start(wgi[:, :, :], w_gate.rearrange("(h p) c -> p h c", p=P)).then_inc(ints_in, 16)
                    sp.dma_start(wui[:, :, :], w_up.rearrange("(h p) c -> p h c", p=P)).then_inc(ints_in, 16)
                    sp.dma_start(wdi[:, :, :], w_down.rearrange("(k p) h -> p k h", p=P)).then_inc(ints_in, 16)
                    sp.wait_ge(loaded, 16 * 16)
                    sp.wait_ge(ints_in, 48)

                @block.gpsimd
                def _(pool):
                    pool.memset(wall[:, :, LR:V0], 0.0).then_inc(pads, 1)
                    pool.memset(brow[:, LR:V0], 0.0).then_inc(pads, 1)
                    pool.memset(ones[:, :], 1.0).then_inc(ones_set, 1)
                    pool.wait_ge(ones_set, 1)
                    pool.affine_select(out=ident[:, :], in_=ones[:, :], compare_op=ALU.is_equal, fill=0.0,
                                       base=0, pattern=[[-1, P]], channel_multiplier=1).then_inc(id_done, 1)
                    pool.memset(mask32[:, :], 0.0).then_inc(zeroed, 1)
                    pool.memset(mask64[:, :], 0.0).then_inc(zeroed, 1)
                    pool.wait_ge(zeroed, 2)
                    pool.memset(mask32[SUB:2 * SUB, 0:SUB], -1.0)
                    pool.memset(mask32[3 * SUB:4 * SUB, 2 * SUB:3 * SUB], -1.0).then_inc(minus, 1)
                    pool.wait_ge(minus, 1)
                    pool.memset(mask64[2 * SUB:4 * SUB, 0:2 * SUB], -1.0).then_inc(minus, 1)
                    pool.wait_ge(minus, 2)
                    pool.memset(eps4[:, :], EPS)
                    pool.memset(mhalf4[:, :], -0.5)
                    pool.memset(zero4[:, :], 0.0)
                    pool.memset(one4[:, :], 1.0)
                    pool.memset(x32[:, :, :], 0.0).then_inc(x32_zero, 1)
                    pool.wait_ge(x32_zero, 1)

                @block.vector
                def _(dve):
                    dve.wait_ge(ones_set, 1)
                    dve.wait_ge(loaded, 16 * 16)
                    dve.tensor_tensor(diff[:, :], dcol[:, 1, :], dcol[:, 0, :], ALU.subtract).then_inc(diff_done, 1)
                    dve.wait_ge(diff_done, 1)
                    for k in range(CB):
                        dve.tensor_scalar(diff_bc[:, k, :], ones[:, :], diff[:, k:k + 1], None,
                                          ALU.mult).then_inc(diff_bc_done, 1)
                    dve.tensor_scalar(bo_bc[:, :], borow[:, :], 1.0 / C, None, ALU.mult).then_inc(misc, 1)
                    for k in range(CB):
                        dve.tensor_scalar(w1f[:, k, :], w1raw[:, k, :], mcol[:, 0, k:k + 1], None,
                                          ALU.mult).then_inc(misc, 1)
                    dve.wait_ge(shift_done, 2)
                    for k in range(CB):
                        dve.scalar_tensor_tensor(out=wfold[:, k, :], in0=wall[:, k, :], scalar=dcol[:, 0, k:k + 1],
                                                 in1=shift[:, :], op0=ALU.mult, op1=ALU.add).then_inc(fold_done, 1)
                    dve.wait_ge(fold_done, CB)
                    dve.tensor_copy(wk[:, :, :], wfold[:, :, C:C + C + 2]).then_inc(misc, 1)
                    dve.wait_ge(b1_ps, 1)
                    dve.tensor_tensor(b1f[:, :], ps[:, 3, 0:CB], mcol[:, 2, :], ALU.add).then_inc(misc, 1)
                    dve.wait_ge(tq_ps, 1)
                    dve.tensor_copy(wqT[:, :, :].rearrange("p a b -> p (a b)"), ps[:, 4, :]).then_inc(tq_done, 1)
                    dve.wait_ge(tq_ps, 2)
                    dve.tensor_copy(wvT[:, :, :].rearrange("p a b -> p (a b)"), ps[:, 5, :]).then_inc(tq_done, 1)
                    dve.wait_ge(vo_ps, 1)
                    dve.tensor_copy(wvo[:, :, :].rearrange("p a b -> p (a b)"), ps[:, 6, :]).then_inc(vo_done, 1)
                    dve.wait_ge(ints_in, 48)
                    dve.tensor_copy(wgf[:, :, :], wgi[:, :, :]).then_inc(ints_f, 1)
                    dve.tensor_copy(wuf[:, :, :], wui[:, :, :]).then_inc(ints_f, 1)
                    dve.tensor_copy(wdf[:, :, :], wdi[:, :, :]).then_inc(ints_f, 1)
                    dve.wait_ge(misc, 5)

                @block.scalar
                def _(act):
                    act.wait_ge(shift_ps, 1)
                    act.activation(shift[:, 0:512], ps[:, 0, :], ACT.Copy, scale=1.0 / C).then_inc(shift_done, 1)
                    act.activation(shift[:, 512:WALL], ps[:, 1, 0:WALL - 512], ACT.Copy, scale=1.0 / C).then_inc(shift_done, 1)
                    g = 0
                    for dst in (wgT, wuT):
                        for k in range(CB):
                            for n in range(0, HB, 2):
                                act.wait_ge(wt_ps, g + 1)
                                act.activation(dst[:, k, n * P:(n + 2) * P], ps[:, g % 2, 0:2 * P], ACT.Copy).then_inc(wt_ev, 1)
                                g += 1
                    for n in range(HB):
                        act.wait_ge(wt_ps, g + 1)
                        act.activation(wdT[:, n, :], ps[:, g % 2, 0:C], ACT.Copy).then_inc(wt_ev, 1)
                        g += 1

                @block.tensor
                def _(pe):
                    pe.wait_ge(loaded, 16 * 16)
                    pe.wait_ge(ones_set, 1)
                    pe.wait_ge(diff_bc_done, CB)
                    for bank, lo, hi in ((0, 0, 512), (1, 512, WALL)):
                        for k in range(CB):
                            pe.matmul(ps[:, bank, 0:hi - lo], diff_bc[:, k, :], wall[:, k, lo:hi], start=(k == 0), stop=False)
                        mm = pe.matmul(ps[:, bank, 0:hi - lo], ones[0:1, :], brow[:, lo:hi], start=False, stop=True)
                    mm.then_inc(shift_ps, 1)
                    for m in range(CB):
                        for k in range(CB):
                            mm = pe.matmul(ps[:, 3, m:m + 1], w1raw[:, k, m * P:(m + 1) * P], mcol[:, 1, k:k + 1],
                                           start=(k == 0), stop=(k == CB - 1))
                    mm.then_inc(b1_ps, 1)
                    pe.wait_ge(id_done, 1)
                    pe.wait_ge(fold_done, CB)
                    for bank, c0 in ((4, 0), (5, V0)):
                        for m in range(CB):
                            for k in range(CB):
                                mm = pe.transpose(ps[:, bank, m * C + k * P:m * C + (k + 1) * P],
                                                  wfold[:, k, c0 + m * P:c0 + (m + 1) * P], ident[:, :])
                        mm.then_inc(tq_ps, 1)
                    pe.wait_ge(tq_done, 2)
                    for m in range(CB):
                        for k in range(CB):
                            mm = pe.matmul(ps[:, 6, m * C:(m + 1) * C], wvT[:, k, m * P:(m + 1) * P], wo[:, k, :],
                                           start=(k == 0), stop=(k == CB - 1))
                    mm.then_inc(vo_ps, 1)
                    pe.wait_ge(ints_f, 3)
                    pe.wait_ge(shift_done, 2)
                    g = 0
                    for src in (wgf, wuf):
                        for k in range(CB):
                            for n in range(0, HB, 2):
                                wait(pe, wt_ev, g - 1)
                                for q in range(2):
                                    mm = pe.transpose(ps[:, g % 2, q * P:(q + 1) * P], src[:, n + q, k * P:(k + 1) * P], ident[:, :])
                                mm.then_inc(wt_ps, 1)
                                g += 1
                    for n in range(HB):
                        pe.wait_ge(wt_ev, g - 1)
                        for k in range(CB):
                            mm = pe.transpose(ps[:, g % 2, k * P:(k + 1) * P], wdf[:, k, n * P:(n + 1) * P], ident[:, :])
                        mm.then_inc(wt_ps, 1)
                        g += 1
                    pe.wait_ge(wt_ev, g)
                    pe.wait_ge(vo_done, 1)
                    pe.wait_ge(x32_zero, 1)
                    pe.nop().then_inc(ready, 1)
            end_program()

        with ExitStack() as kc:
            bst = sb("bst", [P, TB, 6], c=kc)
            mv = sb("mv", [P, TB, 2], c=kc)
            lns = sb("lns", [P, 8, TB], c=kc)
            exln = sb("exln", [P, 4, TB], c=kc)
            sqj = sb("sqj", [P, TB, C], c=kc)
            ssq = sb("ssq", [P, TB], c=kc)
            rn = sb("rn", [P, TB], c=kc)
            knT = sb("knT", [P, CB, T], c=kc)
            x_in, kx_out, gg_out, low_out = sem("x_in"), sem("kx_out"), sem("gg_out"), sem("low_out")
            bn_done, mv_done, ln_done, xh_done = sems("bn_done", TB), sem("mv_done"), sem("ln_done"), sem("xh_done")
            lstep = sems("lstep", 8)
            xhT_ps, xhT_ev = sems("xhT_ps", CB), sems("xhT_ev", CB)
            k_ps, sq_done, rn_done = sems("k_ps", TB), sem("sq_done"), sem("rn_done")
            ex_done, lr_done, kn_done = sem("ex_done"), sem("lr_done"), sem("kn_done")
            knT_ps, knT_ev = sems("knT_ps", CB), sems("knT_ev", CB)
            g_ps, g_ev = sems("g_ps", 3), sems("g_ev", 3)
            T0, T1, K0, G0, G1 = 0, 1, 2, 6, 7
            gparts = ((G0, 0, OFF), (G1, OFF, OFF + 4 * P), (T0, OFF + 4 * P, GW))

            def piped(body, tail):
                def run(eng):
                    body(eng, 0, False, True)
                    body(eng, 1, True, True)
                    with eng.Fori(2, NS - 1) as i:
                        body(eng, i, True, True)
                    body(eng, NS - 1, True, False)
                    tail(eng)
                return run

            with nc.Block() as block:
                def sp_stores(sp, n):
                    sp.wait_ge(kn_done, n + 1)
                    sp.dma_start(kx_d[n], kx[:, :]).then_inc(kx_out, 16)
                    for q in range(3):
                        sp.wait_ge(g_ev[q], n + 1)
                    sp.dma_start(gg_d[n], gg[:, :]).then_inc(gg_out, 16)
                    for a in range(QPB):
                        sp.dma_start(low_v[n][a], gg[a * SUB:(a + 1) * SUB, 0:OFF].rearrange("p (j c) -> p j c", c=P)
                                     [:, :, a * SUB:(a + 1) * SUB]).then_inc(low_out, 16)

                @block.sync
                def _(sp):
                    sp.dma_start(xt[:, :, :], x_v[0]).then_inc(x_in, 16)
                    sp.wait_ge(xh_done, 1)
                    sp.dma_start(xt[:, :, :], x_v[1]).then_inc(x_in, 16)
                    with sp.Fori(0, NS - 2) as i:
                        sp.wait_ge(xh_done, i + 2)
                        sp.dma_start(xt[:, :, :], x_v[i + 2]).then_inc(x_in, 16)
                        sp_stores(sp, i)
                    sp_stores(sp, NS - 2)
                    sp_stores(sp, NS - 1)
                    sp.wait_ge(kx_out, 16 * NS)
                    sp.wait_ge(gg_out, 16 * NS)
                    sp.wait_ge(low_out, 16 * QPB * NS)

                def stats(dve, n):
                    dve.wait_ge(x_in, 16 * (n + 1))
                    wait(dve, ln_done, n)
                    for j in range(TB):
                        dve.bn_stats(bst[:, j, :], xt[:, j, :]).then_inc(bn_done[j], 1)
                    for j in range(TB):
                        dve.wait_ge(ready, 1)
                        dve.wait_ge(bn_done[j], n + 1)
                        agg = dve.bn_aggr(mv[:, j, :], bst[:, j, :])
                    agg.then_inc(mv_done, 1)

                def dve_g(dve, n):
                    dve.wait_ge(g_ps[1], n + 1)
                    wait(dve, gg_out, 16 * n)
                    dve.tensor_copy(gg[:, gparts[1][1]:gparts[1][2]], ps[:, G1, :]).then_inc(g_ev[1], 1)

                def dve_body(dve, i, prev, more):
                    dve.wait_ge(xhT_ps[1], i + 1)
                    wait(dve, k_ps[TB - 1], i)
                    dve.tensor_copy(xhT[:, 1, :], ps[:, T1, :]).then_inc(xhT_ev[1], 1)
                    dve.wait_ge(ln_done, i + 1)
                    wait(dve, kx_out, 16 * i)
                    dve.tensor_copy(kx[:, E_S:KXW], exln[:, :, :].rearrange("p q j -> p (q j)")).then_inc(ex_done, 1)
                    if prev:
                        dve.wait_ge(knT_ps[1], i)
                        wait(dve, g_ps[2], i - 1)
                        dve.tensor_copy(knT[:, 1, :], ps[:, G1, :]).then_inc(knT_ev[1], 1)
                    if more:
                        stats(dve, i + 1)
                    dve.wait_ge(sq_done, i + 1)
                    dve.tensor_copy(kx[:, E_LR:E_LR + TB].rearrange("p (j o) -> p j o", o=1),
                                    ps[:, K0:K0 + TB, C:C + 1]).then_inc(lr_done, 1)
                    dve.wait_ge(rn_done, i + 1)
                    wait(dve, knT_ps[1], i)
                    dve.tensor_tensor(kx3, ps[:, K0:K0 + TB, 0:C], rn[:, :].unsqueeze(2).broadcast_to([P, TB, C]),
                                      ALU.mult).then_inc(kn_done, 1)
                    if prev:
                        dve_g(dve, i - 1)

                @block.vector
                def _(dve):
                    stats(dve, 0)
                    piped(dve_body, lambda e: (
                        e.wait_ge(knT_ps[1], NS),
                        e.tensor_copy(knT[:, 1, :], ps[:, G1, :]).then_inc(knT_ev[1], 1),
                        dve_g(e, NS - 1)))(dve)

                def act_g(act, n):
                    act.wait_ge(g_ps[0], n + 1)
                    wait(act, gg_out, 16 * n)
                    wait(act, low_out, 16 * QPB * n)
                    act.activation(gg[:, 0:OFF], ps[:, G0, :], ACT.Copy).then_inc(g_ev[0], 1)
                    act.wait_ge(g_ps[2], n + 1)
                    act.activation(gg[:, gparts[2][1]:GW], ps[:, T0, 0:2 * P], ACT.Copy).then_inc(g_ev[2], 1)

                def act_body(act, i, prev, more):
                    act.wait_ge(xhT_ps[0], i + 1)
                    wait(act, k_ps[TB - 1], i)
                    act.activation(xhT[:, 0, :], ps[:, T0, :], ACT.Copy).then_inc(xhT_ev[0], 1)
                    if prev:
                        act.wait_ge(knT_ps[0], i)
                        wait(act, g_ps[2], i - 1)
                        act.activation(knT[:, 0, :], ps[:, G0, :], ACT.Copy).then_inc(knT_ev[0], 1)
                    wait(act, rn_done, i)
                    for j in range(TB):
                        act.wait_ge(k_ps[j], i + 1)
                        sq = act.activation(sqj[:, j, :], ps[:, K0 + j, 0:C], ACT.Square, accum_out=ssq[:, j:j + 1])
                    sq.then_inc(sq_done, 1)
                    if prev:
                        act_g(act, i - 1)

                @block.scalar
                def _(act):
                    piped(act_body, lambda e: (
                        e.wait_ge(knT_ps[0], NS),
                        e.activation(knT[:, 0, :], ps[:, G0, :], ACT.Copy).then_inc(knT_ev[0], 1),
                        act_g(e, NS - 1)))(act)

                def norms(pool, n):
                    m, v = mv[:, :, 0], mv[:, :, 1]
                    L = [lns[:, q, :] for q in range(8)]
                    s_, b_, r1, sh = (exln[:, q, :] for q in range(4))
                    steps = [(L[0], v, eps4[:, :], ALU.add), (r1, L[0], mhalf4[:, :], ALU.pow),
                             (L[1], r1, r1, ALU.mult), (L[2], L[1], v, ALU.mult), (L[3], L[2], eps4[:, :], ALU.add),
                             (L[4], L[3], mhalf4[:, :], ALU.pow), (s_, L[4], r1, ALU.mult),
                             (L[5], s_, m, ALU.mult)]
                    pool.wait_ge(mv_done, n + 1)
                    wait(pool, ex_done, n)
                    wait(pool, xh_done, n)
                    for q, (o, a, b, op) in enumerate(steps):
                        pool.tensor_tensor(o, a, b, op).then_inc(lstep[q], 1)
                        pool.wait_ge(lstep[q], n + 1)
                    pool.tensor_tensor(b_, one4[:, :], L[5], ALU.subtract)
                    pool.tensor_tensor(L[6], m, r1, ALU.mult).then_inc(ln_half, 1)
                    pool.wait_ge(ln_half, n + 1)
                    pool.tensor_tensor(sh, zero4[:, :], L[6], ALU.subtract).then_inc(ln_done, 1)

                def make_xh(pool, n):
                    pool.wait_ge(ready, 1)
                    for k in range(CB):
                        wait(pool, xhT_ps[k], n)
                    pool.wait_ge(ln_done, n + 1)
                    for j in range(TB):
                        op = pool.tensor_scalar(xh[:, j, :], xt[:, j, :], exln[:, 0, j:j + 1], exln[:, 1, j:j + 1],
                                                ALU.mult, ALU.add)
                    op.then_inc(xh_done, 1)

                ln_half = sem("ln_half")

                def pool_body(pool, i, prev, more):
                    if more:
                        norms(pool, i + 1)
                    pool.wait_ge(sq_done, i + 1)
                    wait(pool, kn_done, i)
                    pool.tensor_tensor(rn[:, :], ssq[:, :], mhalf4[:, :], ALU.pow).then_inc(rn_done, 1)
                    if more:
                        make_xh(pool, i + 1)

                @block.gpsimd
                def _(pool):
                    norms(pool, 0)
                    make_xh(pool, 0)
                    piped(pool_body, lambda e: None)(pool)

                def pe_gram(pe, n):
                    for k in range(CB):
                        pe.wait_ge(knT_ev[k], n + 1)
                    def group(bank, c0, pairs):
                        for i, j, w in pairs:
                            for k in range(CB):
                                mm = pe.matmul(ps[:, bank, c0:c0 + w], knT[:, k, i * P:(i + 1) * P],
                                               knT[:, k, j * P:j * P + w], start=(k == 0), stop=(k == CB - 1))
                            c0 += w
                        return mm
                    group(G0, 0, [(i, i, P) for i in range(TB)]).then_inc(g_ps[0], 1)
                    group(G1, 0, [(1, 0, P), (3, 0, 3 * P)]).then_inc(g_ps[1], 1)
                    group(T0, 0, [(2, 0, 2 * P)]).then_inc(g_ps[2], 1)

                def pe_knT(pe, n):
                    pe.wait_ge(kn_done, n + 1)
                    wait(pe, g_ev[0], n)
                    wait(pe, g_ev[1], n)
                    for k in range(CB):
                        for j in range(TB):
                            mm = pe.transpose(ps[:, G0 + k, j * P:(j + 1) * P], kx3[:, j, k * P:(k + 1) * P], ident[:, :])
                        mm.then_inc(knT_ps[k], 1)

                def pe_body(pe, i, prev, more):
                    pe.wait_ge(xh_done, i + 1)
                    wait(pe, g_ev[2], i - 1)
                    for k in range(CB):
                        for j in range(TB):
                            mm = pe.transpose(ps[:, T0 + k, j * P:(j + 1) * P], xh[:, j, k * P:(k + 1) * P], ident[:, :])
                        mm.then_inc(xhT_ps[k], 1)
                    if prev:
                        pe_knT(pe, i - 1)
                    for k in range(CB):
                        pe.wait_ge(xhT_ev[k], i + 1)
                    wait(pe, kn_done, i)
                    wait(pe, lr_done, i)
                    for j in range(TB):
                        for k in range(CB):
                            mm = pe.matmul(ps[:, K0 + j, 0:C + 2], xhT[:, k, j * P:(j + 1) * P], wk[:, k, :],
                                           start=(k == 0), stop=(k == CB - 1))
                        mm.then_inc(k_ps[j], 1)
                    if prev:
                        pe_gram(pe, i - 1)

                @block.tensor
                def _(pe):
                    piped(pe_body, lambda e: (
                        pe_knT(e, NS - 1), pe_gram(e, NS - 1)))(pe)
            end_program()

        with ExitStack() as ic:
            low = sb("low", [P, SLOTS, SUB * SUB], c=ic)
            inv = sb("inv", [P, SLOTS, SUB * SUB], c=ic)
            tmp = sb("tmp", [P, SLOTS, SUB // 2 * SUB // 2], c=ic)
            low_in, inv_out = sem("low_in"), sem("inv_out")
            inv_zero, inv_one, prod, subd = sem("inv_zero"), sem("inv_one"), sem("prod"), sem("subd")
            low4 = low[:, :, :].rearrange("p s (r c) -> p s r c", c=SUB)
            inv4 = inv[:, :, :].rearrange("p s (r c) -> p s r c", c=SUB)
            with nc.Block() as block:
                @block.sync
                def _(sp):
                    sp.dma_start(low[:, :, :], low_lane).then_inc(low_in, 16)
                    sp.wait_ge(subd, SUB - 1)
                    sp.dma_start(inv_lane, inv[:, :, :]).then_inc(inv_out, 16)
                    sp.wait_ge(inv_out, 16)

                @block.vector
                def _(dve):
                    dve.memset(inv[:, :, :], 0.0).then_inc(inv_zero, 1)
                    dve.wait_ge(inv_zero, 1)
                    dve.memset(inv[:, :, 0:SUB * SUB:SUB + 1], 1.0).then_inc(inv_one, 1)
                    dve.wait_ge(inv_one, 1)
                    dve.wait_ge(low_in, 16)
                    for j in range(SUB - 1):
                        n, w = SUB - 1 - j, j + 1
                        t4 = tmp[:, :, 0:n * w].rearrange("p s (r c) -> p s r c", c=w)
                        if j:
                            dve.wait_ge(subd, j)
                        dve.tensor_tensor(t4, low4[:, :, j + 1:SUB, j:j + 1].broadcast_to([P, SLOTS, n, w]),
                                          inv4[:, :, j:j + 1, 0:w].broadcast_to([P, SLOTS, n, w]),
                                          ALU.mult).then_inc(prod, 1)
                        dve.wait_ge(prod, j + 1)
                        dve.tensor_tensor(inv4[:, :, j + 1:SUB, 0:w], inv4[:, :, j + 1:SUB, 0:w], t4,
                                          ALU.subtract).then_inc(subd, 1)
            end_program()

        with ExitStack() as mc:
            def mb(name, shape, dt=F32):
                return sb(name, shape, dt, c=mc)

            xT32 = mb("xT32", [P, TB, P])
            p1 = mb("p1", [P, TB, P])
            x64 = mb("x64", [P, TB, P])
            xT64 = mb("xT64", [P, TB, P])
            x128 = mb("x128", [P, TB, P])
            wt = mb("wt", [P, TB, C])
            z = mb("z", [P, TB, C])
            bt = mb("bt", [P, CB, C])
            e_ = mb("e_", [P, CB, C])
            m2 = mb("m2", [P, CB, C])
            a0 = mb("a0", [P, TB, C])
            shf = mb("shf", [P, TB])
            bs2, mv2, ls2, sc2 = mb("bs2", [P, TB, 6]), mb("mv2", [P, TB, 2]), mb("ls2", [P, 2, TB]), mb("sc2", [P, 2, TB])
            bs3, mv3, ls3, sc3 = mb("bs3", [P, TB, 6]), mb("mv3", [P, TB, 2]), mb("ls3", [P, 2, TB]), mb("sc3", [P, 2, TB])
            xh2 = mb("xh2", [P, TB, C])
            xh2T = mb("xh2T", [P, CB, T])
            h1 = mb("h1", [P, CB, T])
            xa = mb("xa", [P, TB, C])
            xa2 = mb("xa2", [P, TB, C])
            x2 = mb("x2", [P, TB, C])
            xh3 = mb("xh3", [P, TB, C])
            x3h = mb("x3h", [P, CB, T], F32R)
            x3l = mb("x3l", [P, CB, T], F32R)
            sg = mb("sg", [P, 2, T])
            hf = mb("hf", [P, 2, T])
            hh = mb("hh", [P, HB, T], F32R)
            hl = mb("hl", [P, HB, T], F32R)
            ot = mb("ot", [P, TB, C])

            inv_in, gg_in, kx_in, xin, out_st = sem("inv_in"), sem("gg_in"), sem("kx_in"), sem("xin"), sem("out_st")
            xT_ps, xT_ev = sem("xT_ps"), sem("xT_ev")
            p32_ps, p32_ev, p64_ps, p64_ev = sem("p32_ps"), sem("p32_ev"), sem("p64_ps"), sem("p64_ev")
            x64_ps, x64_ev, xT64_ps, xT64_ev = sem("x64_ps"), sem("x64_ev"), sem("xT64_ps"), sem("xT64_ev")
            x128_ps, x128_ev = sem("x128_ps"), sem("x128_ev")
            w_ps, w_ev, z_ps, z_ev = sems("w_ps", TB), sems("w_ev", TB), sems("z_ps", TB), sems("z_ev", TB)
            ht_ps, ht_ev = sems("ht_ps", CB), sems("ht_ev", CB)
            bt_ps, bt_ev, e_ps, e_ev, m2_ps, m2_ev = sem("bt_ps"), sem("bt_ev"), sem("e_ps"), sem("e_ev"), sem("m2_ps"), sem("m2_ev")
            y_ps, a0_ev = sems("y_ps", 2), sems("a0_ev", TB)
            bn2, mv2_done, l2, ln2_done = sems("bn2_", TB), sem("mv2_done"), sems("l2_", 3), sem("ln2_done")
            bn3, mv3_done, l3, ln3_done = sems("bn3_", TB), sem("mv3_done"), sems("l3_", 3), sem("ln3_done")
            xhm_done, xh2_done, xh3_done = sem("xhm_done"), sem("xh2_done"), sem("xh3_done")
            xb_done, xa_done, sh_done = sem("xb_done"), sem("xa_done"), sem("sh_done")
            t2_ps, t2_ev = sems("t2_ps", 2), sems("t2_ev", 2)
            m1_ps, h1_ev = sems("m1_ps", 2), sems("h1_ev", 2)
            mo_ps, x2_ev = sems("mo_ps", 2), sems("x2_ev", TB)
            t3_ps, x3h_ev, x3l_ev = sems("t3_ps", 2), sems("x3h_ev", 2), sems("x3l_ev", 2)
            gate_ps, up_ps = sems("gate_ps", HB), sems("up_ps", HB)
            sg_ev, hf_ev, hh_ev, hl_ev = sems("sg_ev", HB), sems("hf_ev", HB), sems("hh_ev", HB), sems("hl_ev", HB)
            fo_ps, ot_ev = sems("fo_ps", 2), sems("ot_ev", 2)

            def diag(j):
                return gg[:, j * P:(j + 1) * P]

            def blk(j):
                return slice(j * P, (j + 1) * P)

            def overlapped(body):
                def run(eng):
                    body(eng, 0, True, False)
                    body(eng, 1, True, True)
                    with eng.Fori(2, NS) as i:
                        body(eng, i, True, True)
                    body(eng, NS, False, True)
                return run

            with nc.Block() as block:
                def pe_transposes(pe, banks, src, done):
                    for k in range(CB):
                        for j in range(TB):
                            mm = pe.transpose(ps[:, banks[k], blk(j)], src[:, j, blk(k)], ident[:, :])
                        mm.then_inc(done[k], 1)

                def pe_zstep(pe, i, j):
                    pe.wait_ge(w_ev[j], i + 1)
                    if j < TB - 1:
                        pe.wait_ge(z_ev[j + 1], i + 1)
                    pe.matmul(ps[:, A1, 0:C], x128[:, j, :], wt[:, j, :], start=True, stop=True).then_inc(z_ps[j], 1)

                def pe_wstep(pe, i, j):
                    pe.wait_ge(z_ev[j + 1], i + 1)
                    if j < TB - 2:
                        pe.wait_ge(w_ev[j + 1], i + 1)
                    for m in range(TB - 1, j, -1):
                        c = GCOL[(m, j)]
                        mm = pe.matmul(ps[:, A0, 0:C], gg[:, c:c + P], z[:, m, :], start=(m == TB - 1), stop=(m == j + 1))
                    mm.then_inc(w_ps[j], 1)

                def pe_bt(pe, i, j):
                    pe.wait_ge(z_ev[j], i + 1)
                    for m in range(CB):
                        mm = pe.matmul(ps[:, A2, m * C:(m + 1) * C], xh[:, j, blk(m)], z[:, j, :],
                                       start=(j == TB - 1 and m == 0), stop=(j == 0), skip_group_check=True)
                    if j == 0:
                        mm.then_inc(bt_ps, 1)

                def pe_square(pe, bank, lhs, rhs, done):
                    for m in range(CB):
                        for k in range(CB):
                            mm = pe.matmul(ps[:, bank, m * C:(m + 1) * C], lhs[:, k, blk(m)], rhs[:, k, :],
                                           start=(k == 0), stop=(k == CB - 1))
                    mm.then_inc(done, 1)

                def pe_tokens(pe, bank, half, lhs, rhs, done):
                    for q in range(2):
                        for k in range(CB):
                            mm = pe.matmul(ps[:, bank, q * C:(q + 1) * C], lhs[:, k, blk(2 * half + q)], rhs[:, k, :],
                                           start=(k == 0), stop=(k == CB - 1))
                    mm.then_inc(done, 1)

                def pe_ffn(pe, i, h):
                    if h == 0:
                        for k in range(CB):
                            pe.wait_ge(x3h_ev[k], i)
                            pe.wait_ge(x3l_ev[k], i)
                    else:
                        pe.wait_ge(sg_ev[h - 1], i)
                    for w, bank, done in ((wgT, FG, gate_ps[h]), (wuT, FU, up_ps[h])):
                        if bank == FU and h:
                            pe.wait_ge(hf_ev[h - 1], i)
                        for k in range(CB):
                            for part in (x3h, x3l):
                                mm = pe.matmul(ps[:, bank, :], w[:, k, blk(h)], part[:, k, :],
                                               start=(k == 0 and part is x3h), stop=(k == CB - 1 and part is x3l))
                        mm.then_inc(done, 1)

                def pe_down(pe, i, half):
                    if half == 0:
                        for h in range(HB):
                            pe.wait_ge(hh_ev[h], i)
                            pe.wait_ge(hl_ev[h], i)
                    for q in range(2):
                        for h in range(HB):
                            for part in (hh, hl):
                                mm = pe.matmul(ps[:, FO0 + half, q * C:(q + 1) * C], part[:, h, blk(2 * half + q)],
                                               wdT[:, h, :], start=(h == 0 and part is hh),
                                               stop=(h == HB - 1 and part is hl))
                    mm.then_inc(fo_ps[half], 1)

                def pe_body(pe, i, att, ffn):
                    if ffn:
                        pe.wait_ge(xh2_done, i)
                        wait(pe, ot_ev[0], i - 1)
                        wait(pe, ot_ev[1], i - 1)
                        pe_transposes(pe, (FO0, FO1), xh2, t2_ps)
                    if att:
                        pe.wait_ge(inv_in, (i + 1) * 16 * QPB)
                        wait(pe, a0_ev[TB - 1], i)
                        for j in range(TB):
                            mm = pe.transpose(ps[:, A2, blk(j)], x32[:, j, :], ident[:, :])
                        mm.then_inc(xT_ps, 1)
                        pe.wait_ge(gg_in, (i + 1) * 16)
                        wait(pe, a0_ev[1], i)
                        for j in range(TB):
                            mm = pe.matmul(ps[:, A0, blk(j)], diag(j), x32[:, j, :], start=True, stop=True)
                        mm.then_inc(p32_ps, 1)
                    if ffn:
                        pe.wait_ge(t2_ev[0], i)
                        pe.wait_ge(t2_ev[1], i)
                        wait(pe, sg_ev[HB - 1], i - 1)
                        wait(pe, hf_ev[HB - 1], i - 1)
                        for m in range(CB):
                            for k in range(CB):
                                mm = pe.matmul(ps[:, FG + m, :], w1f[:, k, blk(m)], xh2T[:, k, :],
                                               start=(k == 0), stop=(k == CB - 1))
                            mm.then_inc(m1_ps[m], 1)
                    if att:
                        pe.wait_ge(p32_ev, i + 1)
                        pe.wait_ge(xT_ev, i + 1)
                        wait(pe, m2_ev, i)
                        for j in range(TB):
                            mm = pe.matmul(ps[:, A1, blk(j)], xT32[:, j, :], p1[:, j, :], start=True, stop=True)
                        mm.then_inc(x64_ps, 1)
                        for j in range(TB):
                            mm = pe.matmul(ps[:, A2, blk(j)], p1[:, j, :], xT32[:, j, :], start=True, stop=True)
                        mm.then_inc(xT64_ps, 1)
                    if ffn:
                        pe.wait_ge(h1_ev[0], i)
                        pe.wait_ge(h1_ev[1], i)
                        pe_tokens(pe, FO0, 0, h1, w2f, mo_ps[0])
                    if att:
                        pe.wait_ge(x64_ev, i + 1)
                        for j in range(TB):
                            mm = pe.matmul(ps[:, A0, blk(j)], diag(j), x64[:, j, :], start=True, stop=True)
                        mm.then_inc(p64_ps, 1)
                    if ffn:
                        pe_tokens(pe, FO1, 1, h1, w2f, mo_ps[1])
                    if att:
                        pe.wait_ge(p64_ev, i + 1)
                        pe.wait_ge(xT64_ev, i + 1)
                        for j in range(TB):
                            mm = pe.matmul(ps[:, A1, blk(j)], xT64[:, j, :], p1[:, j, :], start=True, stop=True)
                        mm.then_inc(x128_ps, 1)
                        pe.wait_ge(xhm_done, i + 1)
                        if ffn:
                            pe.wait_ge(h1_ev[0], i)
                            pe.wait_ge(h1_ev[1], i)
                        pe_transposes(pe, (FG, FU), xh, ht_ps)
                        pe.wait_ge(x128_ev, i + 1)
                        pe_zstep(pe, i, 3)
                        pe_wstep(pe, i, 2)
                        pe_bt(pe, i, 3)
                        pe_zstep(pe, i, 2)
                        pe_wstep(pe, i, 1)
                    if ffn:
                        pe.wait_ge(xh3_done, i)
                        for j in range(TB):
                            pe.wait_ge(x2_ev[j], i)
                        pe_transposes(pe, (FO0, FO1), xh3, t3_ps)
                    if att:
                        pe_bt(pe, i, 2)
                        pe.wait_ge(ht_ev[0], i + 1)
                        pe.wait_ge(ht_ev[1], i + 1)
                        pe_zstep(pe, i, 1)
                    if ffn:
                        pe_ffn(pe, i, 0)
                    if att:
                        pe_wstep(pe, i, 0)
                    if ffn:
                        pe_ffn(pe, i, 1)
                    if att:
                        pe_bt(pe, i, 1)
                        pe_zstep(pe, i, 0)
                    if ffn:
                        pe_ffn(pe, i, 2)
                    if att:
                        pe_bt(pe, i, 0)
                    if ffn:
                        pe_ffn(pe, i, 3)
                    if att:
                        pe.wait_ge(bt_ev, i + 1)
                        pe_square(pe, A0, bt, wvo, e_ps)
                    if ffn:
                        pe_ffn(pe, i, 4)
                    if att:
                        pe.wait_ge(e_ev, i + 1)
                        pe_square(pe, A1, wqT, e_, m2_ps)
                    if ffn:
                        pe_ffn(pe, i, 5)
                    if att:
                        pe.wait_ge(m2_ev, i + 1)
                        pe_tokens(pe, A0, 0, xhT, m2, y_ps[0])
                        pe_tokens(pe, A2, 1, xhT, m2, y_ps[1])
                    if ffn:
                        pe_down(pe, i, 0)
                        pe_down(pe, i, 1)

                @block.tensor
                def _(pe):
                    overlapped(pe_body)(pe)

                def act_ffn(act, i, h):
                    act.wait_ge(gate_ps[h], i)
                    wait(act, hf_ev[h - 2 if h >= 2 else HB - 2 + h], i if h >= 2 else i - 1)
                    act.activation(sg[:, h % 2, :], ps[:, FG, :], ACT.Silu, scale=QUANT).then_inc(sg_ev[h], 1)

                def act_hh(act, i, h):
                    act.wait_ge(hf_ev[h], i)
                    wait(act, fo_ps[1], i - 1)
                    act.activation(hh[:, h, :], hf[:, h % 2, :], ACT.Copy).then_inc(hh_ev[h], 1)

                def act_z(act, i, j):
                    act.wait_ge(z_ps[j], i + 1)
                    wait(act, bt_ps, i)
                    act.activation(z[:, j, :], ps[:, A1, 0:C], ACT.Copy).then_inc(z_ev[j], 1)

                def act_body(act, i, att, ffn):
                    if ffn:
                        act.wait_ge(t2_ps[0], i)
                        act.activation(xh2T[:, 0, :], ps[:, FO0, :], ACT.Copy).then_inc(t2_ev[0], 1)
                    if att:
                        act.wait_ge(xT_ps, i + 1)
                        act.activation(xT32[:, :, :].rearrange("p j c -> p (j c)"), ps[:, A2, :], ACT.Copy).then_inc(xT_ev, 1)
                    if ffn:
                        for m in range(CB):
                            act.wait_ge(m1_ps[m], i)
                            if m == 0:
                                wait(act, mo_ps[1], i - 1)
                            act.activation(h1[:, m, :], ps[:, FG + m, :], ACT.Relu, bias=b1f[:, m:m + 1]).then_inc(h1_ev[m], 1)
                    if att:
                        act.wait_ge(ht_ps[0], i + 1)
                        wait(act, y_ps[1], i)
                        act.activation(xhT[:, 0, :], ps[:, FG, :], ACT.Copy).then_inc(ht_ev[0], 1)
                        act_z(act, i, 3)
                        act_z(act, i, 2)
                    if ffn:
                        for k in range(CB):
                            act.wait_ge(t3_ps[k], i)
                            act.activation(x3h[:, k, :], ps[:, FO0 + k, :], ACT.Copy).then_inc(x3h_ev[k], 1)
                    if att:
                        act_z(act, i, 1)
                    if ffn:
                        act_ffn(act, i, 0)
                        act_hh(act, i, 0)
                        act_ffn(act, i, 1)
                    if att:
                        act_z(act, i, 0)
                    if ffn:
                        act_hh(act, i, 1)
                        act_ffn(act, i, 2)
                        act_hh(act, i, 2)
                    if att:
                        act.wait_ge(bt_ps, i + 1)
                        act.activation(bt[:, :, :].rearrange("p k c -> p (k c)"), ps[:, A2, :], ACT.Copy).then_inc(bt_ev, 1)
                    if ffn:
                        act_ffn(act, i, 3)
                        act_hh(act, i, 3)
                    if att:
                        act.wait_ge(e_ps, i + 1)
                        act.activation(e_[:, :, :].rearrange("p k c -> p (k c)"), ps[:, A0, :], ACT.Copy).then_inc(e_ev, 1)
                    if ffn:
                        act_ffn(act, i, 4)
                        act_hh(act, i, 4)
                        act_ffn(act, i, 5)
                        act_hh(act, i, 5)

                @block.scalar
                def _(act):
                    overlapped(act_body)(act)

                def masked(dve, mask, src_ps, done, i):
                    dve.wait_ge(src_ps, i + 1)
                    if mask is mask64:
                        dve.wait_ge(xT64_ps, i + 1)
                    else:
                        wait(dve, x128_ps, i)
                    dve.tensor_tensor(p1[:, :, :], ps[:, A0, :].rearrange("p (j c) -> p j c", c=P),
                                      mask[:, :].unsqueeze(1).broadcast_to([P, TB, P]), ALU.mult).then_inc(done, 1)

                def plus(dve, dst, bank, src, src_ps, done, i):
                    dve.wait_ge(src_ps, i + 1)
                    dve.tensor_tensor(dst[:, :, :], ps[:, bank, :].rearrange("p (j c) -> p j c", c=P), src[:, :, :],
                                      ALU.add).then_inc(done, 1)

                def dve_w(dve, i, j):
                    dve.wait_ge(w_ps[j], i + 1)
                    dve.scalar_tensor_tensor(out=wt[:, j, :], in0=kx3[:, j, :], scalar=kx[:, E_LR + j:E_LR + j + 1],
                                             in1=ps[:, A0, 0:C], op0=ALU.mult, op1=ALU.subtract).then_inc(w_ev[j], 1)

                def dve_stats(dve, n_done, bst_, mv_, bns, mvd):
                    for j in range(TB):
                        dve.wait_ge(ready, 1)
                        dve.wait_ge(bns[j], n_done)
                        agg = dve.bn_aggr(mv_[:, j, :], bst_[:, j, :])
                    agg.then_inc(mvd, 1)

                def dve_x2(dve, i, half):
                    dve.wait_ge(mo_ps[half], i)
                    if half == 0:
                        dve.wait_ge(xa_done, i)
                        wait(dve, ot_ev[1], i - 1)
                        wait(dve, ln3_done, i - 1)
                    for j in (2 * half, 2 * half + 1):
                        dve.scalar_tensor_tensor(out=x2[:, j, :], in0=xa2[:, j, :], scalar=shf[:, j:j + 1],
                                                 in1=ps[:, FO0 + half, (j % 2) * C:(j % 2 + 1) * C],
                                                 op0=ALU.add, op1=ALU.add).then_inc(x2_ev[j], 1)
                    for j in (2 * half, 2 * half + 1):
                        dve.wait_ge(x2_ev[j], i)
                        dve.bn_stats(bs3[:, j, :], x2[:, j, :]).then_inc(bn3[j], 1)

                def dve_up(dve, i, h):
                    dve.wait_ge(up_ps[h], i)
                    dve.wait_ge(sg_ev[h], i)
                    prev, n = (h - 2, i) if h >= 2 else (HB - 2 + h, i - 1)
                    wait(dve, hh_ev[prev], n)
                    wait(dve, hl_ev[prev], n)
                    dve.tensor_tensor(hf[:, h % 2, :], ps[:, FU, :], sg[:, h % 2, :], ALU.mult).then_inc(hf_ev[h], 1)

                def dve_body(dve, i, att, ffn):
                    if ffn:
                        dve.wait_ge(t2_ps[1], i)
                        dve.tensor_copy(xh2T[:, 1, :], ps[:, FO1, :]).then_inc(t2_ev[1], 1)
                    if att:
                        masked(dve, mask32, p32_ps, p32_ev, i)
                        dve.wait_ge(kx_in, (i + 1) * 16)
                        wait(dve, z_ps[3], i)
                        dve.tensor_scalar(wt[:, 3, :], kx3[:, 3, :], kx[:, E_LR + 3:E_LR + 4], None,
                                          ALU.mult).then_inc(w_ev[3], 1)
                        plus(dve, x64, A1, x32, x64_ps, x64_ev, i)
                        plus(dve, xT64, A2, xT32, xT64_ps, xT64_ev, i)
                    if ffn:
                        dve_x2(dve, i, 0)
                    if att:
                        masked(dve, mask64, p64_ps, p64_ev, i)
                    if ffn:
                        dve_x2(dve, i, 1)
                        dve_stats(dve, i, bs3, mv3, bn3, mv3_done)
                    if att:
                        plus(dve, x128, A1, x64, x128_ps, x128_ev, i)
                        dve.wait_ge(ht_ps[1], i + 1)
                        wait(dve, y_ps[1], i)
                        dve.tensor_copy(xhT[:, 1, :], ps[:, FU, :]).then_inc(ht_ev[1], 1)
                        dve_w(dve, i, 2)
                        dve_w(dve, i, 1)
                    if ffn:
                        for k in range(CB):
                            dve.wait_ge(x3h_ev[k], i)
                            dve.tensor_tensor(x3l[:, k, :], ps[:, FO0 + k, :], x3h[:, k, :].bitcast(F32),
                                              ALU.subtract).then_inc(x3l_ev[k], 1)
                        dve_up(dve, i, 0)
                    if att:
                        dve_w(dve, i, 0)
                    if ffn:
                        for h in range(1, 5):
                            dve_up(dve, i, h)
                    if att:
                        dve.wait_ge(m2_ps, i + 1)
                        dve.tensor_tensor(m2[:, :, :], ps[:, A1, :].rearrange("p (k c) -> p k c", c=C),
                                          bo_bc[:, :].unsqueeze(1).broadcast_to([P, CB, C]), ALU.add).then_inc(m2_ev, 1)
                    if ffn:
                        dve_up(dve, i, 5)
                    if att:
                        dve.wait_ge(xin, (i + 1) * 16)
                        wait(dve, xh2_done, i)
                        wait(dve, xa_done, i)
                        wait(dve, ln2_done, i)
                        for j in range(TB):
                            if j % 2 == 0:
                                dve.wait_ge(y_ps[j // 2], i + 1)
                            dve.scalar_tensor_tensor(out=a0[:, j, :], in0=xt[:, j, :], scalar=kx[:, E_R1 + j:E_R1 + j + 1],
                                                     in1=ps[:, (A0, A2)[j // 2], (j % 2) * C:(j % 2 + 1) * C],
                                                     op0=ALU.mult, op1=ALU.add).then_inc(a0_ev[j], 1)
                        for j in range(TB):
                            dve.wait_ge(a0_ev[j], i + 1)
                            dve.bn_stats(bs2[:, j, :], a0[:, j, :]).then_inc(bn2[j], 1)
                        dve_stats(dve, i + 1, bs2, mv2, bn2, mv2_done)
                    if ffn:
                        wait(dve, out_st, 16 * (i - 1))
                        for half in range(2):
                            dve.wait_ge(fo_ps[half], i)
                            dve.scalar_tensor_tensor(
                                out=ot[:, 2 * half:2 * half + 2, :].rearrange("p j c -> p (j c)"), in0=ps[:, FO0 + half, :],
                                scalar=QUANT * QUANT, in1=x2[:, 2 * half:2 * half + 2, :].rearrange("p j c -> p (j c)"),
                                op0=ALU.mult, op1=ALU.add).then_inc(ot_ev[half], 1)

                @block.vector
                def _(dve):
                    overlapped(dve_body)(dve)

                def pool_norm(pool, n_done, read, n_read, mv_, ls, sc, steps, mvd, done):
                    for k in range(CB):
                        wait(pool, read[k], n_read)
                    pool.wait_ge(mvd, n_done)
                    pool.tensor_tensor(ls[:, 0, :], mv_[:, :, 1], eps4[:, :], ALU.add).then_inc(steps[0], 1)
                    pool.wait_ge(steps[0], n_done)
                    pool.tensor_tensor(sc[:, 0, :], ls[:, 0, :], mhalf4[:, :], ALU.pow).then_inc(steps[1], 1)
                    pool.wait_ge(steps[1], n_done)
                    pool.tensor_tensor(ls[:, 1, :], sc[:, 0, :], mv_[:, :, 0], ALU.mult).then_inc(steps[2], 1)
                    pool.wait_ge(steps[2], n_done)
                    pool.tensor_tensor(sc[:, 1, :], zero4[:, :], ls[:, 1, :], ALU.subtract).then_inc(done, 1)

                def pool_scale(pool, n_done, dst, src, scale, shift, made):
                    pool.wait_ge(ready, 1)
                    pool.wait_ge(made, n_done)
                    for j in range(TB):
                        op = pool.tensor_scalar(dst[:, j, :], src[:, j, :], scale[:, j:j + 1], shift[:, j:j + 1],
                                                ALU.mult, ALU.add)
                    return op

                def pool_body(pool, i, att, ffn):
                    if att:
                        pool.wait_ge(xin, (i + 1) * 16)
                        wait(pool, xa_done, i)
                        pool.tensor_tensor(xa[:, :, :], xt[:, :, :], b2_bc[:, :].unsqueeze(1).broadcast_to([P, TB, C]),
                                           ALU.add).then_inc(xb_done, 1)
                        pool.wait_ge(ready, 1)
                        for k in range(CB):
                            wait(pool, ht_ps[k], i)
                        wait(pool, bt_ps, i)
                        pool.wait_ge(kx_in, (i + 1) * 16)
                        for j in range(TB):
                            op = pool.tensor_scalar(xh[:, j, :], xt[:, j, :], kx[:, E_S + j:E_S + j + 1],
                                                    kx[:, E_B + j:E_B + j + 1], ALU.mult, ALU.add)
                        op.then_inc(xhm_done, 1)
                    if ffn:
                        pool_norm(pool, i, t3_ps, i - 1, mv3, ls3, sc3, l3, mv3_done, ln3_done)
                        pool_scale(pool, i, xh3, x2, sc3[:, 0, :], sc3[:, 1, :], ln3_done).then_inc(xh3_done, 1)
                    if ffn:
                        for h in range(HB):
                            pool.wait_ge(hh_ev[h], i)
                            wait(pool, fo_ps[1], i - 1)
                            pool.tensor_tensor(hl[:, h, :], hf[:, h % 2, :], hh[:, h, :].bitcast(F32),
                                               ALU.subtract).then_inc(hl_ev[h], 1)
                    if att:
                        pool_norm(pool, i + 1, t2_ps, i, mv2, ls2, sc2, l2, mv2_done, ln2_done)
                        pool_scale(pool, i + 1, xh2, a0, sc2[:, 0, :], sc2[:, 1, :], ln2_done).then_inc(xh2_done, 1)
                        for j in range(TB):
                            wait(pool, x2_ev[j], i)
                        pool.wait_ge(xb_done, i + 1)
                        pool.tensor_tensor(shf[:, :], kx[:, E_SH:E_SH + TB], zero4[:, :], ALU.add).then_inc(sh_done, 1)
                        pool.tensor_tensor(xa2[:, :, :], xa[:, :, :], a0[:, :, :], ALU.add).then_inc(xa_done, 1)

                @block.gpsimd
                def _(pool):
                    overlapped(pool_body)(pool)

                def load_inv(sp, n):
                    for a in range(QPB):
                        sp.dma_start(x32[a * SUB:(a + 1) * SUB, :, a * SUB:(a + 1) * SUB], inv_v[n][a]).then_inc(inv_in, 16)

                def load_next(sp, n):
                    sp.wait_ge(x64_ev, n)
                    load_inv(sp, n)
                    sp.wait_ge(w_ps[0], n)
                    sp.dma_start(gg[:, :], gg_d[n]).then_inc(gg_in, 16)
                    sp.wait_ge(a0_ev[TB - 1], n)
                    sp.wait_ge(xhm_done, n)
                    sp.wait_ge(sh_done, n)
                    sp.wait_ge(w_ev[0], n)
                    sp.dma_start(kx[:, :], kx_d[n]).then_inc(kx_in, 16)
                    sp.wait_ge(xb_done, n)
                    sp.dma_start(xt[:, :, :], x_v[n]).then_inc(xin, 16)

                def store_out(sp, n):
                    sp.wait_ge(ot_ev[0], n + 1)
                    sp.wait_ge(ot_ev[1], n + 1)
                    sp.dma_start(out_v[n], ot[:, :, :]).then_inc(out_st, 16)

                @block.sync
                def _(sp):
                    load_inv(sp, 0)
                    sp.dma_start(gg[:, :], gg_d[0]).then_inc(gg_in, 16)
                    sp.dma_start(kx[:, :], kx_d[0]).then_inc(kx_in, 16)
                    sp.dma_start(xt[:, :, :], x_v[0]).then_inc(xin, 16)
                    load_next(sp, 1)
                    with sp.Fori(1, NS - 1) as i:
                        load_next(sp, i + 1)
                        store_out(sp, i - 1)
                    store_out(sp, NS - 2)
                    store_out(sp, NS - 1)
                    sp.wait_ge(out_st, 16 * NS)


_INS = ['L0_attn_x', 'L0_attn_dn_g', 'L0_attn_dn_b', 'L0_attn_gates_w', 'L0_attn_gates_b', 'L0_attn_lr_w',
        'L0_attn_lr_b', 'L0_attn_out_w', 'L0_attn_out_b', 'L0_attn_mn_g', 'L0_attn_mn_b', 'L0_attn_w1', 'L0_attn_b1',
        'L0_attn_w2', 'L0_attn_b2', 'L0_ffn_w_gate', 'L0_ffn_w_up', 'L0_ffn_w_down']


def kernel(**inputs):
    import numpy as _np
    import concourse.bacc as _bacc
    from concourse import mybir as _mybir
    from concourse.bass_utils import run_bass_kernel_spmd as _run

    nc = _bacc.Bacc("TRN2", target_bir_lowering=False, num_devices=1)
    arrays, args = {}, []
    for name in _INS:
        a = _np.ascontiguousarray(inputs[name])
        arrays[f"in_{name}_dram"] = a
        args.append(nc.dram_tensor(f"in_{name}_dram", a.shape, _mybir.dt.from_np(a.dtype), kind="ExternalInput").ap())
    shape = arrays["in_L0_attn_x_dram"].shape
    args.append(nc.dram_tensor("out_0_dram", shape, _mybir.dt.float32, kind="ExternalOutput").ap())
    delta_block_kernel(nc, *args)
    r = _run(nc, [arrays], core_ids=[0])
    return r.results[0]["out_0_dram"]
```

```python
from contextlib import ExitStack

import concourse.bass as bass
from concourse import mybir

ALU = mybir.AluOpType
ACT = mybir.ActivationFunctionType
F32 = mybir.dt.float32
F32R = mybir.dt.float32r
I32 = mybir.dt.int32

P = 128
EPS = 1e-5
QUANT = 1.0 / 127.0
SUB = 32
A0, A1, A2, S0, FG, FU, FO0, FO1 = range(8)


def wait(eng, sem, value):
    if isinstance(value, int) and value <= 0:
        return
    eng.wait_ge(sem, value)


def delta_block_kernel(nc, x, dn_g, dn_b, gates_w, gates_b, lr_w, lr_b, out_w, out_b, mn_g, mn_b,
                       w1, b1, w2, b2, w_gate, w_up, w_down, out):
    NS, T, C = x.shape
    H = w_gate.shape[0]
    TB, CB, HB = T // P, C // P, H // P
    LR, V0, WALL = 2 * C, 2 * C + 2, 3 * C + 2
    OFF = TB * P
    ROW = {3: OFF, 2: OFF + 3 * P, 1: OFF + 5 * P}
    GCOL = {(i, j): ROW[i] + j * P for i in ROW for j in range(i)}
    GW = OFF + 6 * P
    KXE = TB * C
    E_LR, E_S, E_B, E_R1, E_SH = (KXE + TB * q for q in range(5))
    KXW = KXE + 5 * TB
    NSUB = T // SUB
    GROUP = P // NSUB
    SLOTS = NS // GROUP
    QPB = P // SUB
    assert TB == 4 and CB == 2 and NS % GROUP == 0 and NS >= 3

    kx_d = nc.dram_tensor("kx_scratch", [NS, P, KXW], F32, kind="Internal").ap()
    gg_d = nc.dram_tensor("gg_scratch", [NS, P, GW], F32, kind="Internal").ap()
    low_d = nc.dram_tensor("low_scratch", [NS * NSUB, SUB * SUB], F32, kind="Internal").ap()
    inv_d = nc.dram_tensor("inv_scratch", [NS * NSUB, SUB * SUB], F32, kind="Internal").ap()
    x_v = x.rearrange("n (j p) c -> n p j c", p=P)
    out_v = out.rearrange("n (j p) c -> n p j c", p=P)
    low_v = low_d.rearrange("(n j a) (r c) -> n a r j c", j=TB, a=QPB, c=SUB)
    inv_v = inv_d.rearrange("(n j a) (r c) -> n a r j c", j=TB, a=QPB, c=SUB)
    low_lane = low_d.rearrange("(s l) e -> l s e", l=P)
    inv_lane = inv_d.rearrange("(s l) e -> l s e", l=P)

    with ExitStack() as ctx:
        def sb(name, shape, dt=F32, c=ctx):
            return c.enter_context(nc.sbuf_tensor(name, shape, dt))

        held = []

        def sem(name):
            held.append(nc.alloc_semaphore(name=name))
            return held[-1]

        def sems(name, n):
            return [sem(f"{name}{k}") for k in range(n)]

        def end_program():
            nc.clear_and_free_semaphores(held)
            held.clear()
            nc.all_engine_barrier()

        ps = ctx.enter_context(nc.psum_tensor("ps", [P, 8, 512], F32))

        ident = sb("ident", [P, P])
        mask32 = sb("mask32", [P, P])
        mask64 = sb("mask64", [P, P])
        eps4 = sb("eps4", [P, TB])
        mhalf4 = sb("mhalf4", [P, TB])
        zero4 = sb("zero4", [P, TB])
        one4 = sb("one4", [P, TB])
        b1f = sb("b1f", [P, CB])

        def pair(name, shape, c=ctx):
            return sb(name + "_hi", shape, F32R, c=c), sb(name + "_lo", shape, F32R, c=c)

        wk2 = pair("wk", [P, CB, C + 2])
        wqT2 = pair("wqT", [P, CB, C])
        wvo2 = pair("wvo", [P, CB, C])
        w12 = pair("w1", [P, CB, C])
        w22 = pair("w2", [P, CB, C])
        bo_bc = sb("bo_bc", [P, C])
        b2_bc = sb("b2_bc", [P, C])
        wgT = sb("wgT", [P, CB, H], F32R)
        wuT = sb("wuT", [P, CB, H], F32R)
        wdT = sb("wdT", [P, HB, C], F32R)

        xt = sb("xt", [P, TB, C])
        xh = sb("xh", [P, TB, C])
        xhT2 = pair("xhT", [P, CB, T])
        kx = sb("kx", [P, KXW])
        gg = sb("gg", [P, GW])
        x32 = sb("x32", [P, TB, P])
        kx3 = kx[:, 0:KXE].rearrange("p (j c) -> p j c", j=TB)
        ready = ctx.enter_context(nc.semaphore("ready"))

        def three(a2, b2):
            return ((a2[0], b2[0]), (a2[0], b2[1]), (a2[1], b2[0]))

        def split_matmul(pe, dst, a2, a_at, b2, b_at, start, stop, **kw):
            n = 3 * len(a_at)
            for ka, kb in zip(a_at, b_at):
                for a, b in three(a2, b2):
                    n -= 1
                    mm = pe.matmul(dst, a[ka], b[kb], start=start, stop=(stop and n == 0), **kw)
                    start = False
            return mm

        with ExitStack() as sx:
            wall = sb("wall", [P, CB, WALL], c=sx)
            brow = sb("brow", [1, WALL], c=sx)
            dcol = sb("dcol", [P, 2, CB], c=sx)
            mcol = sb("mcol", [P, 3, CB], c=sx)
            wo = sb("wo", [P, CB, C], c=sx)
            w1raw = sb("w1raw", [P, CB, C], c=sx)
            borow = sb("borow", [P, C], c=sx)
            wgi = sb("wgi", [P, HB, C], I32, c=sx)
            wui = sb("wui", [P, HB, C], I32, c=sx)
            wdi = sb("wdi", [P, CB, H], I32, c=sx)
            wgf = sb("wgf", [P, HB, C], c=sx)
            wuf = sb("wuf", [P, HB, C], c=sx)
            wdf = sb("wdf", [P, CB, H], c=sx)
            ones = sb("ones", [P, P], c=sx)
            diff = sb("diff", [P, CB], c=sx)
            diff_bc = sb("diff_bc", [P, CB, P], c=sx)
            shift = sb("shift", [P, WALL], c=sx)
            wfold = sb("wfold", [P, CB, WALL], c=sx)
            wvT = sb("wvT", [P, CB, C], c=sx)
            wqT = sb("wqT", [P, CB, C], c=sx)
            wvo = sb("wvo", [P, CB, C], c=sx)
            w1f = sb("w1f", [P, CB, C], c=sx)
            w2f = sb("w2f", [P, CB, C], c=sx)
            split_hi, split_done = sem("split_hi"), sem("split_done")
            minus = sem("minus")
            pads, loaded, ints_in = sem("pads"), sem("loaded"), sem("ints_in")
            ones_set, zeroed, diff_done, diff_bc_done = sem("ones_set"), sem("zeroed"), sem("diff_done"), sem("diff_bc_done")
            shift_ps, shift_done, fold_done = sem("shift_ps"), sem("shift_done"), sem("fold_done")
            id_done, tq_ps, tq_done, vo_ps, vo_done = sem("id_done"), sem("tq_ps"), sem("tq_done"), sem("vo_ps"), sem("vo_done")
            b1_ps, misc, ints_f, wt_ps, wt_ev, x32_zero = sem("b1_ps"), sem("misc"), sem("ints_f"), sem("wt_ps"), sem("wt_ev"), sem("x32_zero")
            with nc.Block() as block:
                @block.sync
                def _(sp):
                    sp.wait_ge(pads, 2)
                    gv = gates_w.rearrange("(k p) o -> p k o", p=P)
                    col = lambda v: v.rearrange("(k p) -> p k", p=P)
                    row = lambda v: v.rearrange("(a c) -> a c", a=1)
                    for dst, src in (
                        (wall[:, :, 0:2 * C], gv[:, :, 0:2 * C]),
                        (wall[:, :, V0:WALL], gv[:, :, 2 * C:3 * C]),
                        (wall[:, :, LR:LR + 1], lr_w.rearrange("(k p) o -> p k o", p=P)),
                        (brow[:, 0:2 * C], row(gates_b)[:, 0:2 * C]),
                        (brow[:, V0:WALL], row(gates_b)[:, 2 * C:3 * C]),
                        (brow[:, LR:LR + 1], row(lr_b)),
                        (dcol[:, 0, :], col(dn_g)), (dcol[:, 1, :], col(dn_b)),
                        (mcol[:, 0, :], col(mn_g)), (mcol[:, 1, :], col(mn_b)), (mcol[:, 2, :], col(b1)),
                        (wo[:, :, :], out_w.rearrange("(k p) o -> p k o", p=P)),
                        (w1raw[:, :, :], w1.rearrange("(k p) o -> p k o", p=P)),
                        (w2f[:, :, :], w2.rearrange("(k p) o -> p k o", p=P)),
                        (borow[:, :], row(out_b).partition_broadcast(P)),
                        (b2_bc[:, :], row(b2).partition_broadcast(P)),
                    ):
                        with nc.allow_non_contiguous_dma(reason="a few columns, once"):
                            sp.dma_start(dst, src).then_inc(loaded, 16)
                    sp.dma_start(wgi[:, :, :], w_gate.rearrange("(h p) c -> p h c", p=P)).then_inc(ints_in, 16)
                    sp.dma_start(wui[:, :, :], w_up.rearrange("(h p) c -> p h c", p=P)).then_inc(ints_in, 16)
                    sp.dma_start(wdi[:, :, :], w_down.rearrange("(k p) h -> p k h", p=P)).then_inc(ints_in, 16)
                    sp.wait_ge(loaded, 16 * 16)
                    sp.wait_ge(ints_in, 48)

                @block.gpsimd
                def _(pool):
                    pool.memset(wall[:, :, LR:V0], 0.0).then_inc(pads, 1)
                    pool.memset(brow[:, LR:V0], 0.0).then_inc(pads, 1)
                    pool.memset(ones[:, :], 1.0).then_inc(ones_set, 1)
                    pool.wait_ge(ones_set, 1)
                    pool.affine_select(out=ident[:, :], in_=ones[:, :], compare_op=ALU.is_equal, fill=0.0,
                                       base=0, pattern=[[-1, P]], channel_multiplier=1).then_inc(id_done, 1)
                    pool.memset(mask32[:, :], 0.0).then_inc(zeroed, 1)
                    pool.memset(mask64[:, :], 0.0).then_inc(zeroed, 1)
                    pool.wait_ge(zeroed, 2)
                    pool.memset(mask32[SUB:2 * SUB, 0:SUB], -1.0)
                    pool.memset(mask32[3 * SUB:4 * SUB, 2 * SUB:3 * SUB], -1.0).then_inc(minus, 1)
                    pool.wait_ge(minus, 1)
                    pool.memset(mask64[2 * SUB:4 * SUB, 0:2 * SUB], -1.0).then_inc(minus, 1)
                    pool.wait_ge(minus, 2)
                    pool.memset(eps4[:, :], EPS)
                    pool.memset(mhalf4[:, :], -0.5)
                    pool.memset(zero4[:, :], 0.0)
                    pool.memset(one4[:, :], 1.0)
                    pool.memset(x32[:, :, :], 0.0).then_inc(x32_zero, 1)
                    pool.wait_ge(x32_zero, 1)

                @block.vector
                def _(dve):
                    dve.wait_ge(ones_set, 1)
                    dve.wait_ge(loaded, 16 * 16)
                    dve.tensor_tensor(diff[:, :], dcol[:, 1, :], dcol[:, 0, :], ALU.subtract).then_inc(diff_done, 1)
                    dve.wait_ge(diff_done, 1)
                    for k in range(CB):
                        dve.tensor_scalar(diff_bc[:, k, :], ones[:, :], diff[:, k:k + 1], None,
                                          ALU.mult).then_inc(diff_bc_done, 1)
                    dve.tensor_scalar(bo_bc[:, :], borow[:, :], 1.0 / C, None, ALU.mult).then_inc(misc, 1)
                    for k in range(CB):
                        dve.tensor_scalar(w1f[:, k, :], w1raw[:, k, :], mcol[:, 0, k:k + 1], None,
                                          ALU.mult).then_inc(misc, 1)
                    dve.wait_ge(shift_done, 2)
                    for k in range(CB):
                        dve.scalar_tensor_tensor(out=wfold[:, k, :], in0=wall[:, k, :], scalar=dcol[:, 0, k:k + 1],
                                                 in1=shift[:, :], op0=ALU.mult, op1=ALU.add).then_inc(fold_done, 1)
                    dve.wait_ge(fold_done, CB)
                    dve.wait_ge(b1_ps, 1)
                    dve.tensor_tensor(b1f[:, :], ps[:, 3, 0:CB], mcol[:, 2, :], ALU.add).then_inc(misc, 1)
                    dve.wait_ge(tq_ps, 1)
                    dve.tensor_copy(wqT[:, :, :].rearrange("p a b -> p (a b)"), ps[:, 4, :]).then_inc(tq_done, 1)
                    dve.wait_ge(tq_ps, 2)
                    dve.tensor_copy(wvT[:, :, :].rearrange("p a b -> p (a b)"), ps[:, 5, :]).then_inc(tq_done, 1)
                    dve.wait_ge(vo_ps, 1)
                    dve.tensor_copy(wvo[:, :, :].rearrange("p a b -> p (a b)"), ps[:, 6, :]).then_inc(vo_done, 1)
                    dve.wait_ge(ints_in, 48)
                    dve.tensor_copy(wgf[:, :, :], wgi[:, :, :]).then_inc(ints_f, 1)
                    dve.tensor_copy(wuf[:, :, :], wui[:, :, :]).then_inc(ints_f, 1)
                    dve.tensor_copy(wdf[:, :, :], wdi[:, :, :]).then_inc(ints_f, 1)
                    dve.wait_ge(misc, 4)
                    dve.wait_ge(vo_done, 1)
                    dve.wait_ge(tq_done, 2)
                    whole = ((wfold[:, :, C:2 * C + 2], wk2), (wqT[:, :, :], wqT2), (wvo[:, :, :], wvo2),
                             (w1f[:, :, :], w12), (w2f[:, :, :], w22))
                    for w, (hi, lo) in whole:
                        dve.tensor_copy(hi[:, :, :], w).then_inc(split_hi, 1)
                    for n, (w, (hi, lo)) in enumerate(whole):
                        dve.wait_ge(split_hi, n + 1)
                        dve.tensor_tensor(lo[:, :, :], w, hi[:, :, :].bitcast(F32), ALU.subtract).then_inc(split_done, 1)
                    dve.wait_ge(split_done, len(whole))

                @block.scalar
                def _(act):
                    act.wait_ge(shift_ps, 1)
                    act.activation(shift[:, 0:512], ps[:, 0, :], ACT.Copy, scale=1.0 / C).then_inc(shift_done, 1)
                    act.activation(shift[:, 512:WALL], ps[:, 1, 0:WALL - 512], ACT.Copy, scale=1.0 / C).then_inc(shift_done, 1)
                    g = 0
                    for dst in (wgT, wuT):
                        for k in range(CB):
                            for n in range(0, HB, 2):
                                act.wait_ge(wt_ps, g + 1)
                                act.activation(dst[:, k, n * P:(n + 2) * P], ps[:, g % 2, 0:2 * P], ACT.Copy).then_inc(wt_ev, 1)
                                g += 1
                    for n in range(HB):
                        act.wait_ge(wt_ps, g + 1)
                        act.activation(wdT[:, n, :], ps[:, g % 2, 0:C], ACT.Copy).then_inc(wt_ev, 1)
                        g += 1

                @block.tensor
                def _(pe):
                    pe.wait_ge(loaded, 16 * 16)
                    pe.wait_ge(ones_set, 1)
                    pe.wait_ge(diff_bc_done, CB)
                    for bank, lo, hi in ((0, 0, 512), (1, 512, WALL)):
                        for k in range(CB):
                            pe.matmul(ps[:, bank, 0:hi - lo], diff_bc[:, k, :], wall[:, k, lo:hi], start=(k == 0), stop=False)
                        mm = pe.matmul(ps[:, bank, 0:hi - lo], ones[0:1, :], brow[:, lo:hi], start=False, stop=True)
                    mm.then_inc(shift_ps, 1)
                    for m in range(CB):
                        for k in range(CB):
                            mm = pe.matmul(ps[:, 3, m:m + 1], w1raw[:, k, m * P:(m + 1) * P], mcol[:, 1, k:k + 1],
                                           start=(k == 0), stop=(k == CB - 1))
                    mm.then_inc(b1_ps, 1)
                    pe.wait_ge(id_done, 1)
                    pe.wait_ge(fold_done, CB)
                    for bank, c0 in ((4, 0), (5, V0)):
                        for m in range(CB):
                            for k in range(CB):
                                mm = pe.transpose(ps[:, bank, m * C + k * P:m * C + (k + 1) * P],
                                                  wfold[:, k, c0 + m * P:c0 + (m + 1) * P], ident[:, :])
                        mm.then_inc(tq_ps, 1)
                    pe.wait_ge(tq_done, 2)
                    for m in range(CB):
                        for k in range(CB):
                            mm = pe.matmul(ps[:, 6, m * C:(m + 1) * C], wvT[:, k, m * P:(m + 1) * P], wo[:, k, :],
                                           start=(k == 0), stop=(k == CB - 1))
                    mm.then_inc(vo_ps, 1)
                    pe.wait_ge(ints_f, 3)
                    pe.wait_ge(shift_done, 2)
                    g = 0
                    for src in (wgf, wuf):
                        for k in range(CB):
                            for n in range(0, HB, 2):
                                wait(pe, wt_ev, g - 1)
                                for q in range(2):
                                    mm = pe.transpose(ps[:, g % 2, q * P:(q + 1) * P], src[:, n + q, k * P:(k + 1) * P], ident[:, :])
                                mm.then_inc(wt_ps, 1)
                                g += 1
                    for n in range(HB):
                        pe.wait_ge(wt_ev, g - 1)
                        for k in range(CB):
                            mm = pe.transpose(ps[:, g % 2, k * P:(k + 1) * P], wdf[:, k, n * P:(n + 1) * P], ident[:, :])
                        mm.then_inc(wt_ps, 1)
                        g += 1
                    pe.wait_ge(wt_ev, g)
                    pe.wait_ge(vo_done, 1)
                    pe.wait_ge(x32_zero, 1)
                    pe.nop().then_inc(ready, 1)
            end_program()

        with ExitStack() as kc:
            xk = sb("xk", [P, 2, TB, C], c=kc)
            bst = sb("bst", [P, 2, TB, 6], c=kc)
            mv = sb("mv", [P, TB, 2], c=kc)
            lns = sb("lns", [P, 8, TB], c=kc)
            exln = sb("exln", [P, 2, 4, TB], c=kc)
            sqj = sb("sqj", [P, TB, C], c=kc)
            ssq = sb("ssq", [P, TB], c=kc)
            rn = sb("rn", [P, TB], c=kc)
            knT2 = pair("knT", [P, CB, T], c=kc)
            x_in, kx_out, gg_out, low_out = sems("x_in", 2), sem("kx_out"), sem("gg_out"), sem("low_out")
            bn_done, bn_copied = sem("bn_done"), sem("bn_copied")
            mv_done, ln_done, xh_done = sem("mv_done"), sem("ln_done"), sem("xh_done")
            lstep, ln_half = sems("lstep", 8), sem("ln_half")
            xhT_ps, xhT_hi, xhT_lo = sems("xhT_ps", CB), sems("xhT_hi", CB), sems("xhT_lo", CB)
            k_ps, sq_done, rn_done = sems("k_ps", TB), sem("sq_done"), sem("rn_done")
            ex_done, lr_done, kn_done = sem("ex_done"), sem("lr_done"), sem("kn_done")
            knT_ps, knT_hi, knT_lo = sems("knT_ps", CB), sems("knT_hi", CB), sems("knT_lo", CB)
            g_ps, g_ev = sems("g_ps", 3), sems("g_ev", 3)
            T0, T1, K0, G0, G1 = 0, 1, 2, 6, 7
            GROW = {3: (G1, 0), 0: (G0, 0), 2: (G0, P), 1: (T0, 0)}

            def piped(body, tail):
                def run(eng):
                    body(eng, 0, 0, True, 2)
                    body(eng, 1, 1, False, 2)
                    with eng.Fori(1, NS // 2 - 1) as m:
                        body(eng, 2 * m, 0, False, 2)
                        body(eng, 2 * m + 1, 1, False, 2)
                    body(eng, NS - 2, 0, False, 1)
                    body(eng, NS - 1, 1, False, 0)
                    tail(eng)
                return run

            def x_count(n, par):
                return 8 * (n - par) + 16

            with nc.Block() as block:
                def load_x(sp, n, par):
                    sp.dma_start(xk[:, par, :, :], x_v[n]).then_inc(x_in[par], 16)

                def sp_stores(sp, n):
                    for q in range(3):
                        sp.wait_ge(g_ev[q], n + 1)
                    for a in range(QPB):
                        sp.dma_start(low_v[n][a], gg[a * SUB:(a + 1) * SUB, 0:OFF].rearrange("p (j c) -> p j c", c=P)
                                     [:, :, a * SUB:(a + 1) * SUB]).then_inc(low_out, 16)
                    sp.dma_start(gg_d[n], gg[:, :]).then_inc(gg_out, 16)

                def sp_body(sp, i, par, first, load):
                    if load:
                        sp.wait_ge(xh_done, i + 2)
                        load_x(sp, i + 3, 1 - par)
                    sp.wait_ge(kn_done, i + 1)
                    sp.dma_start(kx_d[i], kx[:, :]).then_inc(kx_out, 16)
                    if not first:
                        sp_stores(sp, i - 1)

                @block.sync
                def _(sp):
                    load_x(sp, 0, 0)
                    load_x(sp, 1, 1)
                    sp.wait_ge(xh_done, 1)
                    load_x(sp, 2, 0)
                    sp_body(sp, 0, 0, True, True)
                    sp_body(sp, 1, 1, False, True)
                    with sp.Fori(1, NS // 2 - 2) as m:
                        sp_body(sp, 2 * m, 0, False, True)
                        sp_body(sp, 2 * m + 1, 1, False, True)
                    for n in range(NS - 4, NS):
                        sp_body(sp, n, n % 2, False, n + 3 < NS)
                    sp_stores(sp, NS - 1)
                    sp.wait_ge(kx_out, 16 * NS)
                    sp.wait_ge(gg_out, 16 * NS)
                    sp.wait_ge(low_out, 16 * QPB * NS)

                def stats(dve, n, par):
                    dve.wait_ge(x_in[par], x_count(n, par))
                    wait(dve, ln_done, n)
                    for j in range(TB):
                        bn = dve.bn_stats(bst[:, 0, j, :], xk[:, par, j, :])
                    bn.then_inc(bn_done, 1)
                    dve.wait_ge(bn_done, n + 1)
                    dve.tensor_copy(bst[:, 1, :, :], bst[:, 0, :, :]).then_inc(bn_copied, 1)
                    for j in range(TB):
                        dve.wait_ge(ready, 1)
                        dve.wait_ge(bn_copied, n + 1)
                        agg = dve.bn_aggr(mv[:, j, :], bst[:, 1, j, :])
                    agg.then_inc(mv_done, 1)

                def rest(dve, dst2, bank, hi, lo, n):
                    for k in range(CB):
                        dve.wait_ge(hi[k], n + 1)
                        dve.tensor_tensor(dst2[1][:, k, :], ps[:, bank + k, :], dst2[0][:, k, :].bitcast(F32),
                                          ALU.subtract).then_inc(lo[k], 1)

                def dve_g(dve, n):
                    dve.wait_ge(g_ps[1], n + 1)
                    wait(dve, gg_out, 16 * n)
                    wait(dve, low_out, 16 * QPB * n)
                    dve.tensor_copy(gg[:, ROW[3]:ROW[3] + 3 * P], ps[:, G1, 0:3 * P])
                    dve.tensor_copy(gg[:, 3 * P:4 * P], ps[:, G1, 3 * P:4 * P]).then_inc(g_ev[1], 1)

                def dve_body(dve, i, par, first, left):
                    if not first:
                        rest(dve, knT2, G0, knT_hi, knT_lo, i - 1)
                    wait(dve, kx_out, 16 * i)
                    wait(dve, knT_ps[1], i)
                    dve.wait_ge(ln_done, i + 1)
                    dve.tensor_copy(kx[:, E_S:KXW], exln[:, par, :, :].rearrange("p q j -> p (q j)")).then_inc(ex_done, 1)
                    if left == 2:
                        stats(dve, i + 2, par)
                    dve.wait_ge(sq_done, i + 1)
                    dve.tensor_copy(kx[:, E_LR:E_LR + TB].rearrange("p (j o) -> p j o", o=1),
                                    ps[:, K0:K0 + TB, C:C + 1]).then_inc(lr_done, 1)
                    dve.wait_ge(rn_done, i + 1)
                    dve.tensor_tensor(kx3, ps[:, K0:K0 + TB, 0:C], rn[:, :].unsqueeze(2).broadcast_to([P, TB, C]),
                                      ALU.mult).then_inc(kn_done, 1)
                    if left:
                        rest(dve, xhT2, T0, xhT_hi, xhT_lo, i + 1)
                    if not first:
                        dve_g(dve, i - 1)

                @block.vector
                def _(dve):
                    stats(dve, 0, 0)
                    rest(dve, xhT2, T0, xhT_hi, xhT_lo, 0)
                    stats(dve, 1, 1)
                    piped(dve_body, lambda e: (
                        rest(e, knT2, G0, knT_hi, knT_lo, NS - 1), dve_g(e, NS - 1)))(dve)

                def act_g(act, n):
                    act.wait_ge(g_ps[0], n + 1)
                    wait(act, gg_out, 16 * n)
                    wait(act, low_out, 16 * QPB * n)
                    act.activation(gg[:, 0:OFF].rearrange("p (j c) -> p j c", c=P)[:, 0:3:2, :],
                                   ps[:, G0, :].rearrange("p (j c) -> p j c", c=P)[:, 0:4:3, :], ACT.Copy)
                    act.activation(gg[:, ROW[2]:ROW[2] + 2 * P], ps[:, G0, P:3 * P], ACT.Copy).then_inc(g_ev[0], 1)
                    act.wait_ge(g_ps[2], n + 1)
                    act.activation(gg[:, ROW[1]:ROW[1] + P], ps[:, T0, 0:P], ACT.Copy)
                    act.activation(gg[:, P:2 * P], ps[:, T0, P:2 * P], ACT.Copy).then_inc(g_ev[2], 1)

                def rounded(act, dst2, bank, src, hi, n):
                    for k in range(CB):
                        act.wait_ge(src[k], n + 1)
                        act.activation(dst2[0][:, k, :], ps[:, bank + k, :], ACT.Copy).then_inc(hi[k], 1)

                def make_xh(act, n, par):
                    act.wait_ge(ln_done, n + 1)
                    for k in range(CB):
                        wait(act, xhT_ps[k], n)
                    for j in range(TB):
                        op = act.activation(xh[:, j, :], xk[:, par, j, :], ACT.Identity,
                                            scale=exln[:, par, 0, j:j + 1], bias=exln[:, par, 1, j:j + 1])
                    op.then_inc(xh_done, 1)

                def act_body(act, i, par, first, left):
                    if not first:
                        wait(act, g_ps[2], i - 1)
                        rounded(act, knT2, G0, knT_ps, knT_hi, i - 1)
                    if left:
                        make_xh(act, i + 1, 1 - par)
                    wait(act, rn_done, i)
                    for j in range(TB):
                        act.wait_ge(k_ps[j], i + 1)
                        sq = act.activation(sqj[:, j, :], ps[:, K0 + j, 0:C], ACT.Square, accum_out=ssq[:, j:j + 1])
                    sq.then_inc(sq_done, 1)
                    if left:
                        rounded(act, xhT2, T0, xhT_ps, xhT_hi, i + 1)
                    if not first:
                        act_g(act, i - 1)

                @block.scalar
                def _(act):
                    make_xh(act, 0, 0)
                    rounded(act, xhT2, T0, xhT_ps, xhT_hi, 0)
                    piped(act_body, lambda e: (
                        e.wait_ge(g_ps[2], NS - 1),
                        rounded(e, knT2, G0, knT_ps, knT_hi, NS - 1), act_g(e, NS - 1)))(act)

                def norms(pool, n, par, half):
                    m, v = mv[:, :, 0], mv[:, :, 1]
                    L = [lns[:, q, :] for q in range(8)]
                    s_, b_, r1, sh = (exln[:, par, q, :] for q in range(4))
                    steps = [(L[0], v, eps4[:, :], ALU.add), (r1, L[0], mhalf4[:, :], ALU.pow),
                             (L[1], r1, r1, ALU.mult), (L[2], L[1], v, ALU.mult), (L[3], L[2], eps4[:, :], ALU.add),
                             (L[4], L[3], mhalf4[:, :], ALU.pow), (s_, L[4], r1, ALU.mult),
                             (L[5], s_, m, ALU.mult)]
                    if half == 0:
                        pool.wait_ge(mv_done, n + 1)
                        wait(pool, ex_done, n - 1)
                        wait(pool, xh_done, n - 1)
                    for q in range(5 * half, 5 + 3 * half):
                        o, a, b, op = steps[q]
                        pool.tensor_tensor(o, a, b, op).then_inc(lstep[q], 1)
                        pool.wait_ge(lstep[q], n + 1)
                    if half:
                        pool.tensor_tensor(b_, one4[:, :], L[5], ALU.subtract)
                        pool.tensor_tensor(L[6], m, r1, ALU.mult).then_inc(ln_half, 1)
                        pool.wait_ge(ln_half, n + 1)
                        pool.tensor_tensor(sh, zero4[:, :], L[6], ALU.subtract).then_inc(ln_done, 1)

                def pool_body(pool, i, par, first, left):
                    if left == 2:
                        norms(pool, i + 2, par, 0)
                    pool.wait_ge(sq_done, i + 1)
                    wait(pool, kn_done, i)
                    pool.tensor_tensor(rn[:, :], ssq[:, :], mhalf4[:, :], ALU.pow).then_inc(rn_done, 1)
                    if left == 2:
                        norms(pool, i + 2, par, 1)

                @block.gpsimd
                def _(pool):
                    for n in range(2):
                        norms(pool, n, n, 0)
                        norms(pool, n, n, 1)
                    piped(pool_body, lambda e: None)(pool)

                def pe_gram(pe, n):
                    for k in range(CB):
                        pe.wait_ge(knT_lo[k], n + 1)
                    def row(i):
                        bank, c0 = GROW[i]
                        w = (i + 1) * P
                        return split_matmul(pe, ps[:, bank, c0:c0 + w],
                                            knT2, [(slice(None), k, slice(i * P, w)) for k in range(CB)],
                                            knT2, [(slice(None), k, slice(0, w)) for k in range(CB)], True, True)
                    row(3).then_inc(g_ps[1], 1)
                    row(0)
                    row(2).then_inc(g_ps[0], 1)
                    pe.wait_ge(xhT_lo[0], min(n + 3, NS) if isinstance(n, int) else n + 3)
                    row(1).then_inc(g_ps[2], 1)

                def pe_knT(pe, n):
                    pe.wait_ge(kn_done, n + 1)
                    wait(pe, g_ev[0], n)
                    wait(pe, g_ev[1], n)
                    for k in range(CB):
                        for j in range(TB):
                            mm = pe.transpose(ps[:, G0 + k, j * P:(j + 1) * P], kx3[:, j, k * P:(k + 1) * P], ident[:, :])
                        mm.then_inc(knT_ps[k], 1)

                def pe_xhT(pe, n):
                    pe.wait_ge(xh_done, n + 1)
                    wait(pe, g_ev[2], n - 2)
                    for k in range(CB):
                        for j in range(TB):
                            mm = pe.transpose(ps[:, T0 + k, j * P:(j + 1) * P], xh[:, j, k * P:(k + 1) * P], ident[:, :])
                        mm.then_inc(xhT_ps[k], 1)

                def pe_body(pe, i, par, first, left):
                    if not first:
                        pe_knT(pe, i - 1)
                    for k in range(CB):
                        pe.wait_ge(xhT_lo[k], i + 1)
                    wait(pe, kn_done, i)
                    for j in range(TB):
                        split_matmul(pe, ps[:, K0 + j, 0:C + 2],
                                     xhT2, [(slice(None), k, slice(j * P, (j + 1) * P)) for k in range(CB)],
                                     wk2, [(slice(None), k, slice(None)) for k in range(CB)],
                                     True, True).then_inc(k_ps[j], 1)
                    if left:
                        pe_xhT(pe, i + 1)
                    if not first:
                        pe_gram(pe, i - 1)

                @block.tensor
                def _(pe):
                    pe_xhT(pe, 0)
                    piped(pe_body, lambda e: (
                        pe_knT(e, NS - 1), pe_gram(e, NS - 1)))(pe)
            end_program()

        with ExitStack() as ic:
            low = sb("low", [P, SLOTS, SUB * SUB], c=ic)
            inv = sb("inv", [P, SLOTS, SUB * SUB], c=ic)
            tmp = sb("tmp", [P, SLOTS, SUB // 2 * SUB // 2], c=ic)
            low_in, inv_out = sem("low_in"), sem("inv_out")
            inv_zero, inv_one, prod, subd = sem("inv_zero"), sem("inv_one"), sem("prod"), sem("subd")
            low4 = low[:, :, :].rearrange("p s (r c) -> p s r c", c=SUB)
            inv4 = inv[:, :, :].rearrange("p s (r c) -> p s r c", c=SUB)
            with nc.Block() as block:
                @block.sync
                def _(sp):
                    sp.dma_start(low[:, :, :], low_lane).then_inc(low_in, 16)
                    sp.wait_ge(subd, SUB - 1)
                    sp.dma_start(inv_lane, inv[:, :, :]).then_inc(inv_out, 16)
                    sp.wait_ge(inv_out, 16)

                @block.vector
                def _(dve):
                    dve.memset(inv[:, :, :], 0.0).then_inc(inv_zero, 1)
                    dve.wait_ge(inv_zero, 1)
                    dve.memset(inv[:, :, 0:SUB * SUB:SUB + 1], 1.0).then_inc(inv_one, 1)
                    dve.wait_ge(inv_one, 1)
                    dve.wait_ge(low_in, 16)
                    for j in range(SUB - 1):
                        n, w = SUB - 1 - j, j + 1
                        t4 = tmp[:, :, 0:n * w].rearrange("p s (r c) -> p s r c", c=w)
                        if j:
                            dve.wait_ge(subd, j)
                        dve.tensor_tensor(t4, low4[:, :, j + 1:SUB, j:j + 1].broadcast_to([P, SLOTS, n, w]),
                                          inv4[:, :, j:j + 1, 0:w].broadcast_to([P, SLOTS, n, w]),
                                          ALU.mult).then_inc(prod, 1)
                        dve.wait_ge(prod, j + 1)
                        dve.tensor_tensor(inv4[:, :, j + 1:SUB, 0:w], inv4[:, :, j + 1:SUB, 0:w], t4,
                                          ALU.subtract).then_inc(subd, 1)
            end_program()

        with ExitStack() as mc:
            def mb(name, shape, dt=F32):
                return sb(name, shape, dt, c=mc)

            xT32 = mb("xT32", [P, TB, P])
            p1 = mb("p1", [P, TB, P])
            x64 = mb("x64", [P, TB, P])
            xT64 = mb("xT64", [P, TB, P])
            x128 = mb("x128", [P, TB, P])
            wt = mb("wt", [P, TB, C])
            xhm2 = pair("xhm", [P, TB, C], c=mc)
            gl2 = pair("gl", [P, GW - OFF], c=mc)
            z2 = pair("z", [P, TB, C], c=mc)
            bt2 = pair("bt", [P, CB, C], c=mc)
            e2 = pair("e", [P, CB, C], c=mc)
            m2 = mb("m2", [P, CB, C])
            m22 = pair("m2", [P, CB, C], c=mc)
            a0 = mb("a0", [P, TB, C])
            shf = mb("shf", [P, TB])
            bs2, mv2, ls2, sc2 = mb("bs2", [P, TB, 6]), mb("mv2", [P, TB, 2]), mb("ls2", [P, 2, TB]), mb("sc2", [P, 2, TB])
            bs3, mv3, ls3, sc3 = mb("bs3", [P, TB, 6]), mb("mv3", [P, TB, 2]), mb("ls3", [P, 2, TB]), mb("sc3", [P, 2, TB])
            xn = mb("xn", [P, TB, C])
            xh2T2 = pair("xh2T", [P, CB, T], c=mc)
            h1 = mb("h1", [P, CB, T])
            h12 = pair("h1", [P, CB, T], c=mc)
            xa = mb("xa", [P, TB, C])
            xa2 = mb("xa2", [P, TB, C])
            x2 = mb("x2", [P, TB, C])
            xh3T2 = pair("xh3T", [P, CB, T], c=mc)
            x3h, x3l = xh3T2
            sg = mb("sg", [P, 2, T])
            hf = mb("hf", [P, 2, T])
            hh = mb("hh", [P, HB, T], F32R)
            hl = mb("hl", [P, HB, T], F32R)
            ot = mb("ot", [P, TB, C])
            x2k = mb("x2k", [P, TB, C])

            inv_in, gg_in, kx_in, xin, out_st = sem("inv_in"), sem("gg_in"), sem("kx_in"), sem("xin"), sem("out_st")
            xT_ps, xT_ev = sem("xT_ps"), sem("xT_ev")
            p32_ps, p32_ev, p64_ps, p64_ev = sem("p32_ps"), sem("p32_ev"), sem("p64_ps"), sem("p64_ev")
            x64_ps, x64_ev, xT64_ps, xT64_ev = sem("x64_ps"), sem("x64_ev"), sem("xT64_ps"), sem("xT64_ev")
            x128_ps, x128_ev = sem("x128_ps"), sem("x128_ev")
            w_ps, w_ev, z_ps = sems("w_ps", TB - 1), sems("w_ev", TB), sems("z_ps", TB)
            z_hi, z_ev = sems("z_hi", TB), sems("z_ev", TB)
            ht_ps, ht_hi, ht_ev = sems("ht_ps", CB), sems("ht_hi", CB), sems("ht_ev", CB)
            bt_ps, bt_hi, bt_ev, e_ps, e_hi, e_ev = sem("bt_ps"), sem("bt_hi"), sem("bt_ev"), sem("e_ps"), sem("e_hi"), sem("e_ev")
            m2_ps, m2_sum, m2_hi, m2_ev = sem("m2_ps"), sem("m2_sum"), sem("m2_hi"), sem("m2_ev")
            xhm_hi, xhm_lo, gl_hi, gl_lo = sem("xhm_hi"), sem("xhm_lo"), sem("gl_hi"), sem("gl_lo")
            y_ps, a0_ev = sems("y_ps", 2), sems("a0_ev", TB)
            bn2, mv2_done, l2, ln2_done = sems("bn2_", TB), sem("mv2_done"), sems("l2_", 3), sem("ln2_done")
            bn3, mv3_done, l3, ln3_done = sems("bn3_", TB), sem("mv3_done"), sems("l3_", 3), sem("ln3_done")
            xhm_done, xh2_done, xh3_done = sem("xhm_done"), sem("xh2_done"), sem("xh3_done")
            xb_done, xa_done, sh_done = sem("xb_done"), sem("xa_done"), sem("sh_done")
            t2_ps, t2_hi, t2_ev = sems("t2_ps", 2), sems("t2_hi", 2), sems("t2_ev", 2)
            m1_ps, h1_ev, h1_hi, h1_lo = sems("m1_ps", 2), sems("h1_ev", 2), sems("h1_hi", 2), sems("h1_lo", 2)
            mo_ps, x2_ev = sems("mo_ps", 2), sems("x2_ev", TB)
            t3_ps, x3h_ev, x3l_ev = sems("t3_ps", 2), sems("x3h_ev", 2), sems("x3l_ev", 2)
            gate_ps, up_ps = sems("gate_ps", HB), sems("up_ps", HB)
            sg_ev, hf_ev, hh_ev, hl_ev = sems("sg_ev", HB), sems("hf_ev", HB), sems("hh_ev", HB), sems("hl_ev", HB)
            fo_ps, ot_ev, x2_kept = sems("fo_ps", 2), sems("ot_ev", 2), sem("x2_kept")

            def diag(j):
                return gg[:, j * P:(j + 1) * P]

            def blk(j):
                return slice(j * P, (j + 1) * P)

            def after(eng, sem, n, each=1):
                if isinstance(n, int):
                    n = min(n, NS)
                wait(eng, sem, n * each)

            def overlapped(body):
                def run(eng):
                    body(eng, 0, True, False, False)
                    body(eng, 1, True, True, False)
                    body(eng, 2, True, True, True)
                    with eng.Fori(3, NS) as i:
                        body(eng, i, True, True, True)
                    body(eng, NS, False, True, True)
                    body(eng, NS + 1, False, False, True)
                return run

            def up_bank(h):
                return (FU, S0)[h % 2]

            with nc.Block() as block:
                def pe_transposes(pe, banks, src, done):
                    for k in range(CB):
                        for j in range(TB):
                            mm = pe.transpose(ps[:, banks[k], blk(j)], src[:, j, blk(k)], ident[:, :])
                        mm.then_inc(done[k], 1)

                def pe_level(pe, bank, lhs, rhs, done):
                    for j in range(TB):
                        mm = pe.matmul(ps[:, bank, blk(j)], lhs(j), rhs(j), start=True, stop=True)
                    mm.then_inc(done, 1)

                def pe_zstep(pe, i, j):
                    pe.wait_ge(w_ev[j], i + 1)
                    if j < TB - 1:
                        pe.wait_ge(z_ev[j + 1], i + 1)
                    else:
                        pe.wait_ge(x128_ev, i + 1)
                    pe.matmul(ps[:, A1, 0:C], x128[:, j, :], wt[:, j, :], start=True, stop=True).then_inc(z_ps[j], 1)

                def pe_wstep(pe, i, j):
                    pe.wait_ge(z_ev[j + 1], i + 1)
                    if j < TB - 2:
                        pe.wait_ge(w_ev[j + 1], i + 1)
                    if j == TB - 2:
                        pe.wait_ge(gl_lo, i + 1)
                    later = range(TB - 1, j, -1)
                    cols = [GCOL[(m, j)] - OFF for m in later]
                    split_matmul(pe, ps[:, A0, 0:C], gl2, [(slice(None), slice(c, c + P)) for c in cols],
                                 z2, [(slice(None), m, slice(None)) for m in later], True, True).then_inc(w_ps[j], 1)

                def pe_bt(pe, i, j):
                    pe.wait_ge(z_ev[j], i + 1)
                    if j == TB - 1:
                        pe.wait_ge(xhm_lo, i + 1)
                    for m in range(CB):
                        mm = split_matmul(pe, ps[:, A2, m * C:(m + 1) * C], xhm2, [(slice(None), j, blk(m))],
                                          z2, [(slice(None), j, slice(None))], j == TB - 1 and m == 0, j == 0,
                                          skip_group_check=True)
                    if j == 0:
                        mm.then_inc(bt_ps, 1)

                def pe_square(pe, bank, lhs, rhs, done):
                    for m in range(CB):
                        mm = split_matmul(pe, ps[:, bank, m * C:(m + 1) * C], lhs, [(slice(None), k, blk(m)) for k in range(CB)],
                                          rhs, [(slice(None), k, slice(None)) for k in range(CB)], True, True)
                    mm.then_inc(done, 1)

                def pe_tokens(pe, bank, half, lhs, rhs, done):
                    for q in range(2):
                        mm = split_matmul(pe, ps[:, bank, q * C:(q + 1) * C],
                                          lhs, [(slice(None), k, blk(2 * half + q)) for k in range(CB)],
                                          rhs, [(slice(None), k, slice(None)) for k in range(CB)], True, True)
                    mm.then_inc(done, 1)

                def pe_mlp1(pe, m):
                    split_matmul(pe, ps[:, FO0 + m, :], w12, [(slice(None), k, blk(m)) for k in range(CB)],
                                 xh2T2, [(slice(None), k, slice(None)) for k in range(CB)],
                                 True, True).then_inc(m1_ps[m], 1)

                def pe_gate_up(pe, i, h):
                    if h == 0:
                        for k in range(CB):
                            pe.wait_ge(x3h_ev[k], i)
                            pe.wait_ge(x3l_ev[k], i)
                        after(pe, ht_ev[1], i + 1)
                    else:
                        pe.wait_ge(sg_ev[h - 1], i)
                    for w, bank, done in ((wgT, FG, gate_ps[h]), (wuT, up_bank(h), up_ps[h])):
                        if bank != FG:
                            if h >= 2:
                                pe.wait_ge(hf_ev[h - 2], i)
                            elif h == 1:
                                after(pe, ht_ev[0], i + 1)
                            else:
                                after(pe, ot_ev[1], i - 1)
                        for k in range(CB):
                            for part in (x3h, x3l):
                                mm = pe.matmul(ps[:, bank, :], w[:, k, blk(h)], part[:, k, :],
                                               start=(k == 0 and part is x3h), stop=(k == CB - 1 and part is x3l))
                        mm.then_inc(done, 1)

                def pe_down(pe, i, j):
                    for h in range(HB):
                        for part, made in ((hh, hh_ev), (hl, hl_ev)):
                            if j == 0:
                                pe.wait_ge(made[h], i - 1)
                            mm = pe.matmul(ps[:, (FG, FU)[j // 2], (j % 2) * C:(j % 2 + 1) * C], part[:, h, blk(j)],
                                           wdT[:, h, :], start=(h == 0 and part is hh),
                                           stop=(h == HB - 1 and part is hl))
                    if j % 2:
                        mm.then_inc(fo_ps[j // 2], 1)

                def pe_body(pe, i, att, mlp, down):
                    if att:
                        pe.wait_ge(inv_in, (i + 1) * 16 * QPB)
                        after(pe, a0_ev[TB - 1], i)
                        for j in range(TB):
                            mm = pe.transpose(ps[:, A2, blk(j)], x32[:, j, :], ident[:, :])
                        mm.then_inc(xT_ps, 1)
                        pe.wait_ge(gg_in, (i + 1) * 16)
                        after(pe, a0_ev[1], i)
                        pe_level(pe, A0, diag, lambda j: x32[:, j, :], p32_ps)
                    if down:
                        after(pe, sg_ev[HB - 1], i - 1)
                        pe_down(pe, i, 0)
                    if att:
                        pe.wait_ge(p32_ev, i + 1)
                        pe.wait_ge(xT_ev, i + 1)
                        after(pe, m2_sum, i)
                        pe_level(pe, A1, lambda j: xT32[:, j, :], lambda j: p1[:, j, :], x64_ps)
                        pe_level(pe, A2, lambda j: p1[:, j, :], lambda j: xT32[:, j, :], xT64_ps)
                    if mlp:
                        pe.wait_ge(xh2_done, i)
                        for k in range(CB):
                            after(pe, x3h_ev[k], i - 1)
                            after(pe, x3l_ev[k], i - 1)
                        pe_transposes(pe, (FO0, FO1), xn, t2_ps)
                    if down:
                        pe_down(pe, i, 1)
                    if att:
                        pe.wait_ge(x64_ev, i + 1)
                        pe_level(pe, A0, diag, lambda j: x64[:, j, :], p64_ps)
                    if mlp:
                        pe.wait_ge(t2_ev[0], i)
                        pe.wait_ge(t2_ev[1], i)
                        pe_mlp1(pe, 0)
                    if att:
                        pe.wait_ge(p64_ev, i + 1)
                        pe.wait_ge(xT64_ev, i + 1)
                        pe_level(pe, A1, lambda j: xT64[:, j, :], lambda j: p1[:, j, :], x128_ps)
                    if mlp:
                        pe_mlp1(pe, 1)
                    if att:
                        pe_zstep(pe, i, 3)
                    if down:
                        after(pe, hf_ev[HB - 2], i - 1)
                        pe_down(pe, i, 2)
                    if att:
                        pe_wstep(pe, i, 2)
                    if mlp:
                        pe.wait_ge(h1_lo[0], i)
                        pe.wait_ge(h1_lo[1], i)
                        pe_tokens(pe, FO0, 0, h12, w22, mo_ps[0])
                    if att:
                        pe_zstep(pe, i, 2)
                    if mlp:
                        pe_tokens(pe, FO1, 1, h12, w22, mo_ps[1])
                    if att:
                        pe_wstep(pe, i, 1)
                        pe.wait_ge(xhm_done, i + 1)
                        after(pe, hf_ev[HB - 1], i - 1)
                        after(pe, ot_ev[0], i - 1)
                        pe_transposes(pe, (S0, FG), xh, ht_ps)
                        pe_bt(pe, i, 3)
                        pe_zstep(pe, i, 1)
                    if down:
                        pe_down(pe, i, 3)
                    if att:
                        pe_wstep(pe, i, 0)
                        pe_bt(pe, i, 2)
                        pe_zstep(pe, i, 0)
                    if mlp:
                        pe.wait_ge(xh3_done, i)
                        for j in range(TB):
                            pe.wait_ge(x2_ev[j], i)
                        pe_transposes(pe, (FO0, FO1), xn, t3_ps)
                    if att:
                        pe_bt(pe, i, 1)
                        pe_bt(pe, i, 0)
                    if mlp:
                        pe_gate_up(pe, i, 0)
                    if att:
                        pe.wait_ge(bt_ev, i + 1)
                        pe_square(pe, A0, bt2, wvo2, e_ps)
                    if mlp:
                        pe_gate_up(pe, i, 1)
                    if att:
                        pe.wait_ge(e_ev, i + 1)
                        pe_square(pe, A1, wqT2, e2, m2_ps)
                    if mlp:
                        pe_gate_up(pe, i, 2)
                        pe_gate_up(pe, i, 3)
                    if att:
                        pe.wait_ge(m2_ev, i + 1)
                        pe_tokens(pe, A0, 0, xhT2, m22, y_ps[0])
                        pe_tokens(pe, A2, 1, xhT2, m22, y_ps[1])
                    if mlp:
                        pe_gate_up(pe, i, 4)
                        pe_gate_up(pe, i, 5)

                @block.tensor
                def _(pe):
                    overlapped(pe_body)(pe)

                def flat(t):
                    return t[:, :, :].rearrange("p a b -> p (a b)")

                def act_silu(act, i, h):
                    act.wait_ge(gate_ps[h], i)
                    if h >= 2:
                        act.wait_ge(hf_ev[h - 2], i)
                    else:
                        after(act, hf_ev[HB - 2 + h], i - 1)
                    act.activation(sg[:, h % 2, :], ps[:, FG, :], ACT.Silu, scale=QUANT).then_inc(sg_ev[h], 1)

                def act_hh(act, i, h):
                    act.wait_ge(hf_ev[h], i)
                    act.activation(hh[:, h, :], hf[:, h % 2, :], ACT.Copy).then_inc(hh_ev[h], 1)

                def act_z(act, i, j):
                    act.wait_ge(z_ps[j], i + 1)
                    act.activation(z2[0][:, j, :], ps[:, A1, 0:C], ACT.Copy).then_inc(z_hi[j], 1)

                def act_hi(act, dst, banks, src, done, n):
                    for k in range(CB):
                        act.wait_ge(src[k], n)
                        act.activation(dst[:, k, :], ps[:, banks[k], :], ACT.Copy).then_inc(done[k], 1)

                def act_body(act, i, att, mlp, down):
                    if att:
                        act.wait_ge(xT_ps, i + 1)
                        act.activation(flat(xT32), ps[:, A2, :], ACT.Copy).then_inc(xT_ev, 1)
                    if mlp:
                        act_hi(act, xh2T2[0], (FO0, FO1), t2_ps, t2_hi, i)
                        for m in range(CB):
                            act.wait_ge(m1_ps[m], i)
                            act.activation(h1[:, m, :], ps[:, FO0 + m, :], ACT.Relu, bias=b1f[:, m:m + 1]).then_inc(h1_ev[m], 1)
                    if att:
                        act_z(act, i, 3)
                        act_z(act, i, 2)
                        act_hi(act, xhT2[0], (S0, FG), ht_ps, ht_hi, i + 1)
                        act_z(act, i, 1)
                        act_z(act, i, 0)
                    if mlp:
                        act_hi(act, x3h, (FO0, FO1), t3_ps, x3h_ev, i)
                    if att:
                        act.wait_ge(bt_ps, i + 1)
                        act.activation(flat(bt2[0]), ps[:, A2, :], ACT.Copy).then_inc(bt_hi, 1)
                    if mlp:
                        act_silu(act, i, 0)
                        for j in range(TB):
                            act.wait_ge(x2_ev[j], i)
                        after(act, ot_ev[1], i - 1)
                        act.activation(x2k[:, :, :], x2[:, :, :], ACT.Copy).then_inc(x2_kept, 1)
                        act_hh(act, i, 0)
                    if att:
                        act.wait_ge(e_ps, i + 1)
                        act.activation(flat(e2[0]), ps[:, A0, :], ACT.Copy).then_inc(e_hi, 1)
                    if mlp:
                        act_silu(act, i, 1)
                        act_hh(act, i, 1)
                    if att:
                        act.wait_ge(m2_sum, i + 1)
                        act.activation(m22[0][:, :, :], m2[:, :, :], ACT.Copy).then_inc(m2_hi, 1)
                    if mlp:
                        for h in range(2, HB):
                            act_silu(act, i, h)
                            act_hh(act, i, h)

                @block.scalar
                def _(act):
                    overlapped(act_body)(act)

                def masked(dve, mask, src_ps, done, i):
                    dve.wait_ge(src_ps, i + 1)
                    dve.tensor_tensor(p1[:, :, :], ps[:, A0, :].rearrange("p (j c) -> p j c", c=P),
                                      mask[:, :].unsqueeze(1).broadcast_to([P, TB, P]), ALU.mult).then_inc(done, 1)

                def plus(dve, dst, bank, src, src_ps, done, i):
                    dve.wait_ge(src_ps, i + 1)
                    dve.tensor_tensor(dst[:, :, :], ps[:, bank, :].rearrange("p (j c) -> p j c", c=P), src[:, :, :],
                                      ALU.add).then_inc(done, 1)

                def dve_w(dve, i, j):
                    dve.wait_ge(w_ps[j], i + 1)
                    dve.scalar_tensor_tensor(out=wt[:, j, :], in0=kx3[:, j, :], scalar=kx[:, E_LR + j:E_LR + j + 1],
                                             in1=ps[:, A0, 0:C], op0=ALU.mult, op1=ALU.subtract).then_inc(w_ev[j], 1)

                def dve_stats(dve, n_done, bst_, mv_, bns, mvd):
                    for j in range(TB):
                        dve.wait_ge(ready, 1)
                        dve.wait_ge(bns[j], n_done)
                        agg = dve.bn_aggr(mv_[:, j, :], bst_[:, j, :])
                    agg.then_inc(mvd, 1)

                def dve_x2(dve, i, half):
                    dve.wait_ge(mo_ps[half], i)
                    if half == 0:
                        dve.wait_ge(xa_done, i)
                        dve.wait_ge(sh_done, i)
                        after(dve, x2_kept, i - 1)
                        after(dve, ln3_done, i - 1)
                    for j in (2 * half, 2 * half + 1):
                        dve.scalar_tensor_tensor(out=x2[:, j, :], in0=xa2[:, j, :], scalar=shf[:, j:j + 1],
                                                 in1=ps[:, FO0 + half, (j % 2) * C:(j % 2 + 1) * C],
                                                 op0=ALU.add, op1=ALU.add).then_inc(x2_ev[j], 1)

                def dve_x2_stats(dve, i, half):
                    for j in (2 * half, 2 * half + 1):
                        dve.wait_ge(x2_ev[j], i)
                        dve.bn_stats(bs3[:, j, :], x2[:, j, :]).then_inc(bn3[j], 1)

                def dve_up(dve, i, h):
                    dve.wait_ge(up_ps[h], i)
                    dve.wait_ge(sg_ev[h], i)
                    for made in (hh_ev, hl_ev):
                        if h >= 2:
                            dve.wait_ge(made[h - 2], i)
                        else:
                            after(dve, made[HB - 2 + h], i - 1)
                    dve.tensor_tensor(hf[:, h % 2, :], ps[:, up_bank(h), :], sg[:, h % 2, :], ALU.mult).then_inc(hf_ev[h], 1)

                def dve_rest(dve, lo, whole, hi, hi_done, n_done, done):
                    dve.wait_ge(hi_done, n_done)
                    dve.tensor_tensor(lo, whole, hi.bitcast(F32), ALU.subtract).then_inc(done, 1)

                def dve_hl(dve, i, h):
                    dve_rest(dve, hl[:, h, :], hf[:, h % 2, :], hh[:, h, :], hh_ev[h], i, hl_ev[h])

                def dve_z(dve, i, j):
                    dve_rest(dve, z2[1][:, j, :], ps[:, A1, 0:C], z2[0][:, j, :], z_hi[j], i + 1, z_ev[j])

                def dve_h1(dve, i, m):
                    dve.wait_ge(h1_ev[m], i)
                    dve.tensor_copy(h12[0][:, m, :], h1[:, m, :]).then_inc(h1_hi[m], 1)
                    dve_rest(dve, h12[1][:, m, :], h1[:, m, :], h12[0][:, m, :], h1_hi[m], i, h1_lo[m])

                def dve_lo(dve, lo, hi, banks, hi_done, done, n):
                    for k in range(CB):
                        dve_rest(dve, lo[:, k, :], ps[:, banks[k], :], hi[:, k, :], hi_done[k], n, done[k])

                def dve_out(dve, i, half):
                    dve.wait_ge(fo_ps[half], i - 1)
                    if half == 0:
                        after(dve, out_st, i - 2, 16)
                        dve.wait_ge(x2_kept, i - 1)
                    dve.scalar_tensor_tensor(
                        out=ot[:, 2 * half:2 * half + 2, :].rearrange("p j c -> p (j c)"), in0=ps[:, (FG, FU)[half], :],
                        scalar=QUANT * QUANT, in1=x2k[:, 2 * half:2 * half + 2, :].rearrange("p j c -> p (j c)"),
                        op0=ALU.mult, op1=ALU.add).then_inc(ot_ev[half], 1)

                def bank3(bank):
                    return ps[:, bank, :].rearrange("p (k c) -> p k c", c=C)

                def dve_body(dve, i, att, mlp, down):
                    if att:
                        masked(dve, mask32, p32_ps, p32_ev, i)
                        dve.wait_ge(gg_in, (i + 1) * 16)
                        after(dve, w_ps[0], i)
                        dve.tensor_copy(gl2[0][:, :], gg[:, OFF:GW]).then_inc(gl_hi, 1)
                        plus(dve, x64, A1, x32, x64_ps, x64_ev, i)
                        plus(dve, xT64, A2, xT32, xT64_ps, xT64_ev, i)
                    if mlp:
                        dve_lo(dve, xh2T2[1], xh2T2[0], (FO0, FO1), t2_hi, t2_ev, i)
                    if down:
                        dve_out(dve, i, 0)
                    if att:
                        masked(dve, mask64, p64_ps, p64_ev, i)
                    if att:
                        dve.wait_ge(kx_in, (i + 1) * 16)
                        dve.tensor_scalar(wt[:, 3, :], kx3[:, 3, :], kx[:, E_LR + 3:E_LR + 4], None,
                                          ALU.mult).then_inc(w_ev[3], 1)
                    if mlp:
                        dve_h1(dve, i, 0)
                    if att:
                        plus(dve, x128, A1, x64, x128_ps, x128_ev, i)
                    if mlp:
                        dve_h1(dve, i, 1)
                    if att:
                        dve_z(dve, i, 3)
                        dve.wait_ge(xhm_done, i + 1)
                        after(dve, bt_ps, i)
                        dve.tensor_copy(xhm2[0][:, :, :], xh[:, :, :]).then_inc(xhm_hi, 1)
                        dve_w(dve, i, 2)
                    if mlp:
                        dve_x2(dve, i, 0)
                    if att:
                        dve_z(dve, i, 2)
                    if mlp:
                        dve_x2_stats(dve, i, 0)
                        dve_x2(dve, i, 1)
                    if att:
                        dve_w(dve, i, 1)
                    if mlp:
                        dve_x2_stats(dve, i, 1)
                        dve_stats(dve, i, bs3, mv3, bn3, mv3_done)
                    if att:
                        dve_lo(dve, xhT2[1], xhT2[0], (S0, FG), ht_hi, ht_ev, i + 1)
                        dve_z(dve, i, 1)
                    if down:
                        dve_out(dve, i, 1)
                    if att:
                        dve_w(dve, i, 0)
                        dve_z(dve, i, 0)
                    if mlp:
                        dve_lo(dve, x3l, x3h, (FO0, FO1), x3h_ev, x3l_ev, i)
                    if att:
                        dve_rest(dve, bt2[1][:, :, :], bank3(A2), bt2[0][:, :, :], bt_hi, i + 1, bt_ev)
                    if mlp:
                        dve_up(dve, i, 0)
                    if att:
                        dve_rest(dve, e2[1][:, :, :], bank3(A0), e2[0][:, :, :], e_hi, i + 1, e_ev)
                    if mlp:
                        dve_up(dve, i, 1)
                    if att:
                        dve.wait_ge(m2_ps, i + 1)
                        dve.tensor_tensor(m2[:, :, :], bank3(A1), bo_bc[:, :].unsqueeze(1).broadcast_to([P, CB, C]),
                                          ALU.add).then_inc(m2_sum, 1)
                        dve_rest(dve, m22[1][:, :, :], m2[:, :, :], m22[0][:, :, :], m2_hi, i + 1, m2_ev)
                    if mlp:
                        dve_up(dve, i, 2)
                        dve_up(dve, i, 3)
                    if att:
                        dve.wait_ge(xin, (i + 1) * 16)
                        after(dve, xa_done, i)
                        after(dve, ln2_done, i)
                        for j in range(TB):
                            if j % 2 == 0:
                                dve.wait_ge(y_ps[j // 2], i + 1)
                            dve.scalar_tensor_tensor(out=a0[:, j, :], in0=xt[:, j, :], scalar=kx[:, E_R1 + j:E_R1 + j + 1],
                                                     in1=ps[:, (A0, A2)[j // 2], (j % 2) * C:(j % 2 + 1) * C],
                                                     op0=ALU.mult, op1=ALU.add).then_inc(a0_ev[j], 1)
                        for j in range(TB):
                            dve.wait_ge(a0_ev[j], i + 1)
                            dve.bn_stats(bs2[:, j, :], a0[:, j, :]).then_inc(bn2[j], 1)
                        dve_stats(dve, i + 1, bs2, mv2, bn2, mv2_done)
                    if mlp:
                        dve_up(dve, i, 4)
                        dve_hl(dve, i, 4)
                        dve_up(dve, i, 5)
                        dve_hl(dve, i, 5)

                @block.vector
                def _(dve):
                    overlapped(dve_body)(dve)

                def pool_norm(pool, n_done, read, n_read, mv_, ls, sc, steps, mvd, done):
                    for k in range(CB):
                        after(pool, read[k], n_read)
                    pool.wait_ge(mvd, n_done)
                    pool.tensor_tensor(ls[:, 0, :], mv_[:, :, 1], eps4[:, :], ALU.add).then_inc(steps[0], 1)
                    pool.wait_ge(steps[0], n_done)
                    pool.tensor_tensor(sc[:, 0, :], ls[:, 0, :], mhalf4[:, :], ALU.pow).then_inc(steps[1], 1)
                    pool.wait_ge(steps[1], n_done)
                    pool.tensor_tensor(ls[:, 1, :], sc[:, 0, :], mv_[:, :, 0], ALU.mult).then_inc(steps[2], 1)
                    pool.wait_ge(steps[2], n_done)
                    pool.tensor_tensor(sc[:, 1, :], zero4[:, :], ls[:, 1, :], ALU.subtract).then_inc(done, 1)

                def pool_scale(pool, n_done, dst, src, scale, shift, made):
                    pool.wait_ge(ready, 1)
                    pool.wait_ge(made, n_done)
                    for j in range(TB):
                        op = pool.tensor_scalar(dst[:, j, :], src[:, j, :], scale[:, j:j + 1], shift[:, j:j + 1],
                                                ALU.mult, ALU.add)
                    return op

                def pool_body(pool, i, att, mlp, down):
                    if mlp:
                        pool_norm(pool, i, t3_ps, i - 1, mv2, ls2, sc2, l2, mv2_done, ln2_done)
                        pool_scale(pool, i, xn, a0, sc2[:, 0, :], sc2[:, 1, :], ln2_done).then_inc(xh2_done, 1)
                    if att:
                        pool.wait_ge(gl_hi, i + 1)
                        pool.tensor_tensor(gl2[1][:, :], gg[:, OFF:GW], gl2[0][:, :].bitcast(F32),
                                           ALU.subtract).then_inc(gl_lo, 1)
                    if mlp:
                        for j in range(TB):
                            after(pool, x2_ev[j], i - 1)
                        pool.wait_ge(xb_done, i)
                        pool.tensor_tensor(xa2[:, :, :], xa[:, :, :], a0[:, :, :], ALU.add).then_inc(xa_done, 1)
                    if att:
                        pool.wait_ge(xin, (i + 1) * 16)
                        after(pool, xa_done, i)
                        pool.tensor_tensor(xa[:, :, :], xt[:, :, :], b2_bc[:, :].unsqueeze(1).broadcast_to([P, TB, C]),
                                           ALU.add).then_inc(xb_done, 1)
                        pool.wait_ge(ready, 1)
                        for k in range(CB):
                            after(pool, ht_ps[k], i)
                        after(pool, xhm_lo, i)
                        pool.wait_ge(kx_in, (i + 1) * 16)
                        for j in range(TB):
                            op = pool.tensor_scalar(xh[:, j, :], xt[:, j, :], kx[:, E_S + j:E_S + j + 1],
                                                    kx[:, E_B + j:E_B + j + 1], ALU.mult, ALU.add)
                        op.then_inc(xhm_done, 1)
                        pool.wait_ge(xhm_hi, i + 1)
                        pool.tensor_tensor(xhm2[1][:, :, :], xh[:, :, :], xhm2[0][:, :, :].bitcast(F32),
                                           ALU.subtract).then_inc(xhm_lo, 1)
                    if mlp:
                        pool_norm(pool, i, t2_ps, i, mv3, ls3, sc3, l3, mv3_done, ln3_done)
                        pool_scale(pool, i, xn, x2, sc3[:, 0, :], sc3[:, 1, :], ln3_done).then_inc(xh3_done, 1)
                    if att:
                        for j in range(TB):
                            after(pool, x2_ev[j], i)
                        pool.tensor_tensor(shf[:, :], kx[:, E_SH:E_SH + TB], zero4[:, :], ALU.add).then_inc(sh_done, 1)
                    if mlp:
                        for h in range(HB - 2):
                            pool.wait_ge(hh_ev[h], i)
                            pool.tensor_tensor(hl[:, h, :], hf[:, h % 2, :], hh[:, h, :].bitcast(F32),
                                               ALU.subtract).then_inc(hl_ev[h], 1)

                @block.gpsimd
                def _(pool):
                    overlapped(pool_body)(pool)

                def load_inv(sp, n):
                    for a in range(QPB):
                        sp.dma_start(x32[a * SUB:(a + 1) * SUB, :, a * SUB:(a + 1) * SUB], inv_v[n][a]).then_inc(inv_in, 16)

                def load_blocks(sp, n):
                    sp.wait_ge(x64_ev, n)
                    load_inv(sp, n)
                    sp.wait_ge(p64_ps, n)
                    sp.wait_ge(gl_lo, n)
                    sp.dma_start(gg[:, :], gg_d[n]).then_inc(gg_in, 16)

                def load_rows(sp, n):
                    sp.wait_ge(a0_ev[TB - 1], n)
                    sp.wait_ge(sh_done, n)
                    sp.dma_start(kx[:, :], kx_d[n]).then_inc(kx_in, 16)
                    sp.wait_ge(xb_done, n)
                    sp.dma_start(xt[:, :, :], x_v[n]).then_inc(xin, 16)

                def store_out(sp, n):
                    sp.wait_ge(ot_ev[0], n + 1)
                    sp.wait_ge(ot_ev[1], n + 1)
                    sp.dma_start(out_v[n], ot[:, :, :]).then_inc(out_st, 16)

                @block.sync
                def _(sp):
                    load_inv(sp, 0)
                    sp.dma_start(gg[:, :], gg_d[0]).then_inc(gg_in, 16)
                    sp.dma_start(kx[:, :], kx_d[0]).then_inc(kx_in, 16)
                    sp.dma_start(xt[:, :, :], x_v[0]).then_inc(xin, 16)
                    for n in (1, 2):
                        load_blocks(sp, n)
                        load_rows(sp, n)
                    with sp.Fori(2, NS - 1) as i:
                        load_blocks(sp, i + 1)
                        store_out(sp, i - 2)
                        load_rows(sp, i + 1)
                    for n in range(NS - 3, NS):
                        store_out(sp, n)
                    sp.wait_ge(out_st, 16 * NS)


_INS = ['L0_attn_x', 'L0_attn_dn_g', 'L0_attn_dn_b', 'L0_attn_gates_w', 'L0_attn_gates_b', 'L0_attn_lr_w',
        'L0_attn_lr_b', 'L0_attn_out_w', 'L0_attn_out_b', 'L0_attn_mn_g', 'L0_attn_mn_b', 'L0_attn_w1', 'L0_attn_b1',
        'L0_attn_w2', 'L0_attn_b2', 'L0_ffn_w_gate', 'L0_ffn_w_up', 'L0_ffn_w_down']


def kernel(**inputs):
    import numpy as _np
    import concourse.bacc as _bacc
    from concourse import mybir as _mybir
    from concourse.bass_utils import run_bass_kernel_spmd as _run

    nc = _bacc.Bacc("TRN2", target_bir_lowering=False, num_devices=1)
    arrays, args = {}, []
    for name in _INS:
        a = _np.ascontiguousarray(inputs[name])
        arrays[f"in_{name}_dram"] = a
        args.append(nc.dram_tensor(f"in_{name}_dram", a.shape, _mybir.dt.from_np(a.dtype), kind="ExternalInput").ap())
    shape = arrays["in_L0_attn_x_dram"].shape
    args.append(nc.dram_tensor("out_0_dram", shape, _mybir.dt.float32, kind="ExternalOutput").ap())
    delta_block_kernel(nc, *args)
    r = _run(nc, [arrays], core_ids=[0])
    return r.results[0]["out_0_dram"]
```

```python
from contextlib import ExitStack

import concourse.bass as bass
from concourse import mybir

ALU = mybir.AluOpType
ACT = mybir.ActivationFunctionType
F32 = mybir.dt.float32
F32R = mybir.dt.float32r
I32 = mybir.dt.int32

P = 128
EPS = 1e-5
QUANT = 1.0 / 127.0
SUB = 32
A0, A1, A2, S0, FG, FU, FO0, FO1 = range(8)


def wait(eng, sem, value):
    if isinstance(value, int) and value <= 0:
        return
    eng.wait_ge(sem, value)


def delta_block_kernel(nc, x, dn_g, dn_b, gates_w, gates_b, lr_w, lr_b, out_w, out_b, mn_g, mn_b,
                       w1, b1, w2, b2, w_gate, w_up, w_down, out):
    NS, T, C = x.shape
    H = w_gate.shape[0]
    TB, CB, HB = T // P, C // P, H // P
    OFF = TB * P
    ROW = {3: OFF, 2: OFF + 3 * P, 1: OFF + 5 * P}
    GCOL = {(i, j): ROW[i] + j * P for i in ROW for j in range(i)}
    GW = OFF + 6 * P
    KXE = TB * C
    E_LR, E_S, E_B, E_R1, E_SH = (KXE + TB * q for q in range(5))
    KXW = KXE + 5 * TB
    NSUB = T // SUB
    GROUP = P // NSUB
    SLOTS = NS // GROUP
    QPB = P // SUB
    assert TB == 4 and CB == 2 and NS % GROUP == 0 and NS >= 3

    kx_d = nc.dram_tensor("kx_scratch", [NS, P, KXW], F32, kind="Internal").ap()
    gg_d = nc.dram_tensor("gg_scratch", [NS, P, GW], F32, kind="Internal").ap()
    low_d = nc.dram_tensor("low_scratch", [NS * NSUB, SUB * SUB], F32, kind="Internal").ap()
    inv_d = nc.dram_tensor("inv_scratch", [NS * NSUB, SUB * SUB], F32, kind="Internal").ap()
    x_v = x.rearrange("n (j p) c -> n p j c", p=P)
    out_v = out.rearrange("n (j p) c -> n p j c", p=P)
    low_v = low_d.rearrange("(n j a) (r c) -> n a r j c", j=TB, a=QPB, c=SUB)
    inv_v = inv_d.rearrange("(n j a) (r c) -> n a r j c", j=TB, a=QPB, c=SUB)
    low_lane = low_d.rearrange("(s l) e -> l s e", l=P)
    inv_lane = inv_d.rearrange("(s l) e -> l s e", l=P)

    with ExitStack() as ctx:
        def sb(name, shape, dt=F32, c=ctx):
            return c.enter_context(nc.sbuf_tensor(name, shape, dt))

        held = []

        def sem(name):
            held.append(nc.alloc_semaphore(name=name))
            return held[-1]

        def sems(name, n):
            return [sem(f"{name}{k}") for k in range(n)]

        def end_program():
            nc.clear_and_free_semaphores(held)
            held.clear()
            nc.all_engine_barrier()

        ps = ctx.enter_context(nc.psum_tensor("ps", [P, 8, 512], F32))

        ident = sb("ident", [P, P])
        mask32 = sb("mask32", [P, P])
        mask64 = sb("mask64", [P, P])
        eps4 = sb("eps4", [P, TB])
        mhalf4 = sb("mhalf4", [P, TB])
        zero4 = sb("zero4", [P, TB])
        one4 = sb("one4", [P, TB])
        b1f = sb("b1f", [P, CB])

        def pair(name, shape, c=ctx):
            return sb(name + "_hi", shape, F32R, c=c), sb(name + "_lo", shape, F32R, c=c)

        wk2 = pair("wk", [P, CB, C + 2])
        wqT2 = pair("wqT", [P, CB, C])
        wvo2 = pair("wvo", [P, CB, C])
        w12 = pair("w1", [P, CB, C])
        w22 = pair("w2", [P, CB, C])
        bo_bc = sb("bo_bc", [P, C])
        b2_bc = sb("b2_bc", [P, C])
        wgT = sb("wgT", [P, CB, H], F32R)
        wuT = sb("wuT", [P, CB, H], F32R)
        wdT = sb("wdT", [P, HB, C], F32R)

        xt = sb("xt", [P, TB, C])
        xh = sb("xh", [P, TB, C])
        xhT2 = pair("xhT", [P, CB, T])
        kx = sb("kx", [P, KXW])
        gg = sb("gg", [P, GW])
        x32 = sb("x32", [P, TB, P])
        kx3 = kx[:, 0:KXE].rearrange("p (j c) -> p j c", j=TB)
        ready = ctx.enter_context(nc.semaphore("ready"))

        def three(a2, b2):
            return ((a2[0], b2[0]), (a2[0], b2[1]), (a2[1], b2[0]))

        def split_matmul(pe, dst, a2, a_at, b2, b_at, start, stop, before=None, **kw):
            n = 3 * len(a_at)
            for q, (ka, kb) in enumerate(zip(a_at, b_at)):
                if before is not None:
                    before(q)
                for a, b in three(a2, b2):
                    n -= 1
                    mm = pe.matmul(dst, a[ka], b[kb], start=start, stop=(stop and n == 0), **kw)
                    start = False
            return mm

        gates_v = gates_w.rearrange("(k p) o -> p k o", p=P)

        def col(v):
            return v.rearrange("(k p) -> p k", p=P)

        def row(v):
            return v.rearrange("(a c) -> a c", a=1)

        ones = sb("ones", [P, P])
        dcol = sb("dcol", [P, 2, CB])
        with ExitStack() as pre:
            KW = C + 2
            wall = sb("wallk", [P, CB, KW], c=pre)
            brow = sb("browk", [1, KW], c=pre)
            diff = sb("diff", [P, CB], c=pre)
            diff_bc = sb("diff_bc", [P, CB, P], c=pre)
            shift = sb("shiftk", [P, KW], c=pre)
            wfold = sb("wfoldk", [P, CB, KW], c=pre)
            pads, loaded = sem("pads"), sem("loaded")
            ones_set, zeroed, minus = sem("ones_set"), sem("zeroed"), sem("minus")
            diff_done, diff_bc_done = sem("diff_done"), sem("diff_bc_done")
            shift_ps, shift_done, fold_done = sem("shift_ps"), sem("shift_done"), sem("fold_done")
            split_hi, split_done, id_done, x32_zero = sem("split_hi"), sem("split_done"), sem("id_done"), sem("x32_zero")
            def setup_sp(sp):
                load_x(sp, 0, 0)
                with nc.allow_non_contiguous_dma(reason="a few columns, once"):
                    sp.dma_start(wall[:, :, 0:C], gates_v[:, :, C:2 * C]).then_inc(loaded, 16)
                    sp.dma_start(dcol[:, 0, :], col(dn_g)).then_inc(loaded, 16)
                    sp.dma_start(dcol[:, 1, :], col(dn_b)).then_inc(loaded, 16)
                    sp.dma_start(brow[:, 0:C], row(gates_b)[:, C:2 * C]).then_inc(loaded, 16)
                    sp.wait_ge(pads, 2)
                    sp.dma_start(wall[:, :, C:C + 1], lr_w.rearrange("(k p) o -> p k o", p=P)).then_inc(loaded, 16)
                    sp.dma_start(brow[:, C:C + 1], row(lr_b)).then_inc(loaded, 16)

            def setup_pool(pool):
                pool.memset(wall[:, :, C:KW], 0.0).then_inc(pads, 1)
                pool.memset(brow[:, C:KW], 0.0).then_inc(pads, 1)
                pool.memset(ones[:, :], 1.0).then_inc(ones_set, 1)
                pool.wait_ge(ones_set, 1)
                pool.affine_select(out=ident[:, :], in_=ones[:, :], compare_op=ALU.is_equal, fill=0.0,
                                   base=0, pattern=[[-1, P]], channel_multiplier=1).then_inc(id_done, 1)
                pool.memset(mask32[:, :], 0.0).then_inc(zeroed, 1)
                pool.memset(mask64[:, :], 0.0).then_inc(zeroed, 1)
                pool.wait_ge(zeroed, 2)
                pool.memset(mask32[SUB:2 * SUB, 0:SUB], -1.0)
                pool.memset(mask32[3 * SUB:4 * SUB, 2 * SUB:3 * SUB], -1.0).then_inc(minus, 1)
                pool.wait_ge(minus, 1)
                pool.memset(mask64[2 * SUB:4 * SUB, 0:2 * SUB], -1.0).then_inc(minus, 1)
                pool.wait_ge(minus, 2)
                pool.memset(eps4[:, :], EPS)
                pool.memset(mhalf4[:, :], -0.5)
                pool.memset(zero4[:, :], 0.0)
                pool.memset(one4[:, :], 1.0)
                pool.memset(x32[:, :, :], 0.0).then_inc(x32_zero, 1)
                pool.wait_ge(x32_zero, 1)
                pool.wait_ge(id_done, 1)

            def setup_dve(dve):
                dve.wait_ge(ones_set, 1)
                dve.wait_ge(loaded, 6 * 16)
                dve.tensor_tensor(diff[:, :], dcol[:, 1, :], dcol[:, 0, :], ALU.subtract).then_inc(diff_done, 1)
                dve.wait_ge(diff_done, 1)
                for k in range(CB):
                    dve.tensor_scalar(diff_bc[:, k, :], ones[:, :], diff[:, k:k + 1], None,
                                      ALU.mult).then_inc(diff_bc_done, 1)
                dve.wait_ge(shift_done, 1)
                for k in range(CB):
                    dve.scalar_tensor_tensor(out=wfold[:, k, :], in0=wall[:, k, :], scalar=dcol[:, 0, k:k + 1],
                                             in1=shift[:, :], op0=ALU.mult, op1=ALU.add).then_inc(fold_done, 1)
                dve.wait_ge(fold_done, CB)
                dve.tensor_copy(wk2[0][:, :, :], wfold[:, :, :]).then_inc(split_hi, 1)
                dve.wait_ge(split_hi, 1)
                dve.tensor_tensor(wk2[1][:, :, :], wfold[:, :, :], wk2[0][:, :, :].bitcast(F32),
                                  ALU.subtract).then_inc(split_done, 1)
                dve.wait_ge(split_done, 1)

            def setup_act(act):
                act.wait_ge(shift_ps, 1)
                act.activation(shift[:, :], ps[:, K0, 0:KW], ACT.Copy, scale=1.0 / C).then_inc(shift_done, 1)

            def setup_pe(pe):
                pe.wait_ge(x32_zero, 1)
                pe.nop().then_inc(ready, 1)
                pe.wait_ge(loaded, 6 * 16)
                pe.wait_ge(ones_set, 1)
                pe.wait_ge(diff_bc_done, CB)
                for k in range(CB):
                    pe.matmul(ps[:, K0, 0:KW], diff_bc[:, k, :], wall[:, k, :], start=(k == 0), stop=False)
                pe.matmul(ps[:, K0, 0:KW], ones[0:1, :], brow[:, :], start=False, stop=True).then_inc(shift_ps, 1)

            xk = sb("xk", [P, 2, TB, C], c=pre)
            bst = sb("bst", [P, 2, TB, 6], c=pre)
            mv = sb("mv", [P, TB, 2], c=pre)
            lns = sb("lns", [P, 8, TB], c=pre)
            exln = sb("exln", [P, 2, 4, TB], c=pre)
            sqj = sb("sqj", [P, TB, C], c=pre)
            ssq = sb("ssq", [P, TB], c=pre)
            rn = sb("rn", [P, TB], c=pre)
            knT2 = pair("knT", [P, CB, T], c=pre)
            x_in, kx_out, gg_out, low_out = sems("x_in", 2), sem("kx_out"), sem("gg_out"), sem("low_out")
            bn_done, bn_copied = sem("bn_done"), sem("bn_copied")
            mv_done, ln_done, xh_done = sem("mv_done"), sem("ln_done"), sem("xh_done")
            lstep, ln_half = sems("lstep", 8), sem("ln_half")
            xhT_ps, xhT_hi, xhT_lo = sems("xhT_ps", CB), sems("xhT_hi", CB), sems("xhT_lo", CB)
            k_ps, sq_done, rn_done = sems("k_ps", TB), sem("sq_done"), sem("rn_done")
            ex_done, lr_done, kn_done = sem("ex_done"), sem("lr_done"), sem("kn_done")
            knT_ps, knT_hi, knT_lo = sems("knT_ps", CB), sems("knT_hi", CB), sems("knT_lo", CB)
            g_ps, g_ev = sems("g_ps", 3), sems("g_ev", 3)
            T0, K0, G0, G1 = 0, 2, 6, 7
            GROW = {3: (G1, 0), 0: (G0, 0), 2: (G0, P), 1: (T0, 0)}

            def piped(body, tail):
                def run(eng):
                    body(eng, 0, 0, True, 2)
                    body(eng, 1, 1, False, 2)
                    with eng.Fori(1, NS // 2 - 1) as m:
                        body(eng, 2 * m, 0, False, 2)
                        body(eng, 2 * m + 1, 1, False, 2)
                    body(eng, NS - 2, 0, False, 1)
                    body(eng, NS - 1, 1, False, 0)
                    tail(eng)
                return run

            def x_count(n, par):
                return 8 * (n - par) + 16

            def load_x(sp, n, par):
                sp.dma_start(xk[:, par, :, :], x_v[n]).then_inc(x_in[par], 16)

            def sp_stores(sp, n):
                for q in range(3):
                    sp.wait_ge(g_ev[q], n + 1)
                for a in range(QPB):
                    sp.dma_start(low_v[n][a], gg[a * SUB:(a + 1) * SUB, 0:OFF].rearrange("p (j c) -> p j c", c=P)
                                 [:, :, a * SUB:(a + 1) * SUB]).then_inc(low_out, 16)
                sp.dma_start(gg_d[n], gg[:, :]).then_inc(gg_out, 16)

            def sp_body(sp, i, par, first, load):
                if load:
                    sp.wait_ge(xh_done, i + 2)
                    load_x(sp, i + 3, 1 - par)
                sp.wait_ge(kn_done, i + 1)
                sp.dma_start(kx_d[i], kx[:, :]).then_inc(kx_out, 16)
                if not first:
                    sp_stores(sp, i - 1)

            def keys_sp(sp):
                load_x(sp, 1, 1)
                sp.wait_ge(xh_done, 1)
                load_x(sp, 2, 0)
                sp_body(sp, 0, 0, True, True)
                load_weights(sp, 0)
                sp_body(sp, 1, 1, False, True)
                load_weights(sp, 1)
                with sp.Fori(1, NS // 2 - 2) as m:
                    sp_body(sp, 2 * m, 0, False, True)
                    sp_body(sp, 2 * m + 1, 1, False, True)
                for n in range(NS - 4, NS):
                    sp_body(sp, n, n % 2, False, n + 3 < NS)
                    if n < NS - 2:
                        load_weights(sp, n - (NS - 4) + 2)
                    elif n == NS - 2 and SLOTS > 1:
                        load_low(sp)
                sp_stores(sp, NS - 1)

            def stats(dve, n, par):
                dve.wait_ge(x_in[par], x_count(n, par))
                wait(dve, ln_done, n)
                for j in range(TB):
                    bn = dve.bn_stats(bst[:, 0, j, :], xk[:, par, j, :])
                bn.then_inc(bn_done, 1)
                dve.wait_ge(bn_done, n + 1)
                dve.tensor_copy(bst[:, 1, :, :], bst[:, 0, :, :]).then_inc(bn_copied, 1)
                for j in range(TB):
                    dve.wait_ge(ready, 1)
                    dve.wait_ge(bn_copied, n + 1)
                    agg = dve.bn_aggr(mv[:, j, :], bst[:, 1, j, :])
                agg.then_inc(mv_done, 1)

            def rest(dve, dst2, bank, hi, lo, n, banks=range(CB)):
                for k in banks:
                    dve.wait_ge(hi[k], n + 1)
                    dve.tensor_tensor(dst2[1][:, k, :], ps[:, bank + k, :], dst2[0][:, k, :].bitcast(F32),
                                      ALU.subtract).then_inc(lo[k], 1)

            def dve_g(dve, n):
                dve.wait_ge(g_ps[1], n + 1)
                wait(dve, gg_out, 16 * n)
                wait(dve, low_out, 16 * QPB * n)
                dve.tensor_copy(gg[:, ROW[3]:ROW[3] + 3 * P], ps[:, G1, 0:3 * P])
                dve.tensor_copy(gg[:, 3 * P:4 * P], ps[:, G1, 3 * P:4 * P]).then_inc(g_ev[1], 1)

            def dve_body(dve, i, par, first, left):
                if left == 2:
                    stats(dve, i + 2, par)
                wait(dve, kx_out, 16 * i)
                dve.wait_ge(ln_done, i + 1)
                dve.tensor_copy(kx[:, E_S:KXW], exln[:, par, :, :].rearrange("p q j -> p (q j)")).then_inc(ex_done, 1)
                if not first:
                    rest(dve, knT2, G0, knT_hi, knT_lo, i - 1)
                dve.wait_ge(sq_done, i + 1)
                dve.tensor_copy(kx[:, E_LR:E_LR + TB].rearrange("p (j o) -> p j o", o=1),
                                ps[:, K0:K0 + TB, C:C + 1]).then_inc(lr_done, 1)
                if left:
                    rest(dve, xhT2, T0, xhT_hi, xhT_lo, i + 1, (0,))
                dve.wait_ge(rn_done, i + 1)
                dve.tensor_tensor(kx3, ps[:, K0:K0 + TB, 0:C], rn[:, :].unsqueeze(2).broadcast_to([P, TB, C]),
                                  ALU.mult).then_inc(kn_done, 1)
                if left:
                    rest(dve, xhT2, T0, xhT_hi, xhT_lo, i + 1, (1,))
                if not first:
                    dve_g(dve, i - 1)

            def keys_dve(dve):
                rest(dve, xhT2, T0, xhT_hi, xhT_lo, 0)
                stats(dve, 1, 1)
                piped(dve_body, lambda e: (
                    rest(e, knT2, G0, knT_hi, knT_lo, NS - 1), dve_g(e, NS - 1)))(dve)

            def act_g(act, n):
                act.wait_ge(g_ps[0], n + 1)
                wait(act, gg_out, 16 * n)
                wait(act, low_out, 16 * QPB * n)
                act.activation(gg[:, 0:OFF].rearrange("p (j c) -> p j c", c=P)[:, 0:3:2, :],
                               ps[:, G0, :].rearrange("p (j c) -> p j c", c=P)[:, 0:4:3, :], ACT.Copy)
                act.activation(gg[:, ROW[2]:ROW[2] + 2 * P], ps[:, G0, P:3 * P], ACT.Copy).then_inc(g_ev[0], 1)
                act.wait_ge(g_ps[2], n + 1)
                act.activation(gg[:, ROW[1]:ROW[1] + P], ps[:, T0, 0:P], ACT.Copy)
                act.activation(gg[:, P:2 * P], ps[:, T0, P:2 * P], ACT.Copy).then_inc(g_ev[2], 1)

            def rounded(act, dst2, bank, src, hi, n):
                for k in range(CB):
                    act.wait_ge(src[k], n + 1)
                    act.activation(dst2[0][:, k, :], ps[:, bank + k, :], ACT.Copy).then_inc(hi[k], 1)

            def make_xh(act, n, par, blocks):
                if blocks[0] == 0:
                    act.wait_ge(ln_done, n + 1)
                    for k in range(CB):
                        wait(act, xhT_ps[k], n)
                for j in blocks:
                    op = act.activation(xh[:, j, :], xk[:, par, j, :], ACT.Identity,
                                        scale=exln[:, par, 0, j:j + 1], bias=exln[:, par, 1, j:j + 1])
                if blocks[-1] == TB - 1:
                    op.then_inc(xh_done, 1)

            def act_body(act, i, par, first, left):
                if left:
                    make_xh(act, i + 1, 1 - par, (0, 1))
                if not first:
                    wait(act, g_ps[2], i - 1)
                    rounded(act, knT2, G0, knT_ps, knT_hi, i - 1)
                if left:
                    make_xh(act, i + 1, 1 - par, (2, 3))
                wait(act, rn_done, i)
                for j in range(TB):
                    act.wait_ge(k_ps[j], i + 1)
                    sq = act.activation(sqj[:, j, :], ps[:, K0 + j, 0:C], ACT.Square, accum_out=ssq[:, j:j + 1])
                sq.then_inc(sq_done, 1)
                if left:
                    rounded(act, xhT2, T0, xhT_ps, xhT_hi, i + 1)
                if not first:
                    act_g(act, i - 1)

            def keys_act(act):
                make_xh(act, 0, 0, range(TB))
                rounded(act, xhT2, T0, xhT_ps, xhT_hi, 0)
                piped(act_body, lambda e: (
                    e.wait_ge(g_ps[2], NS - 1),
                    rounded(e, knT2, G0, knT_ps, knT_hi, NS - 1), act_g(e, NS - 1)))(act)

            def norms(pool, n, par, half):
                m, v = mv[:, :, 0], mv[:, :, 1]
                L = [lns[:, q, :] for q in range(8)]
                s_, b_, r1, sh = (exln[:, par, q, :] for q in range(4))
                steps = [(L[0], v, eps4[:, :], ALU.add), (r1, L[0], mhalf4[:, :], ALU.pow),
                         (L[1], r1, r1, ALU.mult), (L[2], L[1], v, ALU.mult), (L[3], L[2], eps4[:, :], ALU.add),
                         (L[4], L[3], mhalf4[:, :], ALU.pow), (s_, L[4], r1, ALU.mult),
                         (L[5], s_, m, ALU.mult)]
                if half == 0:
                    pool.wait_ge(mv_done, n + 1)
                    wait(pool, ex_done, n - 1)
                    wait(pool, xh_done, n - 1)
                for q in range(5 * half, 5 + 3 * half):
                    o, a, b, op = steps[q]
                    pool.tensor_tensor(o, a, b, op).then_inc(lstep[q], 1)
                    pool.wait_ge(lstep[q], n + 1)
                if half:
                    pool.tensor_tensor(b_, one4[:, :], L[5], ALU.subtract)
                    pool.tensor_tensor(L[6], m, r1, ALU.mult).then_inc(ln_half, 1)
                    pool.wait_ge(ln_half, n + 1)
                    pool.tensor_tensor(sh, zero4[:, :], L[6], ALU.subtract).then_inc(ln_done, 1)

            def pool_body(pool, i, par, first, left):
                if left == 2:
                    norms(pool, i + 2, par, 0)
                pool.wait_ge(sq_done, i + 1)
                wait(pool, kn_done, i)
                pool.tensor_tensor(rn[:, :], ssq[:, :], mhalf4[:, :], ALU.pow).then_inc(rn_done, 1)
                if left == 2:
                    norms(pool, i + 2, par, 1)

            def keys_pool(pool):
                for n in range(2):
                    norms(pool, n, n, 0)
                    norms(pool, n, n, 1)
                piped(pool_body, lambda e: None)(pool)

            def pe_gram(pe, n):
                for k in range(CB):
                    pe.wait_ge(knT_lo[k], n + 1)
                def row(i):
                    bank, c0 = GROW[i]
                    w = (i + 1) * P
                    return split_matmul(pe, ps[:, bank, c0:c0 + w],
                                        knT2, [(slice(None), k, slice(i * P, w)) for k in range(CB)],
                                        knT2, [(slice(None), k, slice(0, w)) for k in range(CB)], True, True)
                row(3).then_inc(g_ps[1], 1)
                row(0)
                row(2).then_inc(g_ps[0], 1)
                pe.wait_ge(xhT_lo[0], min(n + 3, NS) if isinstance(n, int) else n + 3)
                row(1).then_inc(g_ps[2], 1)

            def pe_knT(pe, n):
                pe.wait_ge(kn_done, n + 1)
                wait(pe, g_ev[0], n)
                wait(pe, g_ev[1], n)
                for k in range(CB):
                    for j in range(TB):
                        mm = pe.transpose(ps[:, G0 + k, j * P:(j + 1) * P], kx3[:, j, k * P:(k + 1) * P], ident[:, :])
                    mm.then_inc(knT_ps[k], 1)

            def pe_xhT(pe, n):
                pe.wait_ge(xh_done, n + 1)
                wait(pe, g_ev[2], n - 2)
                for k in range(CB):
                    for j in range(TB):
                        mm = pe.transpose(ps[:, T0 + k, j * P:(j + 1) * P], xh[:, j, k * P:(k + 1) * P], ident[:, :])
                    mm.then_inc(xhT_ps[k], 1)

            def pe_body(pe, i, par, first, left):
                for k in range(CB):
                    pe.wait_ge(xhT_lo[k], i + 1)
                wait(pe, kn_done, i)
                for j in range(TB):
                    if j == 1 and not first:
                        pe_knT(pe, i - 1)
                    split_matmul(pe, ps[:, K0 + j, 0:C + 2],
                                 xhT2, [(slice(None), k, slice(j * P, (j + 1) * P)) for k in range(CB)],
                                 wk2, [(slice(None), k, slice(None)) for k in range(CB)],
                                 True, True).then_inc(k_ps[j], 1)
                if left:
                    pe_xhT(pe, i + 1)
                if not first:
                    pe_gram(pe, i - 1)

            def keys_pe(pe):
                pe_xhT(pe, 0)
                pe.wait_ge(split_done, 1)
                piped(pe_body, lambda e: (
                    pe_knT(e, NS - 1), pe_gram(e, NS - 1)))(pe)

            low = sb("low", [P, SLOTS, SUB * SUB], c=pre)
            inv = sb("inv", [P, SLOTS, SUB * SUB], c=pre)
            tmp = sb("tmp", [P, SLOTS, SUB // 2 * SUB // 2], c=pre)
            low_in, low_early, inv_out = sem("low_in"), sem("low_early"), sem("inv_out")
            DVE_SLOTS = max(1, SLOTS - 1)
            cut = DVE_SLOTS - DVE_SLOTS // 2
            groups = [(s0, s1) + tuple(sem(f"{what}{s0}") for what in ("inv_zero", "inv_one", "prod", "subd"))
                      for s0, s1 in ((0, cut), (cut, DVE_SLOTS), (DVE_SLOTS, SLOTS)) if s0 < s1]
            DVE_GROUPS = [g for g, (_, s1, *_) in enumerate(groups) if s1 <= DVE_SLOTS]
            QV = 2 * C
            wqv = sb("wqv", [P, CB, QV], c=pre)
            bqv = sb("bqv", [1, QV], c=pre)
            mcol = sb("mcol", [P, 3, CB], c=pre)
            wo = sb("wo", [P, CB, C], c=pre)
            w1raw = sb("w1raw", [P, CB, C], c=pre)
            borow = sb("borow", [P, C], c=pre)
            wgi = sb("wgi", [P, HB, C], I32, c=pre)
            wui = sb("wui", [P, HB, C], I32, c=pre)
            wdi = sb("wdi", [P, CB, H], I32, c=pre)
            wgf = sb("wgf", [P, HB, C], c=pre)
            wuf = sb("wuf", [P, HB, C], c=pre)
            wdf = sb("wdf", [P, CB, H], c=pre)
            shift_qv = sb("shift", [P, QV], c=pre)
            wscaled = sb("wscaled", [P, CB, QV], c=pre)
            wfold_qv = sb("wfold", [P, CB, QV], c=pre)
            wvT = sb("wvT", [P, CB, C], c=pre)
            wqT = sb("wqT", [P, CB, C], c=pre)
            wvo = sb("wvo", [P, CB, C], c=pre)
            w1f = sb("w1f", [P, CB, C], c=pre)
            w2f = sb("w2f", [P, CB, C], c=pre)
            b1w = sb("b1w", [P, CB], c=pre)
            w_loaded, ints_in, ints_f = sem("w_loaded"), sem("ints_in"), sem("ints_f")
            scaled = sem("scaled")
            w_shift_ps, w_shift_done, w_fold_done = sem("w_shift_ps"), sem("w_shift_done"), sem("w_fold_done")
            tq_ps, tq_done, vo_ps, vo_done = sem("tq_ps"), sem("tq_done"), sem("vo_ps"), sem("vo_done")
            b1_ps, b1_sb, b1_done, w1_done, bo_done = sem("b1_ps"), sem("b1_sb"), sem("b1_done"), sem("w1_done"), sem("bo_done")
            w_split_hi, w_split_done, wt_ps, wt_ev = sem("w_split_hi"), sem("w_split_done"), sem("wt_ps"), sem("wt_ev")
            LOADS = 11
            whole = ((w2f, w22, None, 0), (w1f, w12, w1_done, CB), (wqT, wqT2, tq_done, 1), (wvo, wvo2, vo_done, 1))
            def load_low(sp):
                sp.wait_ge(low_out, 16 * QPB * (NS - GROUP))
                sp.dma_start(low[:, 0:SLOTS - 1, :], low_lane[:, 0:SLOTS - 1, :]).then_inc(low_early, 16)

            def load_weights(sp, part):
                small = (
                    (wqv[:, :, 0:C], gates_v[:, :, 0:C]), (wqv[:, :, C:QV], gates_v[:, :, 2 * C:3 * C]),
                    (bqv[:, 0:C], row(gates_b)[:, 0:C]), (bqv[:, C:QV], row(gates_b)[:, 2 * C:3 * C]),
                    (mcol[:, 0, :], col(mn_g)), (mcol[:, 1, :], col(mn_b)), (mcol[:, 2, :], col(b1)),
                    (wo[:, :, :], out_w.rearrange("(k p) o -> p k o", p=P)),
                    (w1raw[:, :, :], w1.rearrange("(k p) o -> p k o", p=P)),
                    (w2f[:, :, :], w2.rearrange("(k p) o -> p k o", p=P)),
                    (borow[:, :], row(out_b).partition_broadcast(P)),
                )
                assert len(small) == LOADS
                if part == 0:
                    with nc.allow_non_contiguous_dma(reason="a few columns, once"):
                        for dst, src in small:
                            sp.dma_start(dst, src).then_inc(w_loaded, 16)
                    sp.dma_start(b2_bc[:, :], row(b2).partition_broadcast(P)).then_inc(ints_in, 16)
                else:
                    dst, src = ((wgi, w_gate.rearrange("(h p) c -> p h c", p=P)),
                                (wui, w_up.rearrange("(h p) c -> p h c", p=P)),
                                (wdi, w_down.rearrange("(k p) h -> p k h", p=P)))[part - 1]
                    sp.dma_start(dst[:, :, :], src).then_inc(ints_in, 16)

            def invert_sp(sp):
                sp.wait_ge(low_out, 16 * QPB * NS)
                sp.dma_start(low[:, SLOTS - 1, :], low_lane[:, SLOTS - 1, :]).then_inc(low_in, 16)
                sp.wait_ge(kx_out, 16 * NS)
                sp.wait_ge(gg_out, 16 * NS)
                sp.wait_ge(w_loaded, LOADS * 16)
                sp.wait_ge(ints_in, 64)
                if DVE_SLOTS < SLOTS:
                    sp.wait_ge(groups[-1][-1], SUB - 1)
                    sp.dma_start(inv_lane[:, DVE_SLOTS:SLOTS, :], inv[:, DVE_SLOTS:SLOTS, :]).then_inc(inv_out, 16)
                for g in DVE_GROUPS:
                    sp.wait_ge(groups[g][-1], SUB - 1)
                sp.dma_start(inv_lane[:, 0:DVE_SLOTS, :], inv[:, 0:DVE_SLOTS, :]).then_inc(inv_out, 16)
                sp.wait_ge(inv_out, 16 * (1 + (DVE_SLOTS < SLOTS)))

            def invert_start(eng, g):
                s0, s1, zeroed_, ones_, _, _ = groups[g]
                eng.memset(inv[:, s0:s1, :], 0.0).then_inc(zeroed_, 1)
                eng.wait_ge(zeroed_, 1)
                eng.memset(inv[:, s0:s1, 0:SUB * SUB:SUB + 1], 1.0).then_inc(ones_, 1)
                eng.wait_ge(ones_, 1)
                if s0 < SLOTS - 1:
                    eng.wait_ge(low_early, 16)
                if s1 == SLOTS:
                    eng.wait_ge(low_in, 16)

            def invert_step(eng, g, j, half):
                s0, s1, _, _, prod, subd = groups[g]
                ns, n, w = s1 - s0, SUB - 1 - j, j + 1
                low4 = low[:, s0:s1, :].rearrange("p s (r c) -> p s r c", c=SUB)
                inv4 = inv[:, s0:s1, :].rearrange("p s (r c) -> p s r c", c=SUB)
                t4 = tmp[:, s0:s1, 0:n * w].rearrange("p s (r c) -> p s r c", c=w)
                if half == 0:
                    if j:
                        eng.wait_ge(subd, j)
                    eng.tensor_tensor(t4, low4[:, :, j + 1:SUB, j:j + 1].broadcast_to([P, ns, n, w]),
                                      inv4[:, :, j:j + 1, 0:w].broadcast_to([P, ns, n, w]), ALU.mult).then_inc(prod, 1)
                else:
                    eng.wait_ge(prod, j + 1)
                    eng.tensor_tensor(inv4[:, :, j + 1:SUB, 0:w], inv4[:, :, j + 1:SUB, 0:w], t4,
                                      ALU.subtract).then_inc(subd, 1)

            def invert_groups(eng, mine):
                for g in mine:
                    invert_start(eng, g)
                for j in range(SUB - 1):
                    for half in range(2):
                        for g in mine:
                            invert_step(eng, g, j, half)

            def invert_dve(dve):
                invert_groups(dve, DVE_GROUPS)
                for n, (w, (hi, lo), _, _) in enumerate(whole):
                    dve.wait_ge(w_split_hi, n + 1)
                    dve.tensor_tensor(lo[:, :, :], w[:, :, :], hi[:, :, :].bitcast(F32), ALU.subtract).then_inc(w_split_done, 1)
                dve.wait_ge(w_split_done, len(whole))

            def invert_pool(pool):
                pool.wait_ge(scaled, CB)
                pool.wait_ge(w_shift_done, 1)
                for k in range(CB):
                    pool.tensor_tensor(wfold_qv[:, k, :], wscaled[:, k, :], shift_qv[:, :], ALU.add).then_inc(w_fold_done, 1)
                pool.wait_ge(b1_sb, 1)
                pool.tensor_tensor(b1f[:, :], b1w[:, :], mcol[:, 2, :], ALU.add).then_inc(b1_done, 1)
                if DVE_SLOTS < SLOTS:
                    invert_groups(pool, (len(groups) - 1,))
                pool.wait_ge(b1_done, 1)

            def invert_act(act):
                act.wait_ge(w_loaded, LOADS * 16)
                for k in range(CB):
                    act.activation(wscaled[:, k, :], wqv[:, k, :], ACT.Identity, scale=dcol[:, 0, k:k + 1],
                                   bias=zero4[:, 0:1]).then_inc(scaled, 1)
                act.wait_ge(w_shift_ps, 1)
                act.activation(shift_qv[:, :], ps[:, 0, :], ACT.Copy, scale=1.0 / C).then_inc(w_shift_done, 1)
                act.activation(bo_bc[:, :], borow[:, :], ACT.Copy, scale=1.0 / C).then_inc(bo_done, 1)
                for k in range(CB):
                    act.activation(w1f[:, k, :], w1raw[:, k, :], ACT.Identity, scale=mcol[:, 0, k:k + 1],
                                   bias=zero4[:, 0:1]).then_inc(w1_done, 1)
                act.wait_ge(b1_ps, 1)
                act.activation(b1w[:, :], ps[:, 3, 0:CB], ACT.Copy).then_inc(b1_sb, 1)
                act.wait_ge(tq_ps, 1)
                act.activation(wqT[:, :, :].rearrange("p a b -> p (a b)"), ps[:, 4, :], ACT.Copy).then_inc(tq_done, 1)
                act.wait_ge(tq_ps, 2)
                act.activation(wvT[:, :, :].rearrange("p a b -> p (a b)"), ps[:, 5, :], ACT.Copy).then_inc(tq_done, 1)
                act.wait_ge(vo_ps, 1)
                act.activation(wvo[:, :, :].rearrange("p a b -> p (a b)"), ps[:, 6, :], ACT.Copy).then_inc(vo_done, 1)
                for w, (hi, lo), made, n in whole:
                    if made is not None:
                        act.wait_ge(made, n)
                    act.activation(hi[:, :, :], w[:, :, :], ACT.Copy).then_inc(w_split_hi, 1)
                act.wait_ge(ints_in, 64)
                for dst, src in ((wgf, wgi), (wuf, wui), (wdf, wdi)):
                    act.activation(dst[:, :, :], src[:, :, :], ACT.Copy).then_inc(ints_f, 1)
                g = 0
                for dst in (wgT, wuT):
                    for k in range(CB):
                        for n in range(0, HB, 2):
                            act.wait_ge(wt_ps, g + 1)
                            act.activation(dst[:, k, n * P:(n + 2) * P], ps[:, g % 2, 0:2 * P], ACT.Copy).then_inc(wt_ev, 1)
                            g += 1
                for n in range(HB):
                    act.wait_ge(wt_ps, g + 1)
                    act.activation(wdT[:, n, :], ps[:, g % 2, 0:C], ACT.Copy).then_inc(wt_ev, 1)
                    g += 1
                act.wait_ge(bo_done, 1)

            def invert_pe(pe):
                pe.wait_ge(w_loaded, LOADS * 16)
                for q in range(3):
                    pe.wait_ge(g_ev[q], NS)
                for k in range(CB):
                    pe.matmul(ps[:, 0, :], diff_bc[:, k, :], wqv[:, k, :], start=(k == 0), stop=False)
                pe.matmul(ps[:, 0, :], ones[0:1, :], bqv[:, :], start=False, stop=True).then_inc(w_shift_ps, 1)
                for m in range(CB):
                    for k in range(CB):
                        mm = pe.matmul(ps[:, 3, m:m + 1], w1raw[:, k, m * P:(m + 1) * P], mcol[:, 1, k:k + 1],
                                       start=(k == 0), stop=(k == CB - 1))
                mm.then_inc(b1_ps, 1)
                pe.wait_ge(w_fold_done, CB)
                for bank, c0 in ((4, 0), (5, C)):
                    for m in range(CB):
                        for k in range(CB):
                            mm = pe.transpose(ps[:, bank, m * C + k * P:m * C + (k + 1) * P],
                                              wfold_qv[:, k, c0 + m * P:c0 + (m + 1) * P], ident[:, :])
                    mm.then_inc(tq_ps, 1)
                pe.wait_ge(tq_done, 2)
                for m in range(CB):
                    for k in range(CB):
                        mm = pe.matmul(ps[:, 6, m * C:(m + 1) * C], wvT[:, k, m * P:(m + 1) * P], wo[:, k, :],
                                       start=(k == 0), stop=(k == CB - 1))
                mm.then_inc(vo_ps, 1)
                pe.wait_ge(ints_f, 3)
                pe.wait_ge(w_shift_done, 1)
                g = 0
                for src in (wgf, wuf):
                    for k in range(CB):
                        for n in range(0, HB, 2):
                            wait(pe, wt_ev, g - 1)
                            for q in range(2):
                                mm = pe.transpose(ps[:, g % 2, q * P:(q + 1) * P], src[:, n + q, k * P:(k + 1) * P], ident[:, :])
                            mm.then_inc(wt_ps, 1)
                            g += 1
                for n in range(HB):
                    pe.wait_ge(wt_ev, g - 1)
                    for k in range(CB):
                        mm = pe.transpose(ps[:, g % 2, k * P:(k + 1) * P], wdf[:, k, n * P:(n + 1) * P], ident[:, :])
                    mm.then_inc(wt_ps, 1)
                    g += 1
                pe.wait_ge(wt_ev, g)

            with nc.Block() as block:
                @block.sync
                def _(sp):
                    setup_sp(sp)
                    keys_sp(sp)
                    invert_sp(sp)

                @block.gpsimd
                def _(pool):
                    setup_pool(pool)
                    keys_pool(pool)
                    invert_pool(pool)

                @block.vector
                def _(dve):
                    stats(dve, 0, 0)
                    setup_dve(dve)
                    keys_dve(dve)
                    invert_dve(dve)

                @block.scalar
                def _(act):
                    setup_act(act)
                    keys_act(act)
                    invert_act(act)

                @block.tensor
                def _(pe):
                    setup_pe(pe)
                    keys_pe(pe)
                    invert_pe(pe)
            end_program()

        with ExitStack() as mc:
            def mb(name, shape, dt=F32):
                return sb(name, shape, dt, c=mc)

            xT32 = mb("xT32", [P, TB, P])
            p1 = mb("p1", [P, TB, P])
            x64 = mb("x64", [P, TB, P])
            HALF = P // 2
            p2 = mb("p2", [P, TB, HALF])
            wt = mb("wt", [P, TB, C])
            xhm2 = pair("xhm", [P, TB, C], c=mc)
            gl2 = pair("gl", [P, GW - OFF], c=mc)
            z2 = pair("z", [P, TB, C], c=mc)
            bt2 = pair("bt", [P, CB, C], c=mc)
            e2 = pair("e", [P, CB, C], c=mc)
            m2 = mb("m2", [P, CB, C])
            m22 = pair("m2", [P, CB, C], c=mc)
            a0 = mb("a0", [P, TB, C])
            shf = mb("shf", [P, TB])
            bs2, mv2, ls2, sc2 = mb("bs2", [P, TB, 6]), mb("mv2", [P, TB, 2]), mb("ls2", [P, 2, TB]), mb("sc2", [P, 2, TB])
            bs3, mv3, ls3, sc3 = mb("bs3", [P, TB, 6]), mb("mv3", [P, TB, 2]), mb("ls3", [P, 2, TB]), mb("sc3", [P, 2, TB])
            xn = mb("xn", [P, TB, C])
            xh2T2 = pair("xh2T", [P, CB, T], c=mc)
            h1 = mb("h1", [P, CB, T])
            h12 = pair("h1", [P, CB, T], c=mc)
            xa = mb("xa", [P, TB, C])
            xa2 = mb("xa2", [P, TB, C])
            x2 = mb("x2", [P, TB, C])
            xh3T2 = pair("xh3T", [P, CB, T], c=mc)
            x3h, x3l = xh3T2
            sg = mb("sg", [P, 2, T])
            hf = mb("hf", [P, 2, T])
            hh = mb("hh", [P, HB, T], F32R)
            hl = mb("hl", [P, HB, T], F32R)
            ot = mb("ot", [P, TB, C])
            x2k = mb("x2k", [P, TB, C])

            inv_in, gg_in, kx_in, xin, out_st = sem("inv_in"), sem("gg_in"), sem("kx_in"), sem("xin"), sem("out_st")
            xT_ps, xT_ev, x64_odd, p1_zero = sem("xT_ps"), sem("xT_ev"), sem("x64_odd"), sem("p1_zero")
            p32_ps, p32_ev, p64_ps, p64_ev = sem("p32_ps"), sem("p32_ev"), sem("p64_ps"), sem("p64_ev")
            x64_ps, x64_ev, xT64_ps, xT64_ev = sem("x64_ps"), sem("x64_ev"), sem("xT64_ps"), sem("xT64_ev")
            x128_ps, x128_ev = sem("x128_ps"), sem("x128_ev")
            w_ps, w_ev, z_ps = sems("w_ps", TB - 1), sems("w_ev", TB), sems("z_ps", TB)
            z_hi, z_ev = sems("z_hi", TB), sems("z_ev", TB)
            ht_ps, ht_hi, ht_ev = sems("ht_ps", CB), sems("ht_hi", CB), sems("ht_ev", CB)
            bt_ps, bt_hi, bt_ev, e_ps, e_hi, e_ev = sem("bt_ps"), sem("bt_hi"), sem("bt_ev"), sem("e_ps"), sem("e_hi"), sem("e_ev")
            m2_ps, m2_sum, m2_hi, m2_ev = sem("m2_ps"), sem("m2_sum"), sem("m2_hi"), sem("m2_ev")
            xhm_hi, xhm_lo, gl_hi, gl_lo = sem("xhm_hi"), sem("xhm_lo"), sem("gl_hi"), sem("gl_lo")
            y_ps, a0_ev = sems("y_ps", 2), sems("a0_ev", TB)
            bn2, mv2_done, l2, ln2_done = sems("bn2_", TB), sem("mv2_done"), sems("l2_", 3), sem("ln2_done")
            bn3, mv3_done, l3, ln3_done = sems("bn3_", TB), sem("mv3_done"), sems("l3_", 3), sem("ln3_done")
            xhm_done, xh2_done, xh3_done = sem("xhm_done"), sem("xh2_done"), sem("xh3_done")
            xb_done, xa_done, sh_done = sem("xb_done"), sem("xa_done"), sem("sh_done")
            t2_ps, t2_hi, t2_ev = sems("t2_ps", 2), sems("t2_hi", 2), sems("t2_ev", 2)
            m1_ps, h1_ev, h1_hi, h1_lo = sems("m1_ps", 2), sems("h1_ev", 2), sems("h1_hi", 2), sems("h1_lo", 2)
            mo_ps, x2_ev = sems("mo_ps", 2), sems("x2_ev", TB)
            t3_ps, x3h_ev, x3l_ev = sems("t3_ps", 2), sems("x3h_ev", 2), sems("x3l_ev", 2)
            gate_ps, up_ps = sems("gate_ps", HB), sems("up_ps", HB)
            sg_ev, hf_ev, hh_ev, hl_ev = sems("sg_ev", HB), sems("hf_ev", HB), sems("hh_ev", HB), sems("hl_ev", HB)
            fo_ps, ot_ev, x2_kept = sems("fo_ps", 2), sems("ot_ev", 2), sem("x2_kept")

            def quarters(t, first):
                return t.rearrange("p (q c) -> p q c", c=SUB)[:, first::2, :]

            def quarters4(t, first):
                return t[:, :, :].rearrange("p j (q c) -> p j q c", c=SUB)[:, :, first::2, :]

            def diag(j):
                return gg[:, j * P:(j + 1) * P]

            def blk(j):
                return slice(j * P, (j + 1) * P)

            def after(eng, sem, n, each=1):
                if isinstance(n, int):
                    n = min(n, NS)
                wait(eng, sem, n * each)

            def overlapped(body):
                def run(eng):
                    body(eng, 0, True, False, False)
                    body(eng, 1, True, True, False)
                    body(eng, 2, True, True, True)
                    with eng.Fori(3, NS) as i:
                        body(eng, i, True, True, True)
                    body(eng, NS, False, True, True)
                    body(eng, NS + 1, False, False, True)
                return run

            def up_bank(h):
                return (FU, S0)[h % 2]

            with nc.Block() as block:
                def pe_transposes(pe, banks, src, done):
                    for k in range(CB):
                        for j in range(TB):
                            mm = pe.transpose(ps[:, banks[k], blk(j)], src[:, j, blk(k)], ident[:, :])
                        mm.then_inc(done[k], 1)

                def pe_level(pe, bank, lhs, rhs, done):
                    for j in range(TB):
                        mm = pe.matmul(ps[:, bank, j * HALF:(j + 1) * HALF], lhs(j), rhs(j), start=True, stop=True)
                    mm.then_inc(done, 1)

                def pe_zstep(pe, i, j):
                    pe.wait_ge(w_ev[j], i + 1)
                    if j < TB - 1:
                        pe.wait_ge(z_ev[j + 1], i + 1)
                    else:
                        pe.wait_ge(x128_ev, i + 1)
                    pe.matmul(ps[:, A1, 0:C], x64[:, j, :], wt[:, j, :], start=True, stop=True).then_inc(z_ps[j], 1)

                def pe_wstep(pe, i, j):
                    pe.wait_ge(z_ev[j + 1], i + 1)
                    if j < TB - 2:
                        pe.wait_ge(w_ev[j + 1], i + 1)
                    if j == TB - 2:
                        pe.wait_ge(gl_lo, i + 1)
                    later = range(TB - 1, j, -1)
                    cols = [GCOL[(m, j)] - OFF for m in later]
                    split_matmul(pe, ps[:, A0, 0:C], gl2, [(slice(None), slice(c, c + P)) for c in cols],
                                 z2, [(slice(None), m, slice(None)) for m in later], True, True).then_inc(w_ps[j], 1)

                def pe_bt(pe, i, j):
                    pe.wait_ge(z_ev[j], i + 1)
                    if j == TB - 1:
                        pe.wait_ge(xhm_lo, i + 1)
                    for m in range(CB):
                        mm = split_matmul(pe, ps[:, A2, m * C:(m + 1) * C], xhm2, [(slice(None), j, blk(m))],
                                          z2, [(slice(None), j, slice(None))], j == TB - 1 and m == 0, j == 0,
                                          skip_group_check=True)
                    if j == 0:
                        mm.then_inc(bt_ps, 1)

                def pe_square(pe, bank, lhs, rhs, done):
                    for m in range(CB):
                        mm = split_matmul(pe, ps[:, bank, m * C:(m + 1) * C], lhs, [(slice(None), k, blk(m)) for k in range(CB)],
                                          rhs, [(slice(None), k, slice(None)) for k in range(CB)], True, True)
                    mm.then_inc(done, 1)

                def pe_tokens(pe, bank, half, lhs, rhs, done, before=None):
                    for q in range(2):
                        mm = split_matmul(pe, ps[:, bank, q * C:(q + 1) * C],
                                          lhs, [(slice(None), k, blk(2 * half + q)) for k in range(CB)],
                                          rhs, [(slice(None), k, slice(None)) for k in range(CB)], True, True,
                                          before=None if q else before)
                    mm.then_inc(done, 1)

                def pe_mlp1(pe, i, m):
                    for k in range(CB):
                        if m == 0:
                            pe.wait_ge(t2_ev[k], i)
                        mm = split_matmul(pe, ps[:, (FU, S0)[m], :], w12, [(slice(None), k, blk(m))],
                                          xh2T2, [(slice(None), k, slice(None))], k == 0, k == CB - 1)
                    mm.then_inc(m1_ps[m], 1)

                def pe_gate_up(pe, i, h):
                    if h == 0:
                        after(pe, ht_ev[1], i + 1)
                    else:
                        pe.wait_ge(sg_ev[h - 1], i)
                    for w, bank, done in ((wgT, FG, gate_ps[h]), (wuT, up_bank(h), up_ps[h])):
                        if bank != FG:
                            if h >= 2:
                                pe.wait_ge(hf_ev[h - 2], i)
                            elif h == 1:
                                after(pe, ht_ev[0], i + 1)
                            else:
                                after(pe, ot_ev[1], i - 1)
                        for k in range(CB):
                            if h == 0 and bank == FG:
                                pe.wait_ge(x3h_ev[k], i)
                                pe.wait_ge(x3l_ev[k], i)
                            for part in (x3h, x3l):
                                mm = pe.matmul(ps[:, bank, :], w[:, k, blk(h)], part[:, k, :],
                                               start=(k == 0 and part is x3h), stop=(k == CB - 1 and part is x3l))
                        mm.then_inc(done, 1)

                def pe_down(pe, i, j, blocks=range(HB)):
                    for h in blocks:
                        for part, made in ((hh, hh_ev), (hl, hl_ev)):
                            if j == 0:
                                pe.wait_ge(made[h], i - 1)
                            mm = pe.matmul(ps[:, (FG, FU)[j // 2], (j % 2) * C:(j % 2 + 1) * C], part[:, h, blk(j)],
                                           wdT[:, h, :], start=(h == 0 and part is hh),
                                           stop=(h == HB - 1 and part is hl))
                    if j % 2 and h == HB - 1:
                        mm.then_inc(fo_ps[j // 2], 1)

                def pe_body(pe, i, att, mlp, down):
                    if att:
                        pe.wait_ge(inv_in, (i + 1) * 16 * QPB)
                        after(pe, a0_ev[TB - 1], i)
                        for j in range(TB):
                            mm = pe.transpose(ps[:, A2, blk(j)], x32[:, j, :], ident[:, :])
                        mm.then_inc(xT_ps, 1)
                        pe.wait_ge(gg_in, (i + 1) * 16)
                        after(pe, a0_ev[1], i)
                        pe_level(pe, A0, diag, lambda j: quarters(x32[:, j, :], 0), p32_ps)
                    if down:
                        after(pe, sg_ev[HB - 1], i - 1)
                        pe_down(pe, i, 0, range(HB - 1))
                    if att:
                        pe.wait_ge(p32_ev, i + 1)
                        pe.wait_ge(xT_ev, i + 1)
                        after(pe, m2_sum, i)
                        pe_level(pe, A1, lambda j: xT32[:, j, :], lambda j: quarters(p1[:, j, :], 0), x64_ps)
                        pe_level(pe, A2, lambda j: p1[:, j, :], lambda j: quarters(xT32[:, j, :], 1), xT64_ps)
                    if mlp:
                        pe.wait_ge(xh2_done, i)
                        for k in range(CB):
                            after(pe, x3h_ev[k], i - 1)
                            after(pe, x3l_ev[k], i - 1)
                        pe_transposes(pe, (FO0, FO1), xn, t2_ps)
                    if down:
                        pe_down(pe, i, 0, (HB - 1,))
                        pe_down(pe, i, 1)
                    if att:
                        pe.wait_ge(x64_ev, i + 1)
                        pe.wait_ge(x64_odd, i + 1)
                        pe_level(pe, A0, diag, lambda j: x64[:, j, 0:HALF], p64_ps)
                    if mlp:
                        after(pe, hf_ev[HB - 2], i - 1)
                        pe_mlp1(pe, i, 0)
                    if att:
                        pe.wait_ge(p64_ev, i + 1)
                        pe.wait_ge(xT64_ev, i + 1)
                        pe_level(pe, A1, lambda j: xT32[:, j, :], lambda j: p2[:, j, :], x128_ps)
                    if mlp:
                        after(pe, hf_ev[HB - 1], i - 1)
                        pe_mlp1(pe, i, 1)
                    if att:
                        pe_zstep(pe, i, 3)
                    if down:
                        after(pe, h1_ev[0], i)
                        pe_down(pe, i, 2)
                    if att:
                        pe_wstep(pe, i, 2)
                    if mlp:
                        pe_tokens(pe, FO0, 0, h12, w22, mo_ps[0], lambda k: pe.wait_ge(h1_lo[k], i))
                    if att:
                        pe_zstep(pe, i, 2)
                    if mlp:
                        pe_tokens(pe, FO1, 1, h12, w22, mo_ps[1])
                    if att:
                        pe_wstep(pe, i, 1)
                        pe.wait_ge(xhm_done, i + 1)
                        after(pe, h1_ev[1], i)
                        after(pe, ot_ev[0], i - 1)
                        pe_transposes(pe, (S0, FG), xh, ht_ps)
                        pe_bt(pe, i, 3)
                        pe_zstep(pe, i, 1)
                    if down:
                        pe_down(pe, i, 3)
                    if att:
                        pe_wstep(pe, i, 0)
                        pe_bt(pe, i, 2)
                        pe_zstep(pe, i, 0)
                    if mlp:
                        pe.wait_ge(xh3_done, i)
                        for j in range(TB):
                            pe.wait_ge(x2_ev[j], i)
                        pe_transposes(pe, (FO0, FO1), xn, t3_ps)
                    if att:
                        pe_bt(pe, i, 1)
                        pe_bt(pe, i, 0)
                    if mlp:
                        pe_gate_up(pe, i, 0)
                    if att:
                        pe.wait_ge(bt_ev, i + 1)
                        pe_square(pe, A0, bt2, wvo2, e_ps)
                    if mlp:
                        pe_gate_up(pe, i, 1)
                    if att:
                        pe.wait_ge(e_ev, i + 1)
                        pe_square(pe, A1, wqT2, e2, m2_ps)
                    if mlp:
                        pe_gate_up(pe, i, 2)
                        pe_gate_up(pe, i, 3)
                    if att:
                        pe.wait_ge(m2_ev, i + 1)
                        pe_tokens(pe, A0, 0, xhT2, m22, y_ps[0])
                        pe_tokens(pe, A2, 1, xhT2, m22, y_ps[1])
                    if mlp:
                        pe_gate_up(pe, i, 4)
                        pe_gate_up(pe, i, 5)

                @block.tensor
                def _(pe):
                    overlapped(pe_body)(pe)

                def flat(t):
                    return t[:, :, :].rearrange("p a b -> p (a b)")

                def act_silu(act, i, h):
                    act.wait_ge(gate_ps[h], i)
                    if h >= 2:
                        act.wait_ge(hf_ev[h - 2], i)
                    else:
                        after(act, hf_ev[HB - 2 + h], i - 1)
                    act.activation(sg[:, h % 2, :], ps[:, FG, :], ACT.Silu, scale=QUANT).then_inc(sg_ev[h], 1)

                def act_hh(act, i, h):
                    act.wait_ge(hf_ev[h], i)
                    act.activation(hh[:, h, :], hf[:, h % 2, :], ACT.Copy).then_inc(hh_ev[h], 1)

                def act_z(act, i, j):
                    act.wait_ge(z_ps[j], i + 1)
                    act.activation(z2[0][:, j, :], ps[:, A1, 0:C], ACT.Copy).then_inc(z_hi[j], 1)

                def act_hi(act, dst, banks, src, done, n):
                    for k in range(CB):
                        act.wait_ge(src[k], n)
                        act.activation(dst[:, k, :], ps[:, banks[k], :], ACT.Copy).then_inc(done[k], 1)

                def act_body(act, i, att, mlp, down):
                    if att:
                        act.wait_ge(xT_ps, i + 1)
                        act.activation(flat(xT32), ps[:, A2, :], ACT.Copy).then_inc(xT_ev, 1)
                    if down:
                        act_hh(act, i - 1, HB - 1)
                    if att:
                        after(act, z_ps[0], i)
                        act.activation(quarters4(x64, 1), quarters4(x32, 1), ACT.Copy).then_inc(x64_odd, 1)
                    if mlp:
                        act_hi(act, xh2T2[0], (FO0, FO1), t2_ps, t2_hi, i)
                        for m in range(CB):
                            act.wait_ge(m1_ps[m], i)
                            act.activation(h1[:, m, :], ps[:, (FU, S0)[m], :], ACT.Relu, bias=b1f[:, m:m + 1]).then_inc(h1_ev[m], 1)
                    if att:
                        act_z(act, i, 3)
                        act_z(act, i, 2)
                        act_hi(act, xhT2[0], (S0, FG), ht_ps, ht_hi, i + 1)
                        act_z(act, i, 1)
                        act_z(act, i, 0)
                    if mlp:
                        act_hi(act, x3h, (FO0, FO1), t3_ps, x3h_ev, i)
                    if att:
                        act.wait_ge(bt_ps, i + 1)
                        act.activation(flat(bt2[0]), ps[:, A2, :], ACT.Copy).then_inc(bt_hi, 1)
                    if mlp:
                        act_silu(act, i, 0)
                        for j in range(TB):
                            act.wait_ge(x2_ev[j], i)
                        after(act, ot_ev[1], i - 1)
                        act.activation(x2k[:, :, :], x2[:, :, :], ACT.Copy).then_inc(x2_kept, 1)
                        act_hh(act, i, 0)
                    if att:
                        act.wait_ge(e_ps, i + 1)
                        act.activation(flat(e2[0]), ps[:, A0, :], ACT.Copy).then_inc(e_hi, 1)
                    if mlp:
                        act_silu(act, i, 1)
                        act_hh(act, i, 1)
                        act_silu(act, i, 2)
                    if att:
                        act.wait_ge(m2_sum, i + 1)
                        act.activation(m22[0][:, :, :], m2[:, :, :], ACT.Copy).then_inc(m2_hi, 1)
                    if mlp:
                        act_hh(act, i, 2)
                        for h in range(3, HB):
                            act_silu(act, i, h)
                            if h < HB - 1:
                                act_hh(act, i, h)

                @block.scalar
                def _(act):
                    overlapped(act_body)(act)

                def masked(dve, dst, mask, src_ps, done, i):
                    dve.wait_ge(src_ps, i + 1)
                    dve.tensor_tensor(dst, halves(A0, dst), mask, ALU.mult).then_inc(done, 1)

                def plus(dve, dst, bank, src, src_ps, done, i):
                    dve.wait_ge(src_ps, i + 1)
                    dve.tensor_tensor(dst, halves(bank, dst), src, ALU.add).then_inc(done, 1)

                def halves(bank, like):
                    v = ps[:, bank, 0:TB * HALF]
                    if len(like.shape) == 4:
                        return v.rearrange("p (j q c) -> p j q c", j=TB, c=SUB)
                    return v.rearrange("p (j c) -> p j c", c=HALF)

                def dve_w(dve, i, j):
                    dve.wait_ge(w_ps[j], i + 1)
                    dve.scalar_tensor_tensor(out=wt[:, j, :], in0=kx3[:, j, :], scalar=kx[:, E_LR + j:E_LR + j + 1],
                                             in1=ps[:, A0, 0:C], op0=ALU.mult, op1=ALU.subtract).then_inc(w_ev[j], 1)

                def dve_stats(dve, n_done, bst_, mv_, bns, mvd):
                    for j in range(TB):
                        dve.wait_ge(ready, 1)
                        dve.wait_ge(bns[j], n_done)
                        agg = dve.bn_aggr(mv_[:, j, :], bst_[:, j, :])
                    agg.then_inc(mvd, 1)

                def dve_x2(dve, i, half):
                    dve.wait_ge(mo_ps[half], i)
                    if half == 0:
                        dve.wait_ge(xa_done, i)
                        dve.wait_ge(sh_done, i)
                        after(dve, x2_kept, i - 1)
                        after(dve, ln3_done, i - 1)
                    for j in (2 * half, 2 * half + 1):
                        dve.scalar_tensor_tensor(out=x2[:, j, :], in0=xa2[:, j, :], scalar=shf[:, j:j + 1],
                                                 in1=ps[:, FO0 + half, (j % 2) * C:(j % 2 + 1) * C],
                                                 op0=ALU.add, op1=ALU.add).then_inc(x2_ev[j], 1)

                def dve_xh3(dve, blocks):
                    for j in blocks:
                        op = dve.tensor_scalar(xn[:, j, :], x2[:, j, :], sc3[:, 0, j:j + 1], sc3[:, 1, j:j + 1],
                                               ALU.mult, ALU.add)
                    return op

                def dve_x2_stats(dve, i, half):
                    for j in (2 * half, 2 * half + 1):
                        dve.wait_ge(x2_ev[j], i)
                        dve.bn_stats(bs3[:, j, :], x2[:, j, :]).then_inc(bn3[j], 1)

                def dve_up(dve, i, h):
                    dve.wait_ge(up_ps[h], i)
                    dve.wait_ge(sg_ev[h], i)
                    for made in (hh_ev, hl_ev):
                        if h >= 2:
                            dve.wait_ge(made[h - 2], i)
                        else:
                            after(dve, made[HB - 2 + h], i - 1)
                    dve.tensor_tensor(hf[:, h % 2, :], ps[:, up_bank(h), :], sg[:, h % 2, :], ALU.mult).then_inc(hf_ev[h], 1)

                def dve_rest(dve, lo, whole, hi, hi_done, n_done, done):
                    dve.wait_ge(hi_done, n_done)
                    dve.tensor_tensor(lo, whole, hi.bitcast(F32), ALU.subtract).then_inc(done, 1)

                def dve_hl(dve, i, h):
                    dve_rest(dve, hl[:, h, :], hf[:, h % 2, :], hh[:, h, :], hh_ev[h], i, hl_ev[h])

                def dve_z(dve, i, j):
                    dve_rest(dve, z2[1][:, j, :], ps[:, A1, 0:C], z2[0][:, j, :], z_hi[j], i + 1, z_ev[j])

                def dve_h1_hi(dve, i, m):
                    dve.wait_ge(h1_ev[m], i)
                    dve.tensor_copy(h12[0][:, m, :], h1[:, m, :]).then_inc(h1_hi[m], 1)

                def dve_h1_lo(dve, i, m):
                    dve_rest(dve, h12[1][:, m, :], h1[:, m, :], h12[0][:, m, :], h1_hi[m], i, h1_lo[m])

                def dve_lo(dve, lo, hi, banks, hi_done, done, n, which=range(CB)):
                    for k in which:
                        dve_rest(dve, lo[:, k, :], ps[:, banks[k], :], hi[:, k, :], hi_done[k], n, done[k])

                def dve_out(dve, i, half):
                    dve.wait_ge(fo_ps[half], i - 1)
                    if half == 0:
                        after(dve, out_st, i - 2, 16)
                        dve.wait_ge(x2_kept, i - 1)
                    dve.scalar_tensor_tensor(
                        out=ot[:, 2 * half:2 * half + 2, :].rearrange("p j c -> p (j c)"), in0=ps[:, (FG, FU)[half], :],
                        scalar=QUANT * QUANT, in1=x2k[:, 2 * half:2 * half + 2, :].rearrange("p j c -> p (j c)"),
                        op0=ALU.mult, op1=ALU.add).then_inc(ot_ev[half], 1)

                def bank3(bank):
                    return ps[:, bank, :].rearrange("p (k c) -> p k c", c=C)

                def dve_body(dve, i, att, mlp, down):
                    if att:
                        masked(dve, quarters4(p1, 0), mask32[:, :].rearrange("p (q c) -> p q c", c=SUB)[:, 0::2, :]
                               .unsqueeze(1).broadcast_to([P, TB, 2, SUB]), p32_ps, p32_ev, i)
                    if down:
                        dve_hl(dve, i - 1, HB - 1)
                    if att:
                        dve.wait_ge(gg_in, (i + 1) * 16)
                        after(dve, w_ps[0], i)
                        dve.tensor_copy(gl2[0][:, :], gg[:, OFF:GW]).then_inc(gl_hi, 1)
                        plus(dve, quarters4(x64, 0), A1, quarters4(x32, 0), x64_ps, x64_ev, i)
                        plus(dve, quarters4(xT32, 1), A2, quarters4(xT32, 1), xT64_ps, xT64_ev, i)
                    if mlp:
                        dve_lo(dve, xh2T2[1], xh2T2[0], (FO0, FO1), t2_hi, t2_ev, i)
                    if down:
                        dve_out(dve, i, 0)
                    if att:
                        masked(dve, p2[:, :, :], mask64[:, 0:HALF].unsqueeze(1).broadcast_to([P, TB, HALF]),
                               p64_ps, p64_ev, i)
                    if att:
                        dve.wait_ge(kx_in, (i + 1) * 16)
                        dve.tensor_scalar(wt[:, 3, :], kx3[:, 3, :], kx[:, E_LR + 3:E_LR + 4], None,
                                          ALU.mult).then_inc(w_ev[3], 1)
                    if mlp:
                        dve_h1_hi(dve, i, 0)
                    if att:
                        plus(dve, x64[:, :, 0:HALF], A1, x64[:, :, 0:HALF], x128_ps, x128_ev, i)
                    if mlp:
                        dve_h1_lo(dve, i, 0)
                        dve_h1_hi(dve, i, 1)
                    if att:
                        dve_z(dve, i, 3)
                    if mlp:
                        dve_h1_lo(dve, i, 1)
                    if att:
                        dve.wait_ge(xhm_done, i + 1)
                        after(dve, bt_ps, i)
                        dve.tensor_copy(xhm2[0][:, :, :], xh[:, :, :]).then_inc(xhm_hi, 1)
                        dve_w(dve, i, 2)
                    if mlp:
                        dve_x2(dve, i, 0)
                    if att:
                        dve_z(dve, i, 2)
                    if mlp:
                        dve_x2_stats(dve, i, 0)
                        dve_x2(dve, i, 1)
                    if att:
                        dve_w(dve, i, 1)
                    if mlp:
                        dve_x2_stats(dve, i, 1)
                        dve_stats(dve, i, bs3, mv3, bn3, mv3_done)
                    if att:
                        dve_lo(dve, xhT2[1], xhT2[0], (S0, FG), ht_hi, ht_ev, i + 1, (0,))
                        dve_z(dve, i, 1)
                        dve_lo(dve, xhT2[1], xhT2[0], (S0, FG), ht_hi, ht_ev, i + 1, (1,))
                    if mlp:
                        dve.wait_ge(ln3_done, i)
                        dve_xh3(dve, range(2))
                    if att:
                        dve_w(dve, i, 0)
                    if mlp:
                        dve_xh3(dve, range(2, TB)).then_inc(xh3_done, 1)
                    if down:
                        dve_out(dve, i, 1)
                    if att:
                        dve_z(dve, i, 0)
                    if mlp:
                        dve_lo(dve, x3l, x3h, (FO0, FO1), x3h_ev, x3l_ev, i)
                    if att:
                        dve_rest(dve, bt2[1][:, :, :], bank3(A2), bt2[0][:, :, :], bt_hi, i + 1, bt_ev)
                    if mlp:
                        dve_up(dve, i, 0)
                    if att:
                        dve_rest(dve, e2[1][:, :, :], bank3(A0), e2[0][:, :, :], e_hi, i + 1, e_ev)
                    if mlp:
                        dve_up(dve, i, 1)
                    if att:
                        dve.wait_ge(m2_ps, i + 1)
                        dve.tensor_tensor(m2[:, :, :], bank3(A1), bo_bc[:, :].unsqueeze(1).broadcast_to([P, CB, C]),
                                          ALU.add).then_inc(m2_sum, 1)
                    if mlp:
                        dve_up(dve, i, 2)
                    if att:
                        dve_rest(dve, m22[1][:, :, :], m2[:, :, :], m22[0][:, :, :], m2_hi, i + 1, m2_ev)
                    if mlp:
                        dve_up(dve, i, 3)
                    if att:
                        dve.wait_ge(xin, (i + 1) * 16)
                        after(dve, xa_done, i)
                        after(dve, ln2_done, i)
                        for j in range(TB):
                            if j % 2 == 0:
                                dve.wait_ge(y_ps[j // 2], i + 1)
                            dve.scalar_tensor_tensor(out=a0[:, j, :], in0=xt[:, j, :], scalar=kx[:, E_R1 + j:E_R1 + j + 1],
                                                     in1=ps[:, (A0, A2)[j // 2], (j % 2) * C:(j % 2 + 1) * C],
                                                     op0=ALU.mult, op1=ALU.add).then_inc(a0_ev[j], 1)
                        for j in range(TB):
                            dve.wait_ge(a0_ev[j], i + 1)
                            dve.bn_stats(bs2[:, j, :], a0[:, j, :]).then_inc(bn2[j], 1)
                        dve_stats(dve, i + 1, bs2, mv2, bn2, mv2_done)
                    if mlp:
                        dve_up(dve, i, 4)
                        dve_hl(dve, i, 4)
                        dve_up(dve, i, 5)

                @block.vector
                def _(dve):
                    dve.memset(p1[:, :, :], 0.0).then_inc(p1_zero, 1)
                    dve.wait_ge(p1_zero, 1)
                    overlapped(dve_body)(dve)

                def pool_norm(pool, n_done, read, n_read, mv_, ls, sc, steps, mvd, done):
                    for k in range(CB):
                        after(pool, read[k], n_read)
                    pool.wait_ge(mvd, n_done)
                    pool.tensor_tensor(ls[:, 0, :], mv_[:, :, 1], eps4[:, :], ALU.add).then_inc(steps[0], 1)
                    pool.wait_ge(steps[0], n_done)
                    pool.tensor_tensor(sc[:, 0, :], ls[:, 0, :], mhalf4[:, :], ALU.pow).then_inc(steps[1], 1)
                    pool.wait_ge(steps[1], n_done)
                    pool.tensor_tensor(ls[:, 1, :], sc[:, 0, :], mv_[:, :, 0], ALU.mult).then_inc(steps[2], 1)
                    pool.wait_ge(steps[2], n_done)
                    pool.tensor_tensor(sc[:, 1, :], zero4[:, :], ls[:, 1, :], ALU.subtract).then_inc(done, 1)

                def pool_scale(pool, n_done, dst, src, scale, shift, made):
                    pool.wait_ge(ready, 1)
                    pool.wait_ge(made, n_done)
                    for j in range(TB):
                        op = pool.tensor_scalar(dst[:, j, :], src[:, j, :], scale[:, j:j + 1], shift[:, j:j + 1],
                                                ALU.mult, ALU.add)
                    return op

                def pool_body(pool, i, att, mlp, down):
                    if mlp:
                        pool_norm(pool, i, t3_ps, i - 1, mv2, ls2, sc2, l2, mv2_done, ln2_done)
                        pool_scale(pool, i, xn, a0, sc2[:, 0, :], sc2[:, 1, :], ln2_done).then_inc(xh2_done, 1)
                    if att:
                        pool.wait_ge(gl_hi, i + 1)
                        pool.tensor_tensor(gl2[1][:, :], gg[:, OFF:GW], gl2[0][:, :].bitcast(F32),
                                           ALU.subtract).then_inc(gl_lo, 1)
                    if mlp:
                        for j in range(TB):
                            after(pool, x2_ev[j], i - 1)
                        pool.wait_ge(xb_done, i)
                        pool.tensor_tensor(xa2[:, :, :], xa[:, :, :], a0[:, :, :], ALU.add).then_inc(xa_done, 1)
                    if att:
                        pool.wait_ge(xin, (i + 1) * 16)
                        after(pool, xa_done, i)
                        pool.tensor_tensor(xa[:, :, :], xt[:, :, :], b2_bc[:, :].unsqueeze(1).broadcast_to([P, TB, C]),
                                           ALU.add).then_inc(xb_done, 1)
                        pool.wait_ge(ready, 1)
                        for k in range(CB):
                            after(pool, ht_ps[k], i)
                        after(pool, xhm_lo, i)
                        pool.wait_ge(kx_in, (i + 1) * 16)
                        for j in range(TB):
                            op = pool.tensor_scalar(xh[:, j, :], xt[:, j, :], kx[:, E_S + j:E_S + j + 1],
                                                    kx[:, E_B + j:E_B + j + 1], ALU.mult, ALU.add)
                        op.then_inc(xhm_done, 1)
                        pool.wait_ge(xhm_hi, i + 1)
                        pool.tensor_tensor(xhm2[1][:, :, :], xh[:, :, :], xhm2[0][:, :, :].bitcast(F32),
                                           ALU.subtract).then_inc(xhm_lo, 1)
                    if mlp:
                        pool_norm(pool, i, t2_ps, i, mv3, ls3, sc3, l3, mv3_done, ln3_done)
                    if att:
                        for j in range(TB):
                            after(pool, x2_ev[j], i)
                        pool.tensor_tensor(shf[:, :], kx[:, E_SH:E_SH + TB], zero4[:, :], ALU.add).then_inc(sh_done, 1)
                    if mlp:
                        for h in range(HB - 2):
                            pool.wait_ge(hh_ev[h], i)
                            pool.tensor_tensor(hl[:, h, :], hf[:, h % 2, :], hh[:, h, :].bitcast(F32),
                                               ALU.subtract).then_inc(hl_ev[h], 1)

                @block.gpsimd
                def _(pool):
                    overlapped(pool_body)(pool)

                def load_inv(sp, n):
                    for a in range(QPB):
                        sp.dma_start(x32[a * SUB:(a + 1) * SUB, :, a * SUB:(a + 1) * SUB], inv_v[n][a]).then_inc(inv_in, 16)

                def load_blocks(sp, n):
                    sp.wait_ge(x64_ev, n)
                    sp.wait_ge(x64_odd, n)
                    load_inv(sp, n)
                    sp.wait_ge(p64_ps, n)
                    sp.wait_ge(gl_lo, n)
                    sp.dma_start(gg[:, :], gg_d[n]).then_inc(gg_in, 16)

                def load_rows(sp, n):
                    sp.wait_ge(a0_ev[TB - 1], n)
                    sp.wait_ge(sh_done, n)
                    sp.dma_start(kx[:, :], kx_d[n]).then_inc(kx_in, 16)
                    sp.wait_ge(xb_done, n)
                    sp.dma_start(xt[:, :, :], x_v[n]).then_inc(xin, 16)

                def store_out(sp, n):
                    sp.wait_ge(ot_ev[0], n + 1)
                    sp.wait_ge(ot_ev[1], n + 1)
                    sp.dma_start(out_v[n], ot[:, :, :]).then_inc(out_st, 16)

                @block.sync
                def _(sp):
                    load_inv(sp, 0)
                    sp.dma_start(gg[:, :], gg_d[0]).then_inc(gg_in, 16)
                    sp.dma_start(kx[:, :], kx_d[0]).then_inc(kx_in, 16)
                    sp.dma_start(xt[:, :, :], x_v[0]).then_inc(xin, 16)
                    for n in (1, 2):
                        load_blocks(sp, n)
                        load_rows(sp, n)
                    with sp.Fori(2, NS - 1) as i:
                        load_blocks(sp, i + 1)
                        store_out(sp, i - 2)
                        load_rows(sp, i + 1)
                    for n in range(NS - 3, NS):
                        store_out(sp, n)
                    sp.wait_ge(out_st, 16 * NS)


_INS = ['L0_attn_x', 'L0_attn_dn_g', 'L0_attn_dn_b', 'L0_attn_gates_w', 'L0_attn_gates_b', 'L0_attn_lr_w',
        'L0_attn_lr_b', 'L0_attn_out_w', 'L0_attn_out_b', 'L0_attn_mn_g', 'L0_attn_mn_b', 'L0_attn_w1', 'L0_attn_b1',
        'L0_attn_w2', 'L0_attn_b2', 'L0_ffn_w_gate', 'L0_ffn_w_up', 'L0_ffn_w_down']


def kernel(**inputs):
    import numpy as _np
    import concourse.bacc as _bacc
    from concourse import mybir as _mybir
    from concourse.bass_utils import run_bass_kernel_spmd as _run

    nc = _bacc.Bacc("TRN2", target_bir_lowering=False, num_devices=1)
    arrays, args = {}, []
    for name in _INS:
        a = _np.ascontiguousarray(inputs[name])
        arrays[f"in_{name}_dram"] = a
        args.append(nc.dram_tensor(f"in_{name}_dram", a.shape, _mybir.dt.from_np(a.dtype), kind="ExternalInput").ap())
    shape = arrays["in_L0_attn_x_dram"].shape
    args.append(nc.dram_tensor("out_0_dram", shape, _mybir.dt.float32, kind="ExternalOutput").ap())
    delta_block_kernel(nc, *args)
    r = _run(nc, [arrays], core_ids=[0])
    return r.results[0]["out_0_dram"]
```
